# Optimizing a Trainium2 kernel written in Bass

```python
import numpy as np
import jax
import jax.numpy as jnp

def _softmax(x, axis=-1):
    return jax.nn.softmax(x, axis=axis)

def _gelu(x):
    return jax.nn.gelu(x, approximate=True)

def _silu(x):
    return jax.nn.silu(x)

def _sigmoid(x):
    return jax.nn.sigmoid(x)

def _layernorm(x, axis=-1, eps=1e-05):
    m = jnp.mean(x, axis=axis, keepdims=True)
    v = jnp.var(x, axis=axis, keepdims=True)
    return (x - m) / jnp.sqrt(v + eps)

def _scatter_add(tgt, idx, src, axis=0):
    return tgt.at[idx].add(src)

def _segment_sum(src, seg, n):
    return jax.ops.segment_sum(src, seg, n)
kernel_name = 'mk_sandwich_d2_jaxref_r8_0a081d'

def setup_inputs(seed: int=0):
    np.random.seed(seed)
    _w = jnp.asarray

    def _L0_attn_setup():
        import jax, jax.numpy as jnp
        import numpy as np
        import math
        B_, L_, DM = (2, 256, 256)
        DI, DXB, N, DTR, K = (512, 128, 16, 128, 4)
        H = DI // N
        HXB = DXB // N
        REP = H // HXB
        key = jax.random.key(seed)
        ks = jax.random.split(key, 8)
        s = 0.02
        hidden_states = jax.random.normal(ks[0], (B_, L_, DM), jnp.float32)
        in_proj_w = jax.random.normal(ks[1], (2 * DXB + 2 * DI, DM), jnp.float32) * s
        dt_in_proj_w = jax.random.normal(ks[2], (DTR, DM), jnp.float32) * s
        dt_std = DTR ** (-0.5)
        dt_proj_w = jax.random.uniform(ks[3], (DI, DTR), jnp.float32, -dt_std, dt_std)
        dt = jnp.exp(jax.random.uniform(ks[4], (DI,), jnp.float32) * (math.log(0.1) - math.log(0.001)) + math.log(0.001))
        dt = jnp.clip(dt, 0.0001)
        dt_proj_b = dt + jnp.log(-jnp.expm1(-dt))
        conv_w = jax.random.normal(ks[5], (DI, K), jnp.float32) * s
        conv_b = jnp.zeros((DI,), jnp.float32)
        A_log = jnp.log(jnp.broadcast_to(jnp.arange(1, N + 1, dtype=jnp.float32), (DI, N)))
        D = jnp.ones((DI,), jnp.float32)
        out_proj_w = jax.random.normal(ks[6], (DM, DI), jnp.float32) * s
        return dict(hidden_states=hidden_states, in_proj_w=in_proj_w, dt_in_proj_w=dt_in_proj_w, dt_proj_w=dt_proj_w, dt_proj_b=dt_proj_b, conv_w=conv_w, conv_b=conv_b, A_log=A_log, D=D, out_proj_w=out_proj_w)
    _L0_attn_in = _L0_attn_setup()

    def _L0_ffn_setup():
        import jax, jax.numpy as jnp
        import numpy as np
        TOP_K = 2
        key = jax.random.key(seed)
        k1, k2, k3, k4, k5 = jax.random.split(key, 5)
        B, S, H, O, E = (2, 128, 256, 256, 8)
        hidden_states = jax.random.normal(k1, (B, S, H), dtype=jnp.float32)
        router_w = jax.random.normal(k2, (O * E, H), dtype=jnp.float32) * 0.02
        router_b = jnp.zeros((O * E,), dtype=jnp.float32)
        expert_w = jax.random.normal(k3, (E, O, H), dtype=jnp.float32) * 0.02
        expert_b = jnp.zeros((E, O), dtype=jnp.float32)
        return {'hidden_states': hidden_states, 'router_w': router_w, 'router_b': router_b, 'expert_w': expert_w, 'expert_b': expert_b}
    _L0_ffn_in = _L0_ffn_setup()

    def _L1_attn_setup():
        import jax, jax.numpy as jnp
        import numpy as np
        EPS = 1e-12

        def _ln(x, g, b):
            m = x.mean(-1, keepdims=True)
            v = x.var(-1, keepdims=True)
            return (x - m) / jnp.sqrt(v + EPS) * g + b

        def _shift(x):
            return jnp.pad(x[:, :-1], ((0, 0), (1, 0), (0, 0)))
        key = jax.random.key(seed)
        ks = jax.random.split(key, 20)
        B, T, H = (4, 256, 256)
        I = 4 * H
        f32 = jnp.float32

        def gamma(k):
            return 1.0 + 0.1 * jax.random.normal(k, (H,), f32)

        def beta(k):
            return 0.1 * jax.random.normal(k, (H,), f32)

        def w(k, i, o):
            return 0.02 * jax.random.normal(k, (i, o), f32)
        return {'x': jax.random.normal(ks[0], (B, T, H), f32), 'ln1_g': gamma(ks[1]), 'ln1_b': beta(ks[2]), 'ln2_g': gamma(ks[3]), 'ln2_b': beta(ks[4]), 'tm_g': gamma(ks[5]), 'tm_b': beta(ks[6]), 'time_decay': -(0.2 + jax.random.uniform(ks[7], (H,), f32)), 'time_first': jax.random.uniform(ks[8], (H,), f32), 'Wk': w(ks[9], H, H), 'Wv': w(ks[10], H, H), 'Wr': w(ks[11], H, H), 'Wo': w(ks[12], H, H), 'bo': jnp.zeros((H,), f32), 'cm_g': gamma(ks[13]), 'cm_b': beta(ks[14]), 'Wck': w(ks[15], H, I), 'Wcv': w(ks[16], I, H), 'Wcr': w(ks[17], H, H)}
    _L1_attn_in = _L1_attn_setup()

    def _L1_ffn_setup():
        import jax, jax.numpy as jnp
        import numpy as np
        EPS = 1e-08

        def _quantize(w):
            gamma = jnp.mean(jnp.abs(w))
            return jnp.clip(jnp.round(w / (gamma + EPS)), -1.0, 1.0)

        def _bitlinear(x, w):
            return jnp.matmul(x, _quantize(w).T)
        key = jax.random.key(seed)
        k1, k2, k3, k4 = jax.random.split(key, 4)
        d, h = (256, 704)
        x = jax.random.normal(k1, (4, 256, d), dtype=jnp.float32)
        w1 = jax.random.normal(k2, (h, d), dtype=jnp.float32)
        w2 = jax.random.normal(k3, (h, d), dtype=jnp.float32)
        w3 = jax.random.normal(k4, (d, h), dtype=jnp.float32)
        return {'x': x, 'w1': w1, 'w2': w2, 'w3': w3}
    _L1_ffn_in = _L1_ffn_setup()
    _d = {'L0_attn_hidden_states': _L0_attn_in['hidden_states'], 'L0_attn_in_proj_w': _L0_attn_in['in_proj_w'], 'L0_attn_dt_in_proj_w': _L0_attn_in['dt_in_proj_w'], 'L0_attn_dt_proj_w': _L0_attn_in['dt_proj_w'], 'L0_attn_dt_proj_b': _L0_attn_in['dt_proj_b'], 'L0_attn_conv_w': _L0_attn_in['conv_w'], 'L0_attn_conv_b': _L0_attn_in['conv_b'], 'L0_attn_A_log': _L0_attn_in['A_log'], 'L0_attn_D': _L0_attn_in['D'], 'L0_attn_out_proj_w': _L0_attn_in['out_proj_w'], 'L0_ffn_router_w': _L0_ffn_in['router_w'], 'L0_ffn_router_b': _L0_ffn_in['router_b'], 'L0_ffn_expert_w': _L0_ffn_in['expert_w'], 'L0_ffn_expert_b': _L0_ffn_in['expert_b'], 'L1_attn_ln1_g': _L1_attn_in['ln1_g'], 'L1_attn_ln1_b': _L1_attn_in['ln1_b'], 'L1_attn_ln2_g': _L1_attn_in['ln2_g'], 'L1_attn_ln2_b': _L1_attn_in['ln2_b'], 'L1_attn_tm_g': _L1_attn_in['tm_g'], 'L1_attn_tm_b': _L1_attn_in['tm_b'], 'L1_attn_time_decay': _L1_attn_in['time_decay'], 'L1_attn_time_first': _L1_attn_in['time_first'], 'L1_attn_Wk': _L1_attn_in['Wk'], 'L1_attn_Wv': _L1_attn_in['Wv'], 'L1_attn_Wr': _L1_attn_in['Wr'], 'L1_attn_Wo': _L1_attn_in['Wo'], 'L1_attn_bo': _L1_attn_in['bo'], 'L1_attn_cm_g': _L1_attn_in['cm_g'], 'L1_attn_cm_b': _L1_attn_in['cm_b'], 'L1_attn_Wck': _L1_attn_in['Wck'], 'L1_attn_Wcv': _L1_attn_in['Wcv'], 'L1_attn_Wcr': _L1_attn_in['Wcr'], 'L1_ffn_w1': _L1_ffn_in['w1'], 'L1_ffn_w2': _L1_ffn_in['w2'], 'L1_ffn_w3': _L1_ffn_in['w3']}
    _x0 = _d['L0_attn_hidden_states']
    _d['L0_attn_hidden_states'] = jax.random.normal(jax.random.fold_in(jax.random.key(seed), 1), (4, 512, 256), dtype=_x0.dtype)
    del _x0
    return _d

def reference(L0_attn_hidden_states, L0_attn_in_proj_w, L0_attn_dt_in_proj_w, L0_attn_dt_proj_w, L0_attn_dt_proj_b, L0_attn_conv_w, L0_attn_conv_b, L0_attn_A_log, L0_attn_D, L0_attn_out_proj_w, L0_ffn_router_w, L0_ffn_router_b, L0_ffn_expert_w, L0_ffn_expert_b, L1_attn_ln1_g, L1_attn_ln1_b, L1_attn_ln2_g, L1_attn_ln2_b, L1_attn_tm_g, L1_attn_tm_b, L1_attn_time_decay, L1_attn_time_first, L1_attn_Wk, L1_attn_Wv, L1_attn_Wr, L1_attn_Wo, L1_attn_bo, L1_attn_cm_g, L1_attn_cm_b, L1_attn_Wck, L1_attn_Wcv, L1_attn_Wcr, L1_ffn_w1, L1_ffn_w2, L1_ffn_w3):

    def _L0_attn_ref(hidden_states, in_proj_w, dt_in_proj_w, dt_proj_w, dt_proj_b, conv_w, conv_b, A_log, D, out_proj_w):
        import jax, jax.numpy as jnp
        import numpy as np
        import math
        B_, L_, DM = (2, 256, 256)
        DI, DXB, N, DTR, K = (512, 128, 16, 128, 4)
        H = DI // N
        HXB = DXB // N
        REP = H // HXB
        b, l, _ = hidden_states.shape
        zxbc = hidden_states @ in_proj_w.T
        z = zxbc[..., :DI]
        x = zxbc[..., DI:DI + DXB]
        Bmat = zxbc[..., DI + DXB:DI + 2 * DXB]
        C = zxbc[..., DI + 2 * DXB:]
        dt = hidden_states @ dt_in_proj_w.T @ dt_proj_w.T
        dt = jax.nn.softplus(dt + dt_proj_b)
        xh = jnp.repeat(x.reshape(b, l, HXB, N), REP, axis=2)
        xfull = xh.reshape(b, l, DI)
        xc = jnp.moveaxis(xfull, -1, 1)
        xp = jnp.pad(xc, ((0, 0), (0, 0), (K - 1, 0)))
        conv = sum((conv_w[None, :, k, None] * xp[:, :, k:k + l] for k in range(K)))
        xact = jax.nn.silu(conv + conv_b[None, :, None])
        xact = jnp.moveaxis(xact, 1, -1)
        Bh = jnp.repeat(Bmat.reshape(b, l, HXB, N), REP, axis=2)
        Ch = C.reshape(b, l, H, N)
        A = -jnp.exp(A_log).reshape(H, N, N)
        xh4 = xact.reshape(b, l, H, N)
        dth = dt.reshape(b, l, H, N)

        def step(h, inp):
            xt, dtt, Bt, Ct = inp
            dA = jnp.exp(dtt[..., None] * A)
            h = h * dA + (dtt * xt)[..., None] * Bt[:, :, None, :]
            yt = jnp.einsum('bhpn,bhn->bhp', h, Ct)
            return (h, yt)
        h0 = jnp.zeros((b, H, N, N), hidden_states.dtype)
        xs = (jnp.moveaxis(xh4, 1, 0), jnp.moveaxis(dth, 1, 0), jnp.moveaxis(Bh, 1, 0), jnp.moveaxis(Ch, 1, 0))
        _, ys = jax.lax.scan(step, h0, xs)
        y = jnp.moveaxis(ys, 0, 1).reshape(b, l, DI)
        y = (y + D * xact) * jax.nn.silu(z)
        return y @ out_proj_w.T

    def _L0_ffn_ref(hidden_states, router_w, router_b, expert_w, expert_b):
        import jax, jax.numpy as jnp
        import numpy as np
        TOP_K = 2
        B, S, H = hidden_states.shape
        E, O, _ = expert_w.shape
        T = B * S
        h = hidden_states.reshape(T, H)
        logits = (h @ router_w.T + router_b).reshape(T, O, E)
        probs = jax.nn.softmax(logits.astype(jnp.float32), axis=-1)
        w, sel = jax.lax.top_k(probs, TOP_K)
        w = w / jnp.sum(w, axis=-1, keepdims=True)
        w = w.astype(h.dtype)
        t_idx = jnp.arange(T)[:, None, None]
        c = jnp.zeros((T, E), dtype=h.dtype).at[t_idx, sel].add(w)
        expert_out = jnp.einsum('th,eoh->teo', h, expert_w) + expert_b[None, :, :]
        final = jnp.einsum('te,teo->to', c, expert_out)
        return final.reshape(B, S, O)

    def _L1_attn_ref(x, ln1_g, ln1_b, ln2_g, ln2_b, tm_g, tm_b, time_decay, time_first, Wk, Wv, Wr, Wo, bo, cm_g, cm_b, Wck, Wcv, Wcr):
        import jax, jax.numpy as jnp
        import numpy as np
        EPS = 1e-12

        def _ln(x, g, b):
            m = x.mean(-1, keepdims=True)
            v = x.var(-1, keepdims=True)
            return (x - m) / jnp.sqrt(v + EPS) * g + b

        def _shift(x):
            return jnp.pad(x[:, :-1], ((0, 0), (1, 0), (0, 0)))
        B, T, H = x.shape
        x1 = _ln(x, ln1_g, ln1_b)
        xln = _ln(x1, tm_g, tm_b)
        xs = _shift(xln)
        mix = xln * time_first + xs * (1.0 - time_first)
        v = xln @ Wv
        r = jax.nn.sigmoid(mix @ Wr)
        dec = jnp.exp(time_decay[None, :] * (T - 1 - jnp.arange(T))[:, None])
        vmix = jnp.einsum('bth,th->bh', v, dec)[:, None, :]
        time_out = r * (vmix @ Wo + bo)
        x2 = x + time_out
        xc = _ln(_ln(x2, ln2_g, ln2_b), cm_g, cm_b)
        xcs = _shift(xc)
        kc = jnp.square(jax.nn.relu(xcs @ Wck))
        vc = kc @ Wcv
        rc = jax.nn.sigmoid(xc @ Wcr)
        return x2 + rc * vc

    def _L1_ffn_ref(x, w1, w2, w3):
        import jax, jax.numpy as jnp
        import numpy as np
        EPS = 1e-08

        def _quantize(w):
            gamma = jnp.mean(jnp.abs(w))
            return jnp.clip(jnp.round(w / (gamma + EPS)), -1.0, 1.0)

        def _bitlinear(x, w):
            return jnp.matmul(x, _quantize(w).T)
        x1 = _bitlinear(x, w1)
        x2 = _bitlinear(x, w2)
        hidden = jax.nn.sigmoid(x1) * x2
        return _bitlinear(hidden, w3)
    x = L0_attn_hidden_states
    x = x + _layernorm(_L0_attn_ref(_layernorm(x, axis=-1), L0_attn_in_proj_w, L0_attn_dt_in_proj_w, L0_attn_dt_proj_w, L0_attn_dt_proj_b, L0_attn_conv_w, L0_attn_conv_b, L0_attn_A_log, L0_attn_D, L0_attn_out_proj_w), axis=-1)
    x = x + _layernorm(_L0_ffn_ref(_layernorm(x, axis=-1), L0_ffn_router_w, L0_ffn_router_b, L0_ffn_expert_w, L0_ffn_expert_b), axis=-1)
    x = x + _layernorm(_L1_attn_ref(_layernorm(x, axis=-1), L1_attn_ln1_g, L1_attn_ln1_b, L1_attn_ln2_g, L1_attn_ln2_b, L1_attn_tm_g, L1_attn_tm_b, L1_attn_time_decay, L1_attn_time_first, L1_attn_Wk, L1_attn_Wv, L1_attn_Wr, L1_attn_Wo, L1_attn_bo, L1_attn_cm_g, L1_attn_cm_b, L1_attn_Wck, L1_attn_Wcv, L1_attn_Wcr), axis=-1)
    x = x + _layernorm(_L1_ffn_ref(_layernorm(x, axis=-1), L1_ffn_w1, L1_ffn_w2, L1_ffn_w3), axis=-1)
    return x

_drawn_inputs = setup_inputs


def setup_inputs(seed=0):
    import zlib

    import numpy as np

    out = dict(_drawn_inputs(seed))
    spreads = {'L0_attn_conv_b': (0.0, 0.1),
     'L0_attn_D': (1.0, 0.2),
     'L0_ffn_router_b': (0.0, 0.1),
     'L0_ffn_expert_b': (0.0, 0.1),
     'L1_attn_bo': (0.0, 0.388)}
    factors = {'L0_attn_dt_in_proj_w': 8.0,
     'L0_attn_dt_proj_w': 8.0,
     'L0_attn_dt_proj_b': 4.184,
     'L0_attn_A_log': 5.867,
     'L1_attn_ln1_g': 8.0,
     'L1_attn_ln1_b': 8.0,
     'L1_attn_ln2_g': 8.0,
     'L1_attn_ln2_b': 8.0,
     'L1_attn_tm_g': 8.0,
     'L1_attn_tm_b': 8.0,
     'L1_attn_time_decay': 6.09,
     'L1_attn_time_first': 8.0,
     'L1_attn_Wr': 8.0,
     'L1_attn_cm_g': 8.0,
     'L1_attn_cm_b': 8.0,
     'L1_attn_Wck': 3.559,
     'L1_attn_Wcv': 3.221,
     'L1_attn_Wcr': 8.0}
    for name, (base, spread) in spreads.items():
        noise = np.random.default_rng([zlib.crc32(name.encode()), seed]).standard_normal(out[name].shape)
        drawn = base * np.exp(spread * noise) if base else spread * noise
        out[name] = jnp.asarray(drawn.astype(out[name].dtype))
    for name, factor in factors.items():
        out[name] = (out[name] * factor).astype(out[name].dtype)
    return out
```

```python
from contextlib import ExitStack

import concourse.bass as bass
from concourse import mybir

F32 = mybir.dt.float32
BF16 = mybir.dt.bfloat16
ACT = mybir.ActivationFunctionType
ALU = mybir.AluOpType
AX = mybir.AxisListType.X

P = 128
NB, T, DM = 4, 512, 256
NJ = T // P
KD = DM // P
DI, DXB, NS, DTR, KC = 512, 128, 16, 128, 4
NCT = DI // P
NP = P // NS
NT = P // NP
NQ = 4
REP = 4
NH = DI // NS
NG = DXB // NS
NE = 8
HID = 704
HR = HID // 8
NM = -(-HID // P)
NI = 4 * DM // P
EPS, EPS2, EPS3 = 1e-5, 1e-12, 1e-8
MAGIC = 1.5 * 2.0 ** 23

CZ, CX, CC, CB = 0, DI, 2 * DI, 3 * DI
CW = 3 * DI + DXB

STAGES = 4
U_BUFS, H_BUFS, HC_BUFS, C_BUFS, B_BUFS = 2, 2, 3, 4, 2
Y_LAG = 3
GATE_AT = 2

DTB, CNB, DSK, TAP = 0, 1, 2, 3
G1, B1, G2, B2, BO = range(5)
TG, TB, CG, CBE, TF, TD = range(6)
R_STEPS = 19

FRONT_BANKS, MOE_BANKS = 4, 3
UNIT_AT = {1: ("dt", "x"), 5: ("C", "z")}


def front_order():
    names = [("xT", 0), ("xT", 1), ("dtr", 0), ("B", 0)]
    names += [(kind, 0) for pair in UNIT_AT.values() for kind in pair]
    for ct in range(NCT):
        for i in range(NT):
            names += [("dA", ct * NT + i), ("dtx", ct * NT + i)]
            if i in UNIT_AT and ct + 1 < NCT:
                names += [(kind, ct + 1) for kind in UNIT_AT[i]]
    names += [("out", j) for j in range(NJ)]
    assert len(names) % FRONT_BANKS == 0
    return names


def moe_order():
    names = [("mT", 0), ("mT", 1)]
    for j in range(NJ + 1):
        if j < NJ:
            names += [("route", 4 * j + c) for c in range(4)]
        if j > 0:
            names += [("expert", 4 * (j - 1) + c) for c in range(4)]
    names += [("pad", 0), ("pad", 1)]
    assert len(names) % MOE_BANKS == 0
    return names


def rwkv_order():
    names = [("tT", 0), ("tT", 1), ("v", 0), ("v", 1), ("r", 0), ("r", 1), ("q", 0), ("pad", 0)]
    names += [("cT", 0), ("cT", 1)] + [("ck", m) for m in range(NI)] + [("cr", 0), ("cr", 1)]
    names += [("cv", 0), ("cv", 1), ("pad", 1), ("pad", 2)]
    assert len(names) % 4 == 0
    return names


def ffn_order():
    names = [("fT", 0), ("fT", 1)] + [(w, m) for m in range(NM) for w in ("w1", "w2")] + [("w3", 0), ("w3", 1)]
    assert len(names) % 4 == 0
    return names


FRONT, MOE, RWKV, FFN = front_order(), moe_order(), rwkv_order(), ffn_order()
FRONT_AT, MOE_AT, RWKV_AT, FFN_AT = ({name: n for n, name in enumerate(o)} for o in (FRONT, MOE, RWKV, FFN))


LAST = 1 << 20


class Signal:

    def __init__(self, sem, per_batch, unit=1):
        self.sem, self.per_batch, self.unit = sem, per_batch, unit

    def at(self, b, k):
        if isinstance(b, int):
            return (b * self.per_batch + k) * self.unit
        return b * (self.per_batch * self.unit) + k * self.unit

    def begun(self, b, k):
        return not isinstance(b, int) or b * self.per_batch + k > 0

    def in_register(self, eng, b, k):
        return self.at(b, k) if isinstance(b, int) else eng.to_reg(self.at(b, k))


class Steps:

    def __init__(self, raised, b):
        self.sem, self.raised, self.b, self.k = raised.sem, raised, b, 0

    def next(self):
        self.k += 1
        return self.raised.at(self.b, self.k)

    def end(self):
        assert self.k == self.raised.per_batch, (self.sem, self.k)


def run_until(strand, slot):
    while strand is not None and strand[0] <= slot:
        try:
            strand[0] = next(strand[1])
        except StopIteration:
            strand[0] = LAST + 1
            break


def rounds(eng, first, second, prepare):
    first(0, [0, prepare()] if prepare else None)
    first(1, [0, second(0)])
    with eng.Fori(2, NB) as b:
        first(b, [0, second(b - 1)])
    run_until([0, second(NB - 1)], LAST)


def at_b(ap, b):
    return ap[b:b + 1] if isinstance(b, int) else ap[bass.ds(b, 1)]


def hybrid_layers_kernel(nc, a, out):
    kernel_ctx = ExitStack()
    with kernel_ctx:
        def sig(name, per_batch=1, unit=1):
            return Signal(kernel_ctx.enter_context(nc.semaphore(name)), per_batch, unit)

        def keep(name, shape, dt=F32):
            return kernel_ctx.enter_context(nc.sbuf_tensor(name, shape, dt))

        bank = [kernel_ctx.enter_context(nc.psum_tensor(f"bank{i}", [P, 512], F32)) for i in range(8)]
        ident = keep("ident", [P, P])
        neg_half = keep("neg_half", [P, NJ])
        junk = keep("junk", [P, NJ, DM], BF16)
        x2_all = keep("x2_all", [P, NB, NJ, DM])
        consts = sig("consts", 0)

        class Norm:

            def __init__(self, name, stat, n, n_pow, junk=junk):
                self.junk = junk
                self.mean, self.sq = sig(name + "_mean", n), sig(name + "_sq", n)
                self.var, self.rstd = sig(name + "_var", n_pow), sig(name + "_rstd", n_pow)
                self.total, self.neg, self.ss, self.v, self.r = (stat[:, i, :] for i in range(5))

        def norm_mean(dve, own, ln, src):
            nc.vector.tensor_reduce(ln.total, src, AX, ALU.add).then_inc(own.sem, 1)
            dve.wait_ge(own.sem, own.next())
            nc.vector.tensor_scalar(ln.neg, ln.total, -1.0 / DM, None, ALU.mult).then_inc(ln.mean.sem, 1)

        def norm_square(act, b, ln, k, src):
            act.wait_ge(ln.mean.sem, ln.mean.at(b, k + 1))
            for j in range(NJ):
                ins = nc.scalar.activation(ln.junk[:, j, :], src[:, j, :], ACT.Square, bias=ln.neg[:, j:j + 1],
                                           accum_out=ln.ss[:, j:j + 1])
            ins.then_inc(ln.sq.sem, 1)

        def norm_var(dve, b, ln, k, k_pow, eps):
            dve.wait_ge(ln.sq.sem, ln.sq.at(b, k + 1))
            nc.vector.tensor_scalar(ln.v, ln.ss, 1.0 / DM, eps, ALU.mult, ALU.add).then_inc(ln.var.sem, 1)

        def norm_rstd(pool, b, ln, k_pow):
            pool.wait_ge(ln.var.sem, ln.var.at(b, k_pow + 1))
            nc.gpsimd.tensor_tensor(ln.r, ln.v, neg_half[:, :], ALU.pow).then_inc(ln.rstd.sem, 1)

        def norm_apply(dve, b, ln, k_pow, dst, src):
            dve.wait_ge(ln.rstd.sem, ln.rstd.at(b, k_pow + 1))
            for j in range(NJ):
                ins = nc.vector.tensor_scalar(dst[:, j, :], src[:, j, :], ln.neg[:, j:j + 1], ln.r[:, j:j + 1],
                                              ALU.add, ALU.mult)
            return ins

        def transpose_tiles(dst_bank, src, k):
            for j in range(NJ):
                ins = nc.tensor.transpose(dst_bank[:, j * P:(j + 1) * P], src[:, j, k * P:(k + 1) * P], ident[:, :])
            return ins

        with ExitStack() as ctx:
            def sb(name, shape, dt=F32):
                return ctx.enter_context(nc.sbuf_tensor(name, shape, dt))

            ones_bf = sb("ones_bf", [P, P], BF16)
            one_hot = sb("one_hot", [P, 4, P], BF16)
            state_sum = sb("state_sum", [P, 4, 32])
            projT = sb("projT", [P, KD, CW])
            dt_inT = sb("dt_inT", [P, KD, DTR])
            dt_projT = sb("dt_projT", [P, 1, DI])
            outT = sb("outT", [P, NCT, DM])
            A_neg = sb("A_neg", [P, NCT * NT])
            per_ch = sb("per_ch", [P, NCT, 3 + KC])
            routeT = sb("routeT", [P, KD, NE * DM])
            expertT = sb("expertT", [P, KD, NE * DM])

            x0 = sb("x0", [P, NJ, DM])
            fa = sb("fa", [P, NJ, DM])
            xT = sb("xT", [P, KD, T])
            dtr = sb("dtr", [P, T])
            sp_u, sp_r, sp_w = sb("sp_u", [P, T]), sb("sp_r", [P, T]), sb("sp_w", [P, T])
            xr = sb("xr", [P, KC - 1 + T])
            xact = sb("xact", [P, 2, T])
            zs = sb("zs", [P, 2, T])
            bc_sb = sb("bc_sb", [P, 2, T])
            parts = sb("parts", [P, 2, 3, T], BF16)
            rem = sb("rem", [P, T])
            dtx = sb("dtx", [P, T])
            stack = sb("stack", [P, 2, 2, NQ, T], BF16)
            b_rep = sb("b_rep", [P, B_BUFS, T])
            c_rep = sb("c_rep", [P, C_BUFS, T])
            u = sb("u", [P, U_BUFS, T])
            h = sb("h", [P, H_BUFS, T])
            hc = sb("hc", [P, HC_BUFS, T])
            yz = sb("yz", [P, NCT, T])
            f_stat = sb("f_stat", [P, 5, NJ])
            b_dram = nc.dram_tensor("b_dram", [NB, DXB, T], F32, kind="Internal").ap()
            c_dram = nc.dram_tensor("c_dram", [NB, DI, T], F32, kind="Internal").ap()
            bias_dram = nc.dram_tensor("bias_dram", [3, 2, NE * DM], BF16, kind="Internal").ap()

            x1 = sb("x1", [P, NJ, DM])
            ma = sb("ma", [P, NJ, DM])
            mT = sb("mT", [P, KD, T])
            lg = sb("lg", [P, 2, NE, DM])
            hi_t, lo_t = sb("hi_t", [P, 4, DM]), sb("lo_t", [P, 4, DM])
            sel = sb("sel", [P, 2, 2, DM])
            gate_c = sb("gate_c", [P, 2, NE])
            spares = hi_t[:, :, :].rearrange("p a d -> p (a d)").bitcast(BF16).rearrange("p (e d) -> p e d", e=NE)
            acc = hi_t[:, 3, :]
            m_stat = sb("m_stat", [P, 5, NJ])
            stage = c_rep
            y_bank = bank[FRONT_BANKS]
            m_bank = bank[FRONT_BANKS + 1:]
            bias_rows = stack[96:99, 0, :, :, :].rearrange("a v q t -> a v (q t)")

            small_in = sig("small_in", 0, 16)
            f_ln = Norm("f", f_stat, 2, 2)
            x0_in = sig("x0_in", 1, 16)
            xn0 = sig("xn0")
            f_done = sig("f_done", len(FRONT))
            xT_up = sig("xT_up", 2)
            dtr_up = sig("dtr_up")
            bsb_up, csb_up = sig("bsb_up"), sig("csb_up", NCT)
            sp_abs, sp_relu, sp_exp, sp_ln = (sig("sp_" + n, NCT) for n in ("abs", "relu", "exp", "ln"))
            xr_up, conv_up, xact_up, zs_up = (sig(n, NCT) for n in ("xr_up", "conv_up", "xact_up", "zs_up"))
            dt_up, dtx_up = sig("dt_up", NCT), sig("dtx_up", NCT)
            hi_up, rem_up, mid_up, lo_up = (sig(n, 2 * NCT) for n in ("hi_up", "rem_up", "mid_up", "lo_up"))
            stack_in = [sig(f"stack_in{v}", NCT * NQ * 3, 16) for v in range(2)]
            b_out, c_out = sig("b_out", 1, 16), sig("c_out", NCT, 16)
            b_in = [sig(f"b_in{i}", NG // B_BUFS, 16) for i in range(B_BUFS)]
            c_in = [sig(f"c_in{i}", NH // C_BUFS, 16) for i in range(C_BUFS)]
            dA_up, u_up, h_up, hc_up, ysum = (sig(n, NCT * NT) for n in ("dA_up", "u_up", "h_up", "hc_up", "ysum"))
            y_read, yz_up = sig("y_read", NCT), sig("yz_up", NCT)
            fo_up = sig("fo_up", NJ)
            x1_up = sig("x1_up")
            f_step = sig("f_step", 3 + 6 * NCT)

            m_ln = Norm("m", m_stat, 2, 2)
            m_done = sig("m_done", sum(n[0] != "pad" for n in MOE))
            xm_up, mT_up = sig("xm_up"), sig("mT_up", 2)
            lg_up = sig("lg_up", 4 * NJ)
            gap_up, d1_up, tanh_up, c_up = (sig(n, NJ) for n in ("gap_up", "d1_up", "tanh_up", "c_up"))
            mix_up = sig("mix_up", 4 * NJ)
            x2_up = sig("x2_up")
            m_step = sig("m_step", 3 + 12 * NJ)

            prep_in = [sig(f"prep_in{i}", 0, 16) for i in range(STAGES)]
            prep_done, prep_act, prep_dve = sig("prep_done", 0), sig("prep_act", 0), sig("prep_dve", 0)
            bias_split, bias_out, bias_in = sig("bias_split", 0), sig("bias_out", 0, 16), sig("bias_in", 0, 16)

            def front_reader(name):
                kind, i = name
                return {"xT": xT_up, "dtr": dtr_up, "B": bsb_up, "dt": sp_relu, "x": xr_up, "C": csb_up,
                        "z": zs_up, "dA": h_up, "dtx": u_up, "out": fo_up}[kind], i + 1

            def moe_reader(name):
                kind, i = name
                return {"mT": mT_up, "route": lg_up, "expert": mix_up}[kind], i + 1

            units = []

            def unit(loads, turns, dst):
                units.append((loads, turns, dst))

            def row_pair(srcs, dst, col):
                m = len(srcs)
                unit([(r * DM, slice(0, P), s) for r, s in enumerate(srcs)],
                     [(k * m * P + r * P, r * DM + k * P) for r in range(m) for k in range(KD)],
                     dst[:, :, col:col + m * P])

            w_in = a["L0_attn_in_proj_w"]
            row = lambda w, t: w[t * P:(t + 1) * P, :]
            row_pair([row(a["L0_attn_dt_in_proj_w"], 0)], dt_inT, 0)
            unit([(0, slice(0, P), a["L0_attn_dt_proj_w"].rearrange("(t p) k -> p t k", p=P))],
                 [(t * P, t * P) for t in range(NCT)], dt_projT[:, :, :])
            row_pair([row(w_in, (DI + DXB) // P)], projT, CB)
            for t in range(0, NCT, 2):
                loads = []
                for r in range(2):
                    for g in range(2):
                        src = w_in[DI + (2 * (t + r) + g) * NS:DI + (2 * (t + r) + g + 1) * NS, :]
                        loads.append((r * DM, slice(g * REP * NS, (g + 1) * REP * NS),
                                      src.unsqueeze(0).to_broadcast([REP, NS, DM])))
                unit(loads, [(k * 2 * P + r * P, r * DM + k * P) for r in range(2) for k in range(KD)],
                     projT[:, :, CX + t * P:CX + (t + 2) * P])
            for t in range(0, NCT, 2):
                row_pair([row(w_in, (DI + 2 * DXB) // P + t + r) for r in range(2)], projT, CC + t * P)
            for t in range(0, NCT, 2):
                row_pair([row(w_in, t + r) for r in range(2)], projT, CZ + t * P)
            for t in range(KD):
                unit([(0, slice(0, P), row(a["L0_attn_out_proj_w"], t))],
                     [(c * P, c * P) for c in range(NCT)], outT[:, :, t * P:(t + 1) * P])
            w_route = a["L0_ffn_router_w"].rearrange("(o e) d -> e o d", e=NE)
            w_expert = a["L0_ffn_expert_w"]
            for w, dst in ((w_route, routeT), (w_expert, expertT)):
                for e in range(NE):
                    row_pair([w[e, 0:P, :], w[e, P:2 * P, :]], dst, e * DM)
            loaded = [0] * STAGES
            unit_loaded = []
            for n, (loads, _, _) in enumerate(units):
                loaded[n % STAGES] += len(loads)
                unit_loaded.append(loaded[n % STAGES])

            def x2_slice(b):
                if isinstance(b, int):
                    return x2_all[:, b, :, :]
                return x2_all[:, bass.ds(b, 1), :, :].rearrange("p b j d -> p (b j) d")

            block = ctx.enter_context(nc.Block())

            @block.sync
            def _(sp):
                def load_unit(n):
                    if n >= STAGES:
                        sp.wait_ge(prep_done.sem, prep_done.at(0, n - STAGES + 1))
                    for col, pp, src in units[n][0]:
                        width = src.shape[-1] * (src.shape[1] if len(src.shape) == 3 and pp == slice(0, P) else 1)
                        dst = stage[pp, n % STAGES, col:col + width]
                        if len(src.shape) == 3 and pp == slice(0, P):
                            dst = dst.rearrange("p (t k) -> p t k", t=src.shape[1])
                        sp.dma_start(dst, src).then_inc(prep_in[n % STAGES].sem, 16)

                def load_x0(b):
                    sp.dma_start(x0[:, :, :], at_b(a["x"], b).rearrange("b (j p) d -> p (b j) d", p=P)
                                 ).then_inc(x0_in.sem, 16)

                def stack_parts(b, ct, v):
                    last = FRONT_AT[("dtx", (ct - 2) % NCT * NT + NT - 1)] + 1
                    freed = f_done.in_register(sp, b, last if ct >= 2 else last - len(FRONT))
                    sp.wait_ge(lo_up.sem, lo_up.at(b, 2 * ct + v + 1))
                    if f_done.begun(b, last if ct >= 2 else last - len(FRONT)):
                        sp.wait_ge(f_done.sem, freed)
                    for q in range(NQ):
                        for part in range(3):
                            sp.dma_start(stack[32 * part:32 * part + 32, ct % 2, v, q, :],
                                         parts[32 * q:32 * q + 32, v, part, :]).then_inc(stack_in[v].sem, 16)

                def c_replica(b, hd):
                    freed = hc_up.in_register(sp, b, 2 * (hd - C_BUFS) + 2)
                    if hd % 8 == 0:
                        sp.wait_ge(c_out.sem, c_out.at(b, hd // 8 + 1))
                    if hc_up.begun(b, 2 * (hd - C_BUFS) + 2):
                        sp.wait_ge(hc_up.sem, freed)
                    src = at_b(c_dram, b)[:, hd * NS:(hd + 1) * NS, :].rearrange("b n t -> (b n) t")
                    sp.dma_start(c_rep[:, hd % C_BUFS, :], src.unsqueeze(0).to_broadcast([NP, NS, T])
                                 ).then_inc(c_in[hd % C_BUFS].sem, 16)

                def b_replica(b, g):
                    if g == 0:
                        sp.wait_ge(b_out.sem, b_out.at(b, 1))
                    if u_up.begun(b, 8 * (g - B_BUFS) + 8):
                        sp.wait_ge(u_up.sem, u_up.at(b, 8 * (g - B_BUFS) + 8))
                    src = at_b(b_dram, b)[:, g * NS:(g + 1) * NS, :].rearrange("b n t -> (b n) t")
                    sp.dma_start(b_rep[:, g % B_BUFS, :], src.unsqueeze(0).to_broadcast([NP, NS, T])
                                 ).then_inc(b_in[g % B_BUFS].sem, 16)

                def c_write(b, ct):
                    sp.wait_ge(csb_up.sem, csb_up.at(b, ct + 1))
                    sp.dma_start(at_b(c_dram, b)[:, ct * P:(ct + 1) * P, :].rearrange("b n t -> (b n) t"),
                                 bc_sb[:, 1, :]).then_inc(c_out.sem, 16)

                def front(b):
                    sp.wait_ge(bsb_up.sem, bsb_up.at(b, 1))
                    sp.dma_start(at_b(b_dram, b).rearrange("b n t -> (b n) t"), bc_sb[:, 0, :]).then_inc(b_out.sem, 16)
                    for g in range(B_BUFS):
                        b_replica(b, g)
                    c_write(b, 0)
                    for hd in range(C_BUFS):
                        c_replica(b, hd)
                    for v in range(2):
                        stack_parts(b, 0, v)
                    for ct in range(NCT):
                        for i in range(8):
                            hd = 8 * ct + i + C_BUFS
                            if i == 4 and ct + 1 < NCT:
                                c_write(b, ct + 1)
                            if hd < NH:
                                c_replica(b, hd)
                            if i in (3, 7) and 2 * ct + i // 4 + B_BUFS < NG:
                                b_replica(b, 2 * ct + i // 4 + B_BUFS)
                            if i in (5, 6) and ct + 1 < NCT:
                                stack_parts(b, ct + 1, i - 5)

                by_ch = lambda ap: ap.rearrange("(c p) -> p c", p=P)
                load_x0(0)
                for n in range(STAGES):
                    load_unit(n)
                for i, nm in ((DTB, "dt_proj_b"), (CNB, "conv_b"), (DSK, "D")):
                    sp.dma_start(per_ch[:, :, i], by_ch(a["L0_attn_" + nm]),
                                 allow_slow_non_contiguous=True).then_inc(small_in.sem, 16)
                sp.dma_start(per_ch[:, :, TAP:TAP + KC], a["L0_attn_conv_w"].rearrange("(c p) k -> p c k", p=P)
                             ).then_inc(small_in.sem, 16)
                sp.dma_start(sp_w[0:NCT * NT, 0:P], a["L0_attn_A_log"].rearrange("(s c) n -> s (c n)", c=NP)
                             ).then_inc(small_in.sem, 16)
                sp.dma_start(sp_u[:, 0:16], a["L0_ffn_router_b"].rearrange("(p i) -> p i", p=P)).then_inc(small_in.sem, 16)
                sp.dma_start(sp_u[:, 16:32], a["L0_ffn_expert_b"].rearrange("e (q i) -> (e q) i", i=16)
                             ).then_inc(small_in.sem, 16)
                for n in range(STAGES, len(units)):
                    load_unit(n)
                sp.wait_ge(bias_split.sem, bias_split.at(0, 3))
                for part in range(3):
                    for v in range(2):
                        sp.dma_start(bias_dram[part, v, :].rearrange("(p i) -> p i", p=P),
                                     parts[:, 0, part, 16 * v:16 * v + 16]).then_inc(bias_out.sem, 16)
                sp.wait_ge(bias_out.sem, bias_out.at(0, 6))
                sp.dma_start(bias_rows, bias_dram).then_inc(bias_in.sem, 16)
                front(0)
                with sp.Fori(1, NB) as b:
                    sp.wait_ge(x1_up.sem, x1_up.at(b, 0))
                    load_x0(b)
                    front(b)

            @block.tensor
            def _(pe):
                def prepare():
                    pe.wait_ge(consts.sem, consts.at(0, 7))
                    for n, (loads, turns, dst) in enumerate(units):
                        pe.wait_ge(prep_in[n % STAGES].sem, prep_in[n % STAGES].at(0, unit_loaded[n]))
                        if n >= 4:
                            emptied = prep_act if n % 2 == 0 else prep_dve
                            pe.wait_ge(emptied.sem, emptied.at(0, (n - 4) // 2 + 1))
                        for col, scol in turns:
                            ins = nc.tensor.transpose(bank[n % 4][:, col:col + P], stage[:, n % STAGES, scol:scol + P],
                                                      ident[:, :])
                        ins.then_inc(prep_done.sem, 1)
                    pe.wait_ge(small_in.sem, small_in.at(0, 7))
                    nc.tensor.transpose(y_bank[:, 0:NCT * NT], sp_w[0:NCT * NT, 0:P], ident[0:NCT * NT, 0:NCT * NT]
                                        ).then_inc(prep_done.sem, 1)
                    pe.wait_ge(prep_act.sem, prep_act.at(0, (len(units) + 1) // 2 + 1))
                    pe.wait_ge(prep_dve.sem, prep_dve.at(0, len(units) // 2 + 1))

                def front_bank(b, name):
                    n = FRONT_AT[name]
                    freed_by, k = front_reader(FRONT[n - FRONT_BANKS])
                    if freed_by.begun(b, k if n >= FRONT_BANKS else k - freed_by.per_batch):
                        pe.wait_ge(freed_by.sem, freed_by.at(b, k if n >= FRONT_BANKS else k - freed_by.per_batch))
                    return bank[n % FRONT_BANKS]

                def project(b, name, lhsT, rhs):
                    dst = front_bank(b, name)
                    for k, (l, r) in enumerate(zip(lhsT, rhs)):
                        ins = nc.tensor.matmul(dst[:, :], l, r, start=(k == 0), stop=(k == len(lhsT) - 1))
                    ins.then_inc(f_done.sem, 1)

                x_feat = [xT[:, k, :] for k in range(KD)]

                def unit_product(b, kind, ct):
                    if kind == "dt":
                        pe.wait_ge(dtr_up.sem, dtr_up.at(b, 1))
                        project(b, (kind, ct), [dt_projT[:, 0, ct * P:(ct + 1) * P]], [dtr[:, :]])
                    else:
                        c0 = {"x": CX, "C": CC, "z": CZ}[kind] + ct * P
                        project(b, (kind, ct), [projT[:, k, c0:c0 + P] for k in range(KD)], x_feat)

                def state_sums(b, s):
                    ct, q, k = s // NT, s % NT // 4, s % 4
                    if s % NT == 0:
                        if y_read.begun(b, ct):
                            pe.wait_ge(y_read.sem, y_read.at(b, ct))
                    pe.wait_ge(hc_up.sem, hc_up.at(b, s + 1))
                    nc.tensor.matmul(y_bank[32 * q:32 * q + 32, :], state_sum[:, k, :], hc[:, s % HC_BUFS, :],
                                     start=(k == 0), stop=(k == 3)).then_inc(ysum.sem, 1)

                def front(b, moe):
                    pe.wait_ge(xn0.sem, xn0.at(b, 1))
                    for k in range(KD):
                        transpose_tiles(front_bank(b, ("xT", k)), fa, k).then_inc(f_done.sem, 1)
                    run_until(moe, 0)
                    pe.wait_ge(xT_up.sem, xT_up.at(b, 2))
                    project(b, ("dtr", 0), [dt_inT[:, k, :] for k in range(KD)], x_feat)
                    project(b, ("B", 0), [projT[:, k, CB:CB + DXB] for k in range(KD)], x_feat)
                    for pair in UNIT_AT.values():
                        for kind in pair:
                            unit_product(b, kind, 0)
                        run_until(moe, 1)
                    for s in range(NCT * NT):
                        ct, i = s // NT, s % NT
                        if i == 0:
                            for v in range(2):
                                pe.wait_ge(stack_in[v].sem, stack_in[v].at(b, (ct + 1) * NQ * 3))
                        q, k = i // 4, i % 4
                        for v, name in enumerate(("dA", "dtx")):
                            nc.tensor.matmul(front_bank(b, (name, s))[:, :], one_hot[0:96, k, :],
                                             stack[0:96, ct % 2, v, q, :], start=True, stop=True).then_inc(f_done.sem, 1)
                        if i in UNIT_AT and ct + 1 < NCT:
                            for kind in UNIT_AT[i]:
                                unit_product(b, kind, ct + 1)
                        if s >= Y_LAG:
                            state_sums(b, s - Y_LAG)
                        run_until(moe, 8 + s)
                    for s in range(NCT * NT - Y_LAG, NCT * NT):
                        state_sums(b, s)
                    run_until(moe, 8 + NCT * NT)
                    for j in range(NJ):
                        dst = front_bank(b, ("out", j))
                        pe.wait_ge(yz_up.sem, yz_up.at(b, NCT))
                        for ct in range(NCT):
                            ins = nc.tensor.matmul(dst[:, 0:DM], yz[:, ct, j * P:(j + 1) * P], outT[:, ct, :],
                                                   start=(ct == 0), stop=(ct == NCT - 1))
                        ins.then_inc(f_done.sem, 1)
                    run_until(moe, LAST)

                def moe_bank(b, name):
                    n = MOE_AT[name]
                    before = MOE[n - MOE_BANKS]
                    if before[0] == "pad":
                        before = MOE[n - 2 * MOE_BANKS]
                    freed_by, k = moe_reader(before)
                    if freed_by.begun(b, k if n >= MOE_BANKS else k - freed_by.per_batch):
                        pe.wait_ge(freed_by.sem, freed_by.at(b, k if n >= MOE_BANKS else k - freed_by.per_batch))
                    return m_bank[n % MOE_BANKS]

                def moe(b):
                    pe.wait_ge(xm_up.sem, xm_up.at(b, 1))
                    for k in range(KD):
                        transpose_tiles(moe_bank(b, ("mT", k)), ma, k).then_inc(m_done.sem, 1)
                    yield 1
                    pe.wait_ge(mT_up.sem, mT_up.at(b, 2))
                    slot = 8
                    for kind, i in MOE[2:-2]:
                        j, c = i // 4, i % 4
                        w = routeT if kind == "route" else expertT
                        if kind == "route":
                            bias = bias_rows[:, 0, :].rearrange("a (o e) -> a e o", e=NE)[:, 2 * c:2 * c + 2, :]
                        else:
                            bias = bias_rows[:, 1, c * 512:(c + 1) * 512]
                        dst = moe_bank(b, (kind, i))
                        for k in range(KD):
                            nc.tensor.matmul(dst[:, :], mT[:, k, j * P:(j + 1) * P], w[:, k, c * 512:(c + 1) * 512],
                                             start=(k == 0), stop=False)
                        nc.tensor.matmul(dst[:, :].rearrange("p (e o) -> p e o", e=2) if kind == "route" else dst[:, :],
                                         ones_bf[96:99, :], bias, start=False, stop=True,
                                         ).then_inc(m_done.sem, 1)
                        slot += 2
                        yield slot

                prepare()
                pe.wait_ge(bias_in.sem, bias_in.at(0, 1))
                rounds(pe, front, moe, None)

            @block.scalar
            def _(act):
                def prepare():
                    for n in range(0, len(units), 2):
                        act.wait_ge(prep_done.sem, prep_done.at(0, n + 1))
                        dst = units[n][2]
                        nc.scalar.copy(dst, bank[n % 4][:, 0:dst.shape[1] * dst.shape[2]]
                                       .rearrange("p (k c) -> p k c", k=dst.shape[1])).then_inc(prep_act.sem, 1)
                    act.wait_ge(prep_done.sem, prep_done.at(0, len(units) + 1))
                    nc.scalar.activation(A_neg[:, :], y_bank[:, 0:NCT * NT], ACT.Exp).then_inc(prep_act.sem, 1)
                    act.wait_ge(small_in.sem, small_in.at(0, 7))
                    nc.scalar.copy(parts[:, 0, 0, 0:32], sp_u[:, 0:32]).then_inc(bias_split.sem, 1)
                    act.wait_ge(prep_dve.sem, prep_dve.at(0, len(units) // 2 + 2))
                    nc.scalar.copy(parts[:, 0, 1, 0:32], sp_r[:, 0:32]).then_inc(bias_split.sem, 1)

                def soft_plus_terms(b, ct):
                    src = bank[FRONT_AT[("dt", ct)] % FRONT_BANKS][:, :]
                    act.wait_ge(f_done.sem, f_done.at(b, FRONT_AT[("dt", ct)] + 1))
                    if dt_up.begun(b, ct):
                        act.wait_ge(dt_up.sem, dt_up.at(b, ct))
                    bias = per_ch[:, ct, DTB:DTB + 1]
                    nc.scalar.activation(sp_u[:, :], src, ACT.Abs, bias=bias).then_inc(sp_abs.sem, 1)
                    if hi_up.begun(b, 2 * ct - 1):
                        act.wait_ge(hi_up.sem, hi_up.at(b, 2 * ct - 1))
                    if rem_up.begun(b, 2 * ct - 1):
                        act.wait_ge(rem_up.sem, rem_up.at(b, 2 * ct - 1))
                    if dtx_up.begun(b, ct):
                        act.wait_ge(dtx_up.sem, dtx_up.at(b, ct))
                    nc.scalar.activation(sp_r[:, :], src, ACT.Relu, bias=bias).then_inc(sp_relu.sem, 1)
                    act.wait_ge(sp_abs.sem, sp_abs.at(b, ct + 1))
                    nc.scalar.activation(sp_u[:, :], sp_u[:, :], ACT.Exp, scale=-1.0).then_inc(sp_exp.sem, 1)
                    act.wait_ge(sp_exp.sem, sp_exp.at(b, ct + 1))
                    nc.scalar.activation(sp_w[:, :], sp_u[:, :], ACT.Ln, bias=1.0).then_inc(sp_ln.sem, 1)

                def take_x(b, ct):
                    act.wait_ge(f_done.sem, f_done.at(b, FRONT_AT[("x", ct)] + 1))
                    if conv_up.begun(b, ct):
                        act.wait_ge(conv_up.sem, conv_up.at(b, ct))
                    nc.scalar.copy(xr[:, KC - 1:], bank[FRONT_AT[("x", ct)] % FRONT_BANKS][:, :]).then_inc(xr_up.sem, 1)

                def silus(b, ct):
                    act.wait_ge(conv_up.sem, conv_up.at(b, ct + 1))
                    nc.scalar.activation(xact[:, ct % 2, :], xact[:, ct % 2, :], ACT.Silu).then_inc(xact_up.sem, 1)
                    act.wait_ge(f_done.sem, f_done.at(b, FRONT_AT[("z", ct)] + 1))
                    if yz_up.begun(b, ct - 1):
                        act.wait_ge(yz_up.sem, yz_up.at(b, ct - 1))
                    nc.scalar.activation(zs[:, ct % 2, :], bank[FRONT_AT[("z", ct)] % FRONT_BANKS][:, :],
                                         ACT.Silu).then_inc(zs_up.sem, 1)

                def high_part(b, ct, v):
                    made = dtx_up if v else dt_up
                    act.wait_ge(made.sem, made.at(b, ct + 1))
                    if stack_in[v].begun(b, ct * NQ * 3):
                        act.wait_ge(stack_in[v].sem, stack_in[v].at(b, ct * NQ * 3))
                    nc.scalar.copy(parts[:, v, 0, :], (dtx if v else sp_r)[:, :]).then_inc(hi_up.sem, 1)

                def middle_part(b, ct, v):
                    act.wait_ge(rem_up.sem, rem_up.at(b, 2 * ct + v + 1))
                    nc.scalar.copy(parts[:, v, 1, :], rem[:, :]).then_inc(mid_up.sem, 1)

                def front(b, moe):
                    act.wait_ge(x0_in.sem, x0_in.at(b, 1))
                    norm_square(act, b, f_ln, 0, x0)
                    for k in range(KD):
                        act.wait_ge(f_done.sem, f_done.at(b, FRONT_AT[("xT", k)] + 1))
                        nc.scalar.copy(xT[:, k, :], bank[FRONT_AT[("xT", k)] % FRONT_BANKS][:, :]).then_inc(xT_up.sem, 1)
                    run_until(moe, 0)
                    soft_plus_terms(b, 0)
                    take_x(b, 0)
                    high_part(b, 0, 0)
                    silus(b, 0)
                    run_until(moe, 1)
                    middle_part(b, 0, 0)
                    high_part(b, 0, 1)
                    middle_part(b, 0, 1)
                    for s in range(NCT * NT):
                        ct, i = s // NT, s % NT
                        n = FRONT_AT[("dA", s)]
                        act.wait_ge(f_done.sem, f_done.at(b, n + 1))
                        dst = bank[n % FRONT_BANKS][:, :]
                        nc.scalar.activation(dst, dst, ACT.Exp, scale=A_neg[:, s:s + 1]).then_inc(dA_up.sem, 1)
                        if ct + 1 < NCT:
                            if i == 2:
                                soft_plus_terms(b, ct + 1)
                                take_x(b, ct + 1)
                            if i == 5:
                                high_part(b, ct + 1, 0)
                            if i == 6:
                                silus(b, ct + 1)
                            if i == 7:
                                middle_part(b, ct + 1, 0)
                            if i == 8:
                                high_part(b, ct + 1, 1)
                            if i == 10:
                                middle_part(b, ct + 1, 1)
                        run_until(moe, 8 + s)
                    for j in range(NJ):
                        act.wait_ge(f_done.sem, f_done.at(b, FRONT_AT[("out", j)] + 1))
                        nc.scalar.copy(fa[:, j, :], bank[FRONT_AT[("out", j)] % FRONT_BANKS][:, 0:DM]
                                       ).then_inc(fo_up.sem, 1)
                    norm_square(act, b, f_ln, 1, fa)
                    run_until(moe, LAST)

                def moe(b):
                    norm_square(act, b, m_ln, 0, x1)
                    for k in range(KD):
                        act.wait_ge(m_done.sem, m_done.at(b, MOE_AT[("mT", k)] + 1))
                        nc.scalar.copy(mT[:, k, :], m_bank[MOE_AT[("mT", k)] % MOE_BANKS][:, :]).then_inc(mT_up.sem, 1)
                    yield 9
                    slot = 9
                    for n, (kind, i) in enumerate(MOE[2:-2]):
                        j, c = i // 4, i % 4
                        if MOE[2 + n - 3] in [("route", 4 * t + 3) for t in range(NJ)]:
                            t = MOE[2 + n - 3][1] // 4
                            act.wait_ge(gap_up.sem, gap_up.at(b, t + 1))
                            nc.scalar.activation(sel[:, t % 2, 0, :], sel[:, t % 2, 0, :], ACT.Tanh, scale=0.5
                                                 ).then_inc(tanh_up.sem, 1)
                        if kind == "route":
                            act.wait_ge(m_done.sem, m_done.at(b, MOE_AT[(kind, i)] + 1))
                            if c == 0:
                                if c_up.begun(b, j - 1):
                                    act.wait_ge(c_up.sem, c_up.at(b, j - 1))
                            nc.scalar.copy(lg[:, j % 2, 2 * c:2 * c + 2, :],
                                           m_bank[MOE_AT[(kind, i)] % MOE_BANKS][:, :]
                                           .rearrange("p (e o) -> p e o", e=2)).then_inc(lg_up.sem, 1)
                        slot += 2
                        yield slot
                    norm_square(act, b, m_ln, 1, ma)

                prepare()
                rounds(act, front, moe, None)

            @block.vector
            def _(dve):
                def prepare():
                    nc.vector.memset(xr[:, 0:KC - 1], 0.0)
                    for n in range(1, len(units), 2):
                        dve.wait_ge(prep_done.sem, prep_done.at(0, n + 1))
                        dst = units[n][2]
                        nc.vector.tensor_copy(dst, bank[n % 4][:, 0:dst.shape[1] * dst.shape[2]]
                                              .rearrange("p (k c) -> p k c", k=dst.shape[1])).then_inc(prep_dve.sem, 1)
                    dve.wait_ge(prep_act.sem, prep_act.at(0, (len(units) + 1) // 2 + 1))
                    nc.vector.tensor_scalar(A_neg[:, :], A_neg[:, :], -1.0, None, ALU.mult).then_inc(prep_dve.sem, 1)
                    dve.wait_ge(small_in.sem, small_in.at(0, 7))
                    dve.wait_ge(bias_split.sem, bias_split.at(0, 1))
                    nc.vector.tensor_tensor(sp_r[:, 0:32], sp_u[:, 0:32], parts[:, 0, 0, 0:32], ALU.subtract
                                            ).then_inc(prep_dve.sem, 1)
                    dve.wait_ge(bias_split.sem, bias_split.at(0, 2))
                    nc.vector.tensor_tensor(parts[:, 0, 2, 0:32], sp_r[:, 0:32], parts[:, 0, 1, 0:32], ALU.subtract
                                            ).then_inc(bias_split.sem, 1)

                def soft_plus(b, ct, own):
                    exact = dtx[:, :]
                    if hi_up.begun(b, 2 * ct):
                        dve.wait_ge(hi_up.sem, hi_up.at(b, 2 * ct))
                    if rem_up.begun(b, 2 * ct):
                        dve.wait_ge(rem_up.sem, rem_up.at(b, 2 * ct))
                    dve.wait_ge(sp_exp.sem, sp_exp.at(b, ct + 1))
                    nc.vector.tensor_scalar(exact, sp_u[:, :], 1.0, -1.0, ALU.add, ALU.add).then_inc(own.sem, 1)
                    dve.wait_ge(own.sem, own.next())
                    nc.vector.tensor_tensor(exact, sp_u[:, :], exact, ALU.subtract).then_inc(own.sem, 1)
                    dve.wait_ge(own.sem, own.next())
                    dve.wait_ge(sp_ln.sem, sp_ln.at(b, ct + 1))
                    nc.vector.tensor_tensor(exact, exact, sp_w[:, :], ALU.add).then_inc(own.sem, 1)
                    dve.wait_ge(own.sem, own.next())
                    nc.vector.tensor_tensor(sp_r[:, :], sp_r[:, :], exact, ALU.add).then_inc(dt_up.sem, 1)

                def convolve(b, ct, own):
                    dst = xact[:, ct % 2, :]
                    tap = lambda k: per_ch[:, ct, TAP + k:TAP + k + 1]
                    dve.wait_ge(xr_up.sem, xr_up.at(b, ct + 1))
                    nc.vector.tensor_scalar(dst, xr[:, 0:T], tap(0), per_ch[:, ct, CNB:CNB + 1],
                                            ALU.mult, ALU.add).then_inc(own.sem, 1)
                    dve.wait_ge(own.sem, own.next())
                    for k in range(1, KC):
                        ins = nc.vector.scalar_tensor_tensor(dst, xr[:, k:k + T], tap(k), dst, ALU.mult, ALU.add)
                        if k < KC - 1:
                            ins.then_inc(own.sem, 1)
                            dve.wait_ge(own.sem, own.next())
                    ins.then_inc(conv_up.sem, 1)

                def take_c(b, ct):
                    dve.wait_ge(f_done.sem, f_done.at(b, FRONT_AT[("C", ct)] + 1))
                    if c_out.begun(b, ct):
                        dve.wait_ge(c_out.sem, c_out.at(b, ct))
                    nc.vector.tensor_copy(bc_sb[:, 1, :], bank[FRONT_AT[("C", ct)] % FRONT_BANKS][:, :]
                                          ).then_inc(csb_up.sem, 1)

                def dt_times_x(b, ct):
                    dve.wait_ge(xact_up.sem, xact_up.at(b, ct + 1))
                    dve.wait_ge(dt_up.sem, dt_up.at(b, ct + 1))
                    nc.vector.tensor_tensor(dtx[:, :], sp_r[:, :], xact[:, ct % 2, :], ALU.mult).then_inc(dtx_up.sem, 1)

                def input_term(b, s):
                    g, n = s // 8, FRONT_AT[("dtx", s)]
                    dve.wait_ge(f_done.sem, f_done.at(b, n + 1))
                    if s % 8 == 0:
                        dve.wait_ge(b_in[g % B_BUFS].sem, b_in[g % B_BUFS].at(b, g // B_BUFS + 1))
                    nc.vector.tensor_tensor(u[:, s % U_BUFS, :], bank[n % FRONT_BANKS][:, :], b_rep[:, g % B_BUFS, :],
                                            ALU.mult).then_inc(u_up.sem, 1)

                def scan(b, s):
                    dve.wait_ge(dA_up.sem, dA_up.at(b, s + 1))
                    dve.wait_ge(u_up.sem, u_up.at(b, s + 1))
                    if hc_up.begun(b, s - H_BUFS + 1):
                        dve.wait_ge(hc_up.sem, hc_up.at(b, s - H_BUFS + 1))
                    nc.vector.tensor_tensor_scan(h[:, s % H_BUFS, :], bank[FRONT_AT[("dA", s)] % FRONT_BANKS][:, :],
                                                 u[:, s % U_BUFS, :], 0.0, ALU.mult, ALU.add).then_inc(h_up.sem, 1)

                def gate(b, ct):
                    dve.wait_ge(ysum.sem, ysum.at(b, (ct + 1) * NT))
                    nc.vector.scalar_tensor_tensor(yz[:, ct, :], xact[:, ct % 2, :], per_ch[:, ct, DSK:DSK + 1],
                                                   y_bank[:, :], ALU.mult, ALU.add).then_inc(y_read.sem, 1)
                    dve.wait_ge(y_read.sem, y_read.at(b, ct + 1))
                    dve.wait_ge(zs_up.sem, zs_up.at(b, ct + 1))
                    nc.vector.tensor_tensor(yz[:, ct, :], yz[:, ct, :], zs[:, ct % 2, :], ALU.mult).then_inc(yz_up.sem, 1)

                def front(b, moe):
                    own = Steps(f_step, b)
                    dve.wait_ge(x0_in.sem, x0_in.at(b, 1))
                    norm_mean(dve, own, f_ln, x0[:, :, :])
                    norm_var(dve, b, f_ln, 0, 0, EPS)
                    norm_apply(dve, b, f_ln, 0, fa, x0).then_inc(xn0.sem, 1)
                    run_until(moe, 0)
                    dve.wait_ge(f_done.sem, f_done.at(b, FRONT_AT[("dtr", 0)] + 1))
                    nc.vector.tensor_copy(dtr[:, :], bank[FRONT_AT[("dtr", 0)] % FRONT_BANKS][:, :]).then_inc(dtr_up.sem, 1)
                    dve.wait_ge(f_done.sem, f_done.at(b, FRONT_AT[("B", 0)] + 1))
                    if b_out.begun(b, 0):
                        dve.wait_ge(b_out.sem, b_out.at(b, 0))
                    nc.vector.tensor_copy(bc_sb[:, 0, :], bank[FRONT_AT[("B", 0)] % FRONT_BANKS][:, :]
                                          ).then_inc(bsb_up.sem, 1)
                    soft_plus(b, 0, own)
                    convolve(b, 0, own)
                    take_c(b, 0)
                    dt_times_x(b, 0)
                    run_until(moe, 1)
                    input_term(b, 0)
                    for s in range(NCT * NT):
                        ct, i = s // NT, s % NT
                        ahead = i < NT - 1 and not (i in UNIT_AT and ct + 1 < NCT)
                        if s + 1 < NCT * NT and ahead:
                            input_term(b, s + 1)
                        scan(b, s)
                        if s + 1 < NCT * NT and not ahead:
                            input_term(b, s + 1)
                        if ct + 1 < NCT:
                            if i == 3:
                                soft_plus(b, ct + 1, own)
                            if i == 4:
                                convolve(b, ct + 1, own)
                            if i == 5:
                                take_c(b, ct + 1)
                            if i == 7:
                                dt_times_x(b, ct + 1)
                        if i == GATE_AT and ct > 0:
                            gate(b, ct - 1)
                        run_until(moe, 8 + s)
                    gate(b, NCT - 1)
                    run_until(moe, 8 + NCT * NT)
                    dve.wait_ge(fo_up.sem, fo_up.at(b, NJ))
                    norm_mean(dve, own, f_ln, fa[:, :, :])
                    norm_var(dve, b, f_ln, 1, 1, EPS)
                    norm_apply(dve, b, f_ln, 1, fa, fa).then_inc(own.sem, 1)
                    dve.wait_ge(own.sem, own.next())
                    run_until(moe, LAST)
                    if moe is not None:
                        dve.wait_ge(x2_up.sem, x2_up.at(b, 0))
                    nc.vector.tensor_tensor(x1[:, :, :], x0[:, :, :], fa[:, :, :], ALU.add).then_inc(x1_up.sem, 1)
                    own.end()

                def tournament(own, src):
                    tt = nc.vector.tensor_tensor
                    tt(hi_t[:, 0:4, :], src[:, 0:4, :], src[:, 4:8, :], ALU.max)
                    tt(lo_t[:, 0:4, :], src[:, 0:4, :], src[:, 4:8, :], ALU.min).then_inc(own.sem, 1)
                    dve.wait_ge(own.sem, own.next())
                    for w in (2, 1):
                        tt(lo_t[:, 0:w, :], lo_t[:, 0:w, :], lo_t[:, w:2 * w, :], ALU.max).then_inc(own.sem, 1)
                        dve.wait_ge(own.sem, own.next())
                        tt(lo_t[:, w:2 * w, :], hi_t[:, 0:w, :], hi_t[:, w:2 * w, :], ALU.min).then_inc(own.sem, 1)
                        dve.wait_ge(own.sem, own.next())
                        tt(hi_t[:, 0:w, :], hi_t[:, 0:w, :], hi_t[:, w:2 * w, :], ALU.max).then_inc(own.sem, 1)
                        dve.wait_ge(own.sem, own.next())
                        tt(lo_t[:, 0:w, :], lo_t[:, 0:w, :], lo_t[:, w:2 * w, :], ALU.max).then_inc(own.sem, 1)
                        dve.wait_ge(own.sem, own.next())

                def moe(b):
                    own = Steps(m_step, b)
                    dve.wait_ge(x1_up.sem, x1_up.at(b, 1))
                    norm_mean(dve, own, m_ln, x1[:, :, :])
                    norm_var(dve, b, m_ln, 0, 0, EPS)
                    norm_apply(dve, b, m_ln, 0, ma, x1).then_inc(xm_up.sem, 1)
                    yield 12
                    slot = 12

                    def weights(j):
                        dve.wait_ge(lg_up.sem, lg_up.at(b, 4 * j + 4))
                        if d1_up.begun(b, j):
                            dve.wait_ge(d1_up.sem, d1_up.at(b, j))
                        tournament(own, lg[:, j % 2, :, :])
                        nc.vector.tensor_tensor(sel[:, j % 2, 0, :], hi_t[:, 0, :], lo_t[:, 0, :], ALU.subtract
                                                ).then_inc(gap_up.sem, 1)

                    def sums(j):
                        dve.wait_ge(tanh_up.sem, tanh_up.at(b, j + 1))
                        nc.vector.tensor_scalar(sel[:, j % 2, 1, :], sel[:, j % 2, 0, :], -0.5, 0.5, ALU.mult, ALU.add).then_inc(own.sem, 1)
                        dve.wait_ge(own.sem, own.next())
                        dve.wait_ge(d1_up.sem, d1_up.at(b, j + 1))
                        for e in range(NE):
                            spare = spares[:, e, :]
                            for i, op, dst in ((1, ALU.is_ge, spare), (0, ALU.is_gt, lg[:, j % 2, e, :])):
                                ins = nc.vector.scalar_tensor_tensor(dst, lg[:, j % 2, e, :], 0.0,
                                                                     sel[:, j % 2, i, :], op, ALU.mult,
                                                                     accum_out=gate_c[:, i, e:e + 1])
                        ins.then_inc(own.sem, 1)
                        dve.wait_ge(own.sem, own.next())
                        nc.vector.tensor_tensor(gate_c[:, 0, :], gate_c[:, 0, :], gate_c[:, 1, :], ALU.add
                                                ).then_inc(c_up.sem, 1)

                    def mix(j, c):
                        if c == 0:
                            dve.wait_ge(c_up.sem, c_up.at(b, j + 1))
                        dve.wait_ge(m_done.sem, m_done.at(b, MOE_AT[("expert", 4 * j + c)] + 1))
                        src = m_bank[MOE_AT[("expert", 4 * j + c)] % MOE_BANKS]
                        dst = [ma[:, j, :], acc]
                        for e in range(2):
                            w = gate_c[:, 0, 2 * c + e:2 * c + e + 1]
                            x = src[:, e * DM:(e + 1) * DM]
                            if c == 0:
                                ins = nc.vector.tensor_scalar(dst[e], x, w, None, ALU.mult)
                            else:
                                ins = nc.vector.scalar_tensor_tensor(dst[e], x, w, dst[e], ALU.mult, ALU.add)
                        ins.then_inc(mix_up.sem, 1)
                        dve.wait_ge(mix_up.sem, mix_up.at(b, 4 * j + c + 1))
                        if c == 3:
                            nc.vector.tensor_tensor(ma[:, j, :], ma[:, j, :], acc, ALU.add).then_inc(own.sem, 1)
                            dve.wait_ge(own.sem, own.next())

                    for kind, i in MOE[2:-2]:
                        j, c = i // 4, i % 4
                        if kind == "route" and c == 3:
                            weights(j)
                        if kind == "expert":
                            if c == 0:
                                sums(j)
                            mix(j, c)
                        slot += 2
                        yield slot
                    norm_mean(dve, own, m_ln, ma[:, :, :])
                    norm_var(dve, b, m_ln, 1, 1, EPS)
                    norm_apply(dve, b, m_ln, 1, ma, ma).then_inc(own.sem, 1)
                    dve.wait_ge(own.sem, own.next())
                    nc.vector.tensor_tensor(x2_slice(b), x1[:, :, :], ma[:, :, :], ALU.add).then_inc(x2_up.sem, 1)
                    own.end()

                prepare()
                rounds(dve, front, moe, None)

            @block.gpsimd
            def _(pool):
                def prepare():
                    def select(ap, pattern, base, mult, op, fill=0.0):
                        return nc.gpsimd.affine_select(out=ap, in_=ap, compare_op=op, fill=fill, base=base,
                                                       pattern=pattern, channel_multiplier=mult)
                    nc.gpsimd.memset(ident[:, :], 1.0)
                    nc.gpsimd.memset(ones_bf[:, :], 1.0)
                    nc.gpsimd.memset(neg_half[:, :], -0.5)
                    nc.gpsimd.memset(one_hot[:, :, :], 1.0)
                    nc.gpsimd.memset(state_sum[:, :, :], 1.0).then_inc(consts.sem, 1)
                    pool.wait_ge(consts.sem, consts.at(0, 1))
                    select(ident[:, :], [[-1, P]], 0, 1, ALU.is_equal).then_inc(consts.sem, 1)
                    for part in range(3):
                        pool.wait_ge(consts.sem, consts.at(0, 2 + part))
                        select(one_hot[32 * part:32 * part + 32, :, :].rearrange("r k (p n) -> r k p n", p=NP),
                               [[-NP, 4], [-1, NP], [0, NS]], 0, 1, ALU.is_equal).then_inc(consts.sem, 1)
                    pool.wait_ge(consts.sem, consts.at(0, 5))
                    select(state_sum[:, :, :], [[NP * NS, 4], [-NS, 32]], 0, 1, ALU.is_ge).then_inc(consts.sem, 1)
                    pool.wait_ge(consts.sem, consts.at(0, 6))
                    select(state_sum[:, :, :], [[-NP * NS, 4], [NS, 32]], NS - 1, -1, ALU.is_ge).then_inc(consts.sem, 1)
                    pool.wait_ge(consts.sem, consts.at(0, 7))

                def remainder(b, ct, v):
                    pool.wait_ge(hi_up.sem, hi_up.at(b, 2 * ct + v + 1))
                    if lo_up.begun(b, 2 * ct + v):
                        pool.wait_ge(lo_up.sem, lo_up.at(b, 2 * ct + v))
                    nc.gpsimd.tensor_tensor(rem[:, :], (dtx if v else sp_r)[:, :], parts[:, v, 0, :], ALU.subtract
                                            ).then_inc(rem_up.sem, 1)

                def low_part(b, ct, v):
                    pool.wait_ge(mid_up.sem, mid_up.at(b, 2 * ct + v + 1))
                    nc.gpsimd.tensor_tensor(parts[:, v, 2, :], rem[:, :], parts[:, v, 1, :], ALU.subtract
                                            ).then_inc(lo_up.sem, 1)

                def output_term(b, s):
                    hd = s // 2
                    if s % 2 == 0:
                        pool.wait_ge(c_in[hd % C_BUFS].sem, c_in[hd % C_BUFS].at(b, hd // C_BUFS + 1))
                    pool.wait_ge(h_up.sem, h_up.at(b, s + 1))
                    if ysum.begun(b, s - HC_BUFS + 1):
                        pool.wait_ge(ysum.sem, ysum.at(b, s - HC_BUFS + 1))
                    nc.gpsimd.tensor_tensor(hc[:, s % HC_BUFS, :], h[:, s % H_BUFS, :], c_rep[:, hd % C_BUFS, :],
                                            ALU.mult).then_inc(hc_up.sem, 1)

                def front(b, moe):
                    norm_rstd(pool, b, f_ln, 0)
                    run_until(moe, 0)
                    for v in range(2):
                        remainder(b, 0, v)
                        low_part(b, 0, v)
                    run_until(moe, 1)
                    for s in range(NCT * NT):
                        ct, i = s // NT, s % NT
                        output_term(b, s)
                        if ct + 1 < NCT:
                            if i == 7:
                                remainder(b, ct + 1, 0)
                            if i == 9:
                                low_part(b, ct + 1, 0)
                            if i == 10:
                                remainder(b, ct + 1, 1)
                            if i == 12:
                                low_part(b, ct + 1, 1)
                        run_until(moe, 8 + s)
                    norm_rstd(pool, b, f_ln, 1)
                    run_until(moe, LAST)

                def moe(b):
                    norm_rstd(pool, b, m_ln, 0)
                    yield 14
                    slot = 14
                    for kind, i in MOE[2:-2]:
                        j, c = i // 4, i % 4
                        if kind == "route" and c == 3:
                            pool.wait_ge(gap_up.sem, gap_up.at(b, j + 1))
                            nc.gpsimd.tensor_tensor(lg[:, j % 2, :, :], lg[:, j % 2, :, :],
                                                    lo_t[:, 0:1, :].to_broadcast([P, NE, DM]), ALU.subtract
                                                    ).then_inc(d1_up.sem, 1)
                        slot += 2
                        yield slot
                    norm_rstd(pool, b, m_ln, 1)

                prepare()
                rounds(pool, front, moe, None)

        with ExitStack() as ctx:
            def sb(name, shape, dt=F32):
                return ctx.enter_context(nc.sbuf_tensor(name, shape, dt))

            Wv, Wr, Wo, Wcr = (sb(n, [P, KD, DM]) for n in ("Wv", "Wr", "Wo", "Wcr"))
            Wck = sb("Wck", [P, KD, 4 * DM])
            Wcv = sb("Wcv", [P, NI, DM])
            rows = sb("rows", [P, 5, DM])
            cols = sb("cols", [P, KD, 6])
            w12 = sb("w12", [P, 2, NI, DM])
            w3 = sb("w3", [P, KD, HID])
            w1T, w2T = sb("w1T", [P, KD, HID]), sb("w2T", [P, KD, HID])
            w3T = sb("w3T", [P, NM, DM])
            absum, recip = sb("absum", [P, 4]), sb("recip", [P, 4])
            ones = sb("ones", [P, P])
            decay = sb("decay", [P, KD, T])
            ramp = sb("ramp", [P, 3, T])

            ta, tb = sb("ta", [P, NJ, DM]), sb("tb", [P, NJ, DM])
            rt = sb("rt", [P, NJ, DM])
            featT = sb("featT", [P, KD, 1 + T])
            mixT = sb("mixT", [P, KD, T])
            vjunk = sb("vjunk", [P, KD, T], BF16)
            vmix = sb("vmix", [P, KD])
            qh = sb("qh", [P, 1, DM])
            kr = sb("kr", [P, 2, T])
            kcT = sb("kcT", [P, NI, T])
            r_stat = sb("r_stat", [P, 5, NJ])
            r1 = sb("r1", [P, NJ])
            fb = sb("fb", [P, NJ, DM])
            fT = sb("fT", [P, KD, T])
            th = sb("th", [P, 2, T])
            hid = sb("hid", [P, NM, T])
            x4 = sb("x4", [P, NJ, DM])
            g_stat = sb("g_stat", [P, 5, NJ])
            r_bank, g_bank = bank[0:4], bank[4:8]

            rwkv_in, tern_in = sig("rwkv_in", 0, 16), sig("tern_in", 0, 16)
            r_consts, ramp_up, decay_up, abs_up, tot_up, rec_up = (
                sig(n, 0) for n in ("r_consts", "ramp_up", "decay_up", "abs_up", "tot_up", "rec_up"))
            tern_up, turned, turned_up = (sig(n, 0) for n in ("tern_up", "turned", "turned_up"))
            t_step = sig("t_step", 0)
            r_ln = Norm("r", r_stat, 5, 6)
            r_done = sig("r_done", sum(n[0] != "pad" for n in RWKV))
            ln1_up, tm_up, cm_up = sig("ln1_up"), sig("tm_up"), sig("cm_up")
            tT_up, cT_up = sig("tT_up", KD), sig("cT_up", KD)
            mix_in, vmix_up = sig("mix_in", KD), sig("vmix_up", KD)
            r_up, q_up, xa_up = sig("r_up", 2), sig("q_up"), sig("xa_up")
            relu_up, kc_up = sig("relu_up", NI), sig("kc_up", NI)
            cr_up, att_up, x3_up = sig("cr_up", 2), sig("att_up", 2), sig("x3_up")
            r_step = sig("r_step", R_STEPS)

            g_ln = Norm("g", g_stat, 2, 2, sb("g_junk", [P, NJ, DM], BF16))
            g_done = sig("g_done", len(FFN))
            xg_up, fT_up = sig("xg_up"), sig("fT_up", KD)
            th_up, hid_up, w3_up = sig("th_up", NM), sig("hid_up", NM), sig("w3_up", 2)
            x4_up, sent = sig("x4_up"), sig("sent", 1, 16)
            g_step = sig("g_step", 3)

            N_RWKV_IN, N_TERN_IN = 6 + 5 + 6, 3
            r_bank_of = lambda name: r_bank[RWKV_AT[name] % 4]
            g_bank_of = lambda name: g_bank[FFN_AT[name] % 4]
            r_count = lambda name: 1 + sum(n[0] != "pad" for n in RWKV[:RWKV_AT[name]])
            n_ch = [min(P, HID - m * P) for m in range(NM)]

            turns = []
            half = NI // 2
            for v, dst in ((0, w1T), (1, w2T)):
                for k in range(KD):
                    for g in range(2):
                        turns.append(([(t * HR, w12[0:HR, v, g * half + t, k * P:(k + 1) * P]) for t in range(half)],
                                      P, half * HR, dst[:, k, g * half * HR:(g + 1) * half * HR], 1 + v))
            for m in range(NM):
                turns.append(([(t * P, w3[:, t, m * P:m * P + n_ch[m]]) for t in range(KD)],
                              n_ch[m], DM, w3T[0:n_ch[m], m, :], 3))

            def x2_of(b):
                if isinstance(b, int):
                    return x2_all[:, b, :, :]
                return x2_all[:, bass.ds(b, 1), :, :].rearrange("p b j d -> p (b j) d")

            block = ctx.enter_context(nc.Block())

            @block.sync
            def _(sp):
                w = lambda n: a["L1_attn_" + n]
                by_ch = lambda ap: ap.rearrange("(c p) -> p c", p=P)
                load = lambda dst, src, s=rwkv_in, **kw: sp.dma_start(dst, src, **kw).then_inc(s.sem, 16)
                for i, n in ((G1, "ln1_g"), (B1, "ln1_b"), (G2, "ln2_g"), (B2, "ln2_b"), (BO, "bo")):
                    load(rows[:, i, :], w(n).unsqueeze(0).to_broadcast([P, DM]))
                for i, n in ((TG, "tm_g"), (TB, "tm_b"), (CG, "cm_g"), (CBE, "cm_b"), (TF, "time_first"), (TD, "time_decay")):
                    load(cols[:, :, i], by_ch(w(n)), allow_slow_non_contiguous=True)
                for dst, n in ((Wv, "Wv"), (Wr, "Wr"), (Wo, "Wo"), (Wck, "Wck"), (Wcr, "Wcr"), (Wcv, "Wcv")):
                    load(dst[:, :, :], w(n).rearrange("(k p) n -> p k n", p=P))
                for v, n in enumerate(("w1", "w2")):
                    load(w12[0:HR, v, :, :], a["L1_ffn_" + n].rearrange("(t p) d -> p t d", p=HR), tern_in)
                load(w3[:, :, :], a["L1_ffn_w3"].rearrange("(t p) d -> p t d", p=P), tern_in)

                def send(b):
                    sp.wait_ge(x4_up.sem, x4_up.at(b, 1))
                    sp.dma_start(at_b(out, b).rearrange("b (j p) d -> p (b j) d", p=P), x4[:, :, :]
                                 ).then_inc(sent.sem, 16)
                with sp.Fori(0, NB) as b:
                    send(b)
                sp.wait_ge(sent.sem, sent.at(0, NB))

            @block.tensor
            def _(pe):
                def group(dst, pairs):
                    for k, (l, r) in enumerate(pairs):
                        ins = nc.tensor.matmul(dst, l, r, start=(k == 0), stop=(k == len(pairs) - 1))
                    return ins

                def prepare():
                    yield 3
                    pe.wait_ge(abs_up.sem, abs_up.at(0, 3))
                    pe.wait_ge(r_consts.sem, r_consts.at(0, 1))
                    nc.tensor.matmul(g_bank[3][:, 0:4], ones[:, :], absum[:, :], start=True, stop=True
                                     ).then_inc(turned.sem, 1)
                    yield 8
                    for n, (srcs, m, _, _, v) in enumerate(turns):
                        pe.wait_ge(tern_up.sem, tern_up.at(0, v))
                        if n >= 4:
                            pe.wait_ge(turned_up.sem, turned_up.at(0, n - 3))
                        if n == 3:
                            pe.wait_ge(tot_up.sem, tot_up.at(0, 1))
                        for col, src in srcs:
                            w = src.shape[0]
                            ins = nc.tensor.transpose(g_bank[n % 4][0:m, col:col + w], src, ident[0:w, 0:w])
                        ins.then_inc(turned.sem, 1)
                        yield 20 + 4 * n
                    pe.wait_ge(turned_up.sem, turned_up.at(0, len(turns)))

                def mix(b, ffn):
                    at = lambda t: run_until(ffn, t)

                    def free(name):
                        n = RWKV_AT[name]
                        m = n - 4
                        while RWKV[m][0] == "pad":
                            m -= 4
                        kind, i = RWKV[m]
                        s, k = {"tT": (tT_up, i + 1), "v": (vmix_up, i + 1), "r": (r_up, i + 1), "q": (q_up, 1),
                                "cT": (cT_up, i + 1), "ck": (relu_up, i + 1), "cr": (cr_up, i + 1),
                                "cv": (att_up, i + 1)}[kind]
                        if s.begun(b, k if m >= 0 else k - s.per_batch):
                            pe.wait_ge(s.sem, s.at(b, k if m >= 0 else k - s.per_batch))
                        return r_bank_of(name)

                    def turn(kind, src):
                        for k in range(KD):
                            transpose_tiles(free((kind, k)), src, k).then_inc(r_done.sem, 1)

                    now = lambda j: featT[:, :, 1 + j * P:1 + (j + 1) * P]
                    at(40)
                    pe.wait_ge(tm_up.sem, tm_up.at(b, 1))
                    turn("tT", tb)
                    at(50)
                    pe.wait_ge(tT_up.sem, tT_up.at(b, KD))
                    for m in range(KD):
                        group(free(("v", m))[:, :], [(Wv[:, k, m * P:(m + 1) * P], featT[:, k, 1:1 + T]) for k in range(KD)]
                              ).then_inc(r_done.sem, 1)
                    at(54)
                    pe.wait_ge(mix_in.sem, mix_in.at(b, KD))
                    for i in range(2):
                        dst = free(("r", i))
                        for j in range(2):
                            t = (2 * i + j) * P
                            ins = group(dst[:, j * DM:(j + 1) * DM], [(mixT[:, k, t:t + P], Wr[:, k, :]) for k in range(KD)])
                        ins.then_inc(r_done.sem, 1)
                    at(58)
                    pe.wait_ge(vmix_up.sem, vmix_up.at(b, KD))
                    group(free(("q", 0))[:, 0:DM], [(vmix[:, k:k + 1].to_broadcast([P, P]), Wo[:, k, :]) for k in range(KD)]
                          ).then_inc(r_done.sem, 1)
                    at(90)
                    pe.wait_ge(cm_up.sem, cm_up.at(b, 1))
                    turn("cT", tb)
                    for m in range(NI):
                        at(100 + 2 * m)
                        pe.wait_ge(cT_up.sem, cT_up.at(b, KD))
                        group(free(("ck", m))[:, :], [(Wck[:, k, m * P:(m + 1) * P], featT[:, k, 0:T]) for k in range(KD)]
                              ).then_inc(r_done.sem, 1)
                    at(116)
                    for i in range(2):
                        dst = free(("cr", i))
                        for j in range(2):
                            t = 1 + (2 * i + j) * P
                            ins = group(dst[:, j * DM:(j + 1) * DM], [(featT[:, k, t:t + P], Wcr[:, k, :]) for k in range(KD)])
                        ins.then_inc(r_done.sem, 1)
                    at(120)
                    pe.wait_ge(kc_up.sem, kc_up.at(b, NI))
                    for i in range(2):
                        dst = free(("cv", i))
                        for j in range(2):
                            t = (2 * i + j) * P
                            ins = group(dst[:, j * DM:(j + 1) * DM], [(kcT[:, m, t:t + P], Wcv[:, m, :]) for m in range(NI)])
                        ins.then_inc(r_done.sem, 1)
                    at(LAST)

                def ffn(b):
                    def free(name):
                        n = FFN_AT[name]
                        kind, i = FFN[n - 4]
                        s, k = {"fT": (fT_up, i + 1), "w1": (th_up, i + 1), "w2": (hid_up, i + 1),
                                "w3": (w3_up, i + 1)}[kind]
                        if s.begun(b, k if n >= 4 else k - s.per_batch):
                            pe.wait_ge(s.sem, s.at(b, k if n >= 4 else k - s.per_batch))
                        return g_bank_of(name)

                    yield 25
                    pe.wait_ge(xg_up.sem, xg_up.at(b, 1))
                    for k in range(KD):
                        transpose_tiles(free(("fT", k)), fb, k).then_inc(g_done.sem, 1)
                    for m in range(NM):
                        yield 31 + 8 * m
                        pe.wait_ge(fT_up.sem, fT_up.at(b, KD))
                        c = n_ch[m]
                        for kind, w in (("w1", w1T), ("w2", w2T)):
                            group(free((kind, m))[0:c, :], [(w[:, k, m * P:m * P + c], fT[:, k, :]) for k in range(KD)]
                                  ).then_inc(g_done.sem, 1)
                    yield 81
                    pe.wait_ge(hid_up.sem, hid_up.at(b, NM))
                    for i in range(2):
                        dst = free(("w3", i))
                        for j in range(2):
                            t = (2 * i + j) * P
                            ins = group(dst[:, j * DM:(j + 1) * DM],
                                        [(hid[0:n_ch[m], m, t:t + P], w3T[0:n_ch[m], m, :]) for m in range(NM)])
                        ins.then_inc(g_done.sem, 1)

                pe.wait_ge(rwkv_in.sem, rwkv_in.at(0, N_RWKV_IN))
                rounds(pe, mix, ffn, prepare)

            @block.scalar
            def _(act):
                def prepare():
                    yield 1
                    act.wait_ge(tern_in.sem, tern_in.at(0, N_TERN_IN))
                    act.wait_ge(r_consts.sem, r_consts.at(0, 1))
                    for v in range(2):
                        nc.scalar.activation(hid[0:HR, 0:4, :].rearrange("p a t -> p (a t)"),
                                             w12[0:HR, v, :, :].rearrange("p a d -> p (a d)"), ACT.Abs,
                                             accum_out=absum[0:HR, v:v + 1]).then_inc(abs_up.sem, 1)
                        act.wait_ge(abs_up.sem, abs_up.at(0, v + 1))
                    nc.scalar.activation(hid[:, 0:3, :].rearrange("p a t -> p (a t)")[:, 0:KD * HID],
                                         w3[:, :, :].rearrange("p a d -> p (a d)"), ACT.Abs,
                                         accum_out=absum[:, 2:3]).then_inc(abs_up.sem, 1)
                    for n, (srcs, m, width, dst, _) in enumerate(turns):
                        yield 22 + 4 * n
                        act.wait_ge(turned.sem, turned.at(0, n + 2))
                        nc.scalar.copy(dst, g_bank[n % 4][0:m, 0:width]).then_inc(turned_up.sem, 1)

                def take(b, kind, s, gi, bi):
                    for k in range(KD):
                        act.wait_ge(r_done.sem, r_done.at(b, r_count((kind, k))))
                        nc.scalar.activation(featT[:, k, 1:1 + T], r_bank_of((kind, k))[:, :], ACT.Identity,
                                             bias=cols[:, k, bi:bi + 1], scale=cols[:, k, gi:gi + 1]).then_inc(s.sem, 1)

                def mix(b, ffn):
                    at = lambda t: run_until(ffn, t)
                    at(12)
                    norm_square(act, b, r_ln, 0, x2_of(b))
                    at(32)
                    norm_square(act, b, r_ln, 1, tb)
                    at(42)
                    if r_done.begun(b, r_count(("cr", 1)) - r_done.per_batch):
                        act.wait_ge(r_done.sem, r_done.at(b, r_count(("cr", 1)) - r_done.per_batch))
                    take(b, "tT", tT_up, TG, TB)
                    at(56)
                    if att_up.begun(b, 0):
                        act.wait_ge(att_up.sem, att_up.at(b, 0))
                    for i in range(2):
                        act.wait_ge(r_done.sem, r_done.at(b, r_count(("r", i))))
                        nc.scalar.activation(rt[:, 2 * i:2 * i + 2, :].rearrange("p j d -> p (j d)"),
                                             r_bank_of(("r", i))[:, :], ACT.Tanh, scale=0.5).then_inc(r_up.sem, 1)
                    at(72)
                    norm_square(act, b, r_ln, 2, ta)
                    at(82)
                    norm_square(act, b, r_ln, 3, tb)
                    at(92)
                    act.wait_ge(mix_in.sem, mix_in.at(b, KD))
                    take(b, "cT", cT_up, CG, CBE)
                    for m in range(NI):
                        at(101 + 2 * m)
                        act.wait_ge(r_done.sem, r_done.at(b, r_count(("ck", m))))
                        if kc_up.begun(b, m - 1):
                            act.wait_ge(kc_up.sem, kc_up.at(b, m - 1))
                        nc.scalar.activation(kr[:, m % 2, :], r_bank_of(("ck", m))[:, :], ACT.Relu).then_inc(relu_up.sem, 1)
                    at(117)
                    act.wait_ge(xa_up.sem, xa_up.at(b, 1))
                    for i in range(2):
                        act.wait_ge(r_done.sem, r_done.at(b, r_count(("cr", i))))
                        nc.scalar.activation(rt[:, 2 * i:2 * i + 2, :].rearrange("p j d -> p (j d)"),
                                             r_bank_of(("cr", i))[:, :], ACT.Tanh, scale=0.5).then_inc(cr_up.sem, 1)
                    at(132)
                    norm_square(act, b, r_ln, 4, ta)
                    at(LAST)

                def ffn(b):
                    yield 13
                    norm_square(act, b, g_ln, 0, x2_of(b))
                    yield 27
                    for k in range(KD):
                        act.wait_ge(g_done.sem, g_done.at(b, FFN_AT[("fT", k)] + 1))
                        nc.scalar.copy(fT[:, k, :], g_bank_of(("fT", k))[:, :]).then_inc(fT_up.sem, 1)
                    for m in range(NM):
                        yield 33 + 8 * m
                        act.wait_ge(g_done.sem, g_done.at(b, FFN_AT[("w1", m)] + 1))
                        if hid_up.begun(b, m - 1):
                            act.wait_ge(hid_up.sem, hid_up.at(b, m - 1))
                        nc.scalar.activation(th[0:n_ch[m], m % 2, :], g_bank_of(("w1", m))[0:n_ch[m], :], ACT.Tanh,
                                             scale=0.5).then_inc(th_up.sem, 1)
                    yield 83
                    for i in range(2):
                        act.wait_ge(g_done.sem, g_done.at(b, FFN_AT[("w3", i)] + 1))
                        nc.scalar.activation(fb[:, 2 * i:2 * i + 2, :].rearrange("p j d -> p (j d)"),
                                             g_bank_of(("w3", i))[:, :], ACT.Copy, scale=0.5).then_inc(w3_up.sem, 1)
                    yield 87
                    norm_square(act, b, g_ln, 1, fb)

                act.wait_ge(ramp_up.sem, ramp_up.at(0, 1))
                act.wait_ge(rwkv_in.sem, rwkv_in.at(0, N_RWKV_IN))
                for k in range(KD):
                    nc.scalar.activation(decay[:, k, :], ramp[:, 2, :], ACT.Exp, scale=cols[:, k, TD:TD + 1]
                                         ).then_inc(decay_up.sem, 1)
                rounds(act, mix, ffn, prepare)

            @block.vector
            def _(dve):
                stt, tt, ts = nc.vector.scalar_tensor_tensor, nc.vector.tensor_tensor, nc.vector.tensor_scalar

                def prepare():
                    yield 5
                    dve.wait_ge(turned.sem, turned.at(0, 1))
                    ts(recip[:, :], g_bank[3][:, 0:4], 1.0 / (HID * DM), EPS3, ALU.mult, ALU.add).then_inc(tot_up.sem, 1)
                    dve.wait_ge(tot_up.sem, tot_up.at(0, 1))
                    nc.vector.reciprocal(recip[:, :], recip[:, :]).then_inc(rec_up.sem, 1)
                    dve.wait_ge(rec_up.sem, rec_up.at(0, 1))
                    n = 0
                    for v, w in enumerate((w12[0:HR, 0, :, :], w12[0:HR, 1, :, :], w3[:, :, :])):
                        scale = recip[0:w.shape[0], v:v + 1]
                        for in1, in2, op1, op2 in ((scale, MAGIC, ALU.mult, ALU.add), (MAGIC, 1.0, ALU.subtract, ALU.min)):
                            ts(w, w, in1, in2, op1, op2).then_inc(t_step.sem, 1)
                            n += 1
                            dve.wait_ge(t_step.sem, t_step.at(0, n))
                        ts(w, w, -1.0, None, ALU.max).then_inc(tern_up.sem, 1)
                        yield 7

                def mix(b, ffn):
                    at = lambda t: run_until(ffn, t)
                    own = Steps(r_step, b)

                    def affine(dst, src, k_pow, g, beta):
                        dve.wait_ge(r_ln.rstd.sem, r_ln.rstd.at(b, k_pow + 1))
                        for j in range(NJ):
                            ins = stt(dst[:, j, :], src[:, j, :], r_ln.neg[:, j:j + 1], rows[:, g, :], ALU.add, ALU.mult)
                        ins.then_inc(own.sem, 1)
                        dve.wait_ge(own.sem, own.next())
                        for j in range(NJ):
                            ins = stt(dst[:, j, :], dst[:, j, :], r_ln.r[:, j:j + 1], rows[:, beta, :], ALU.mult, ALU.add)
                        ins.then_inc(own.sem, 1)
                        dve.wait_ge(own.sem, own.next())

                    at(10)
                    norm_mean(dve, own, r_ln, x2_of(b))
                    at(14)
                    norm_var(dve, b, r_ln, 0, 0, EPS)
                    at(18)
                    norm_apply(dve, b, r_ln, 0, ta, x2_of(b)).then_inc(own.sem, 1)
                    dve.wait_ge(own.sem, own.next())
                    tt(r_ln.v, r_ln.ss, r_ln.r, ALU.mult).then_inc(own.sem, 1)
                    dve.wait_ge(own.sem, own.next())
                    tt(r_ln.v, r_ln.v, r_ln.r, ALU.mult).then_inc(own.sem, 1)
                    dve.wait_ge(own.sem, own.next())
                    ts(r_ln.v, r_ln.v, 1.0 / DM, EPS2, ALU.mult, ALU.add).then_inc(r_ln.var.sem, 1)
                    at(22)
                    dve.wait_ge(r_ln.rstd.sem, r_ln.rstd.at(b, 2))
                    for j in range(NJ):
                        ins = stt(tb[:, j, :], ta[:, j, :], r_ln.r[:, j:j + 1], rows[:, G1, :], ALU.mult, ALU.mult)
                    ins.then_inc(own.sem, 1)
                    dve.wait_ge(own.sem, own.next())
                    tt(tb[:, :, :], tb[:, :, :], rows[:, B1:B1 + 1, :].to_broadcast([P, NJ, DM]), ALU.add).then_inc(own.sem, 1)
                    dve.wait_ge(own.sem, own.next())
                    at(30)
                    norm_mean(dve, own, r_ln, tb[:, :, :])
                    at(34)
                    norm_var(dve, b, r_ln, 1, 2, EPS2)
                    at(38)
                    norm_apply(dve, b, r_ln, 2, tb, tb).then_inc(tm_up.sem, 1)
                    at(51)
                    for k in range(KD):
                        dve.wait_ge(tT_up.sem, tT_up.at(b, k + 1))
                        tt(mixT[:, k, :], featT[:, k, 1:1 + T], featT[:, k, 0:T], ALU.subtract).then_inc(own.sem, 1)
                        dve.wait_ge(own.sem, own.next())
                        stt(mixT[:, k, :], mixT[:, k, :], cols[:, k, TF:TF + 1], featT[:, k, 0:T], ALU.mult, ALU.add
                            ).then_inc(mix_in.sem, 1)
                    at(52)
                    for m in range(KD):
                        dve.wait_ge(r_done.sem, r_done.at(b, r_count(("v", m))))
                        stt(vjunk[:, m, :], r_bank_of(("v", m))[:, :], 1.0, decay[:, m, :], ALU.mult, ALU.mult,
                            accum_out=vmix[:, m:m + 1]).then_inc(vmix_up.sem, 1)
                    at(60)
                    dve.wait_ge(r_done.sem, r_done.at(b, r_count(("q", 0))))
                    tt(qh[:, 0, :], r_bank_of(("q", 0))[:, 0:DM], rows[:, BO, :], ALU.add).then_inc(q_up.sem, 1)
                    dve.wait_ge(q_up.sem, q_up.at(b, 1))
                    ts(qh[:, 0, :], qh[:, 0, :], 0.5, None, ALU.mult).then_inc(own.sem, 1)
                    dve.wait_ge(own.sem, own.next())
                    dve.wait_ge(r_up.sem, r_up.at(b, 2))
                    stt(rt[:, :, :], rt[:, :, :], 1.0, qh[:, :, :].to_broadcast([P, NJ, DM]), ALU.add, ALU.mult).then_inc(own.sem, 1)
                    dve.wait_ge(own.sem, own.next())
                    tt(ta[:, :, :], ta[:, :, :], rt[:, :, :], ALU.add).then_inc(xa_up.sem, 1)
                    dve.wait_ge(xa_up.sem, xa_up.at(b, 1))
                    at(70)
                    norm_mean(dve, own, r_ln, ta[:, :, :])
                    at(74)
                    norm_var(dve, b, r_ln, 2, 3, EPS2)
                    at(78)
                    affine(tb, ta, 3, G2, B2)
                    at(80)
                    norm_mean(dve, own, r_ln, tb[:, :, :])
                    at(84)
                    norm_var(dve, b, r_ln, 3, 4, EPS2)
                    at(88)
                    norm_apply(dve, b, r_ln, 4, tb, tb).then_inc(cm_up.sem, 1)
                    at(122)
                    dve.wait_ge(cr_up.sem, cr_up.at(b, 2))
                    for i in range(2):
                        part = lambda ap: ap[:, 2 * i:2 * i + 2, :].rearrange("p j d -> p (j d)")
                        dve.wait_ge(r_done.sem, r_done.at(b, r_count(("cv", i))))
                        stt(part(rt), part(rt), 1.0, r_bank_of(("cv", i))[:, :], ALU.add, ALU.mult).then_inc(att_up.sem, 1)
                        dve.wait_ge(att_up.sem, att_up.at(b, i + 1))
                        stt(part(ta), part(rt), 0.5, part(ta), ALU.mult, ALU.add).then_inc(own.sem, 1)
                        dve.wait_ge(own.sem, own.next())
                    at(130)
                    norm_mean(dve, own, r_ln, ta[:, :, :])
                    at(134)
                    norm_var(dve, b, r_ln, 4, 5, EPS)
                    at(138)
                    norm_apply(dve, b, r_ln, 5, ta, ta).then_inc(own.sem, 1)
                    dve.wait_ge(own.sem, own.next())
                    tt(x2_of(b), x2_of(b), ta[:, :, :], ALU.add).then_inc(x3_up.sem, 1)
                    at(LAST)
                    own.end()

                def ffn(b):
                    own = Steps(g_step, b)
                    yield 11
                    dve.wait_ge(x3_up.sem, x3_up.at(b, 1))
                    norm_mean(dve, own, g_ln, x2_of(b))
                    yield 15
                    norm_var(dve, b, g_ln, 0, 0, EPS)
                    yield 19
                    norm_apply(dve, b, g_ln, 0, fb, x2_of(b)).then_inc(xg_up.sem, 1)
                    for m in range(NM):
                        yield 35 + 8 * m
                        c = n_ch[m]
                        dve.wait_ge(g_done.sem, g_done.at(b, FFN_AT[("w2", m)] + 1))
                        dve.wait_ge(th_up.sem, th_up.at(b, m + 1))
                        stt(hid[0:c, m, :], th[0:c, m % 2, :], 1.0, g_bank_of(("w2", m))[0:c, :], ALU.add, ALU.mult
                            ).then_inc(hid_up.sem, 1)
                    yield 85
                    dve.wait_ge(w3_up.sem, w3_up.at(b, 2))
                    norm_mean(dve, own, g_ln, fb[:, :, :])
                    yield 89
                    norm_var(dve, b, g_ln, 1, 1, EPS)
                    yield 93
                    norm_apply(dve, b, g_ln, 1, fb, fb).then_inc(own.sem, 1)
                    dve.wait_ge(own.sem, own.next())
                    if sent.begun(b, 0):
                        dve.wait_ge(sent.sem, sent.at(b, 0))
                    tt(x4[:, :, :], x2_of(b), fb[:, :, :], ALU.add).then_inc(x4_up.sem, 1)
                    own.end()

                nc.vector.memset(featT[:, :, 0:1], 0.0)
                dve.wait_ge(r_consts.sem, r_consts.at(0, 1))
                nc.vector.tensor_tensor_scan(ramp[:, 2, :], ramp[:, 0, :], ramp[:, 1, :], float(T), ALU.mult, ALU.add
                                             ).then_inc(ramp_up.sem, 1)
                dve.wait_ge(rwkv_in.sem, rwkv_in.at(0, N_RWKV_IN))
                dve.wait_ge(decay_up.sem, decay_up.at(0, KD))
                rounds(dve, mix, ffn, prepare)

            @block.gpsimd
            def _(pool):
                def mix(b, ffn):
                    at = lambda t: run_until(ffn, t)
                    for k, t in enumerate((16, 20, 36, 76, 86)):
                        at(t)
                        norm_rstd(pool, b, r_ln, k)
                    for m in range(NI):
                        at(101 + 2 * m)
                        pool.wait_ge(relu_up.sem, relu_up.at(b, m + 1))
                        if m == 0:
                            if r_done.begun(b, 0):
                                pool.wait_ge(r_done.sem, r_done.at(b, 0))
                        nc.gpsimd.tensor_tensor(kcT[:, m, :], kr[:, m % 2, :], kr[:, m % 2, :], ALU.mult
                                                ).then_inc(kc_up.sem, 1)
                    at(136)
                    norm_rstd(pool, b, r_ln, 5)
                    at(LAST)

                def ffn(b):
                    yield 17
                    norm_rstd(pool, b, g_ln, 0)
                    yield 91
                    norm_rstd(pool, b, g_ln, 1)

                nc.gpsimd.memset(absum[:, :], 0.0)
                nc.gpsimd.memset(ones[:, :], 1.0)
                nc.gpsimd.memset(ramp[:, 0, :], 1.0)
                nc.gpsimd.memset(ramp[:, 1, :], -1.0).then_inc(r_consts.sem, 1)
                rounds(pool, mix, ffn, None)



_INS = ["x", "L0_attn_in_proj_w", "L0_attn_dt_in_proj_w", "L0_attn_dt_proj_w", "L0_attn_dt_proj_b",
        "L0_attn_conv_w", "L0_attn_conv_b", "L0_attn_A_log", "L0_attn_D", "L0_attn_out_proj_w",
        "L0_ffn_router_w", "L0_ffn_router_b", "L0_ffn_expert_w", "L0_ffn_expert_b",
        "L1_attn_ln1_g", "L1_attn_ln1_b", "L1_attn_ln2_g", "L1_attn_ln2_b", "L1_attn_tm_g", "L1_attn_tm_b",
        "L1_attn_time_decay", "L1_attn_time_first", "L1_attn_Wv", "L1_attn_Wr", "L1_attn_Wo",
        "L1_attn_bo", "L1_attn_cm_g", "L1_attn_cm_b", "L1_attn_Wck", "L1_attn_Wcv", "L1_attn_Wcr",
        "L1_ffn_w1", "L1_ffn_w2", "L1_ffn_w3"]


def kernel(**inputs):
    import numpy as _np
    import concourse.bacc as _bacc
    from concourse import mybir as _mybir
    from concourse.bass_utils import run_bass_kernel_spmd as _run

    nc = _bacc.Bacc("TRN2", target_bir_lowering=False, num_devices=1)
    arrays, a = {}, {}
    for name in _INS:
        arr = _np.ascontiguousarray(inputs["L0_attn_hidden_states" if name == "x" else name])
        arrays[f"in_{name}_dram"] = arr
        a[name] = nc.dram_tensor(f"in_{name}_dram", arr.shape, _mybir.dt.from_np(arr.dtype), kind="ExternalInput").ap()
    out = nc.dram_tensor("out_0_dram", (NB, T, DM), _mybir.dt.float32, kind="ExternalOutput").ap()
    hybrid_layers_kernel(nc, a, out)
    r = _run(nc, [arrays], core_ids=[0])
    return r.results[0]["out_0_dram"]
```

```python
from contextlib import ExitStack

import concourse.bass as bass
from concourse import mybir

F32 = mybir.dt.float32
BF16 = mybir.dt.bfloat16
F32R = mybir.dt.float32r
ACT = mybir.ActivationFunctionType
ALU = mybir.AluOpType
AX = mybir.AxisListType.X

P = 128
NB, T, DM = 4, 512, 256
NJ = T // P
KD = DM // P
DI, DXB, NS, DTR, KC = 512, 128, 16, 128, 4
NCT = DI // P
NP = P // NS
NT = P // NP
NQ = 4
REP = 4
NH = DI // NS
NG = DXB // NS
NE = 8
HID = 704
HR = HID // 8
NM = -(-HID // P)
NI = 4 * DM // P
EPS, EPS2, EPS3 = 1e-5, 1e-12, 1e-8
MAGIC = 1.5 * 2.0 ** 23

CZ, CX, CC, CB = 0, DI, 2 * DI, 3 * DI
CW = 3 * DI + DXB

STAGES = 4
A_BUFS, U_BUFS, H_BUFS, HC_BUFS, C_BUFS, B_BUFS = 3, 2, 3, 7, 4, 2
Y_LAG, Y_HOLD = 3, 1
GATE_AT = 2

DTB, CNB, DSK, TAP = 0, 1, 2, 3
G1, B1, G2, B2, BO = range(5)
TG, TB, CG, CBE, TF, TD = range(6)
R_STEPS = 19

FRONT_BANKS, MOE_BANKS = 4, 3
UNIT_AT = {1: ("dt", "x"), 5: ("C", "z")}


def front_order():
    names = [("xT", 0), ("xT", 1), ("dtr", 0), ("B", 0)]
    names += [(kind, 0) for pair in UNIT_AT.values() for kind in pair]
    for ct in range(NCT):
        for i in range(NT):
            names += [("dA", ct * NT + i), ("dtx", ct * NT + i)]
            if i in UNIT_AT and ct + 1 < NCT:
                names += [(kind, ct + 1) for kind in UNIT_AT[i]]
    names += [("out", j) for j in range(NJ)]
    assert len(names) % FRONT_BANKS == 0
    return names


def moe_order():
    names = [("mT", 0), ("mT", 1)]
    for j in range(NJ + 1):
        if j < NJ:
            names += [("route", 4 * j + c) for c in range(4)]
        if j > 0:
            names += [("expert", 4 * (j - 1) + c) for c in range(4)]
    names += [("pad", 0), ("pad", 1)]
    assert len(names) % MOE_BANKS == 0
    return names


MOE_EARLY = 6
PE_SLOT = [4, 4] + [5] * (MOE_EARLY - 2) + [8 + 24 * n // 10 for n in range(8 * NJ - MOE_EARLY)]
ACT_SLOT = [5] * MOE_EARLY + [t + 1 for t in PE_SLOT[MOE_EARLY:]]
DVE_SLOT = [8] * 4 + [11] * (MOE_EARLY - 4) + [t + 4 for t in PE_SLOT[MOE_EARLY:]]
POOL_SLOT = [11] * MOE_EARLY + [t + 6 for t in PE_SLOT[MOE_EARLY:]]


def sums_order():
    order, t = [[] for _ in range(NCT * NT + 1)], 0
    for s in range(NCT * NT):
        hold = t > 0 and t % NT == 0 and s < t + Y_LAG + Y_HOLD
        for _ in range(2):
            if not hold and t <= s - Y_LAG:
                if t % NT == 0 and order[s]:
                    break
                order[s].append(t)
                t += 1
    order[-1] = list(range(t, NCT * NT))
    return order


SUMS_AT = sums_order()


def rwkv_order():
    names = [("tT", 0), ("tT", 1), ("v", 0), ("v", 1), ("r", 0), ("r", 1), ("q", 0), ("pad", 0)]
    names += [("cT", 0), ("cT", 1)] + [("ck", m) for m in range(NI)] + [("cr", 0), ("cr", 1)]
    names += [("cv", 0), ("cv", 1), ("pad", 1), ("pad", 2)]
    assert len(names) % 4 == 0
    return names


def ffn_order():
    names = [("fT", 0), ("fT", 1)] + [(w, m) for m in range(NM) for w in ("w1", "w2")] + [("w3", 0), ("w3", 1)]
    assert len(names) % 4 == 0
    return names


FRONT, MOE, RWKV, FFN = front_order(), moe_order(), rwkv_order(), ffn_order()
FRONT_AT, MOE_AT, RWKV_AT, FFN_AT = ({name: n for n, name in enumerate(o)} for o in (FRONT, MOE, RWKV, FFN))


LAST = 1 << 20


class Signal:

    def __init__(self, sem, per_batch, unit=1):
        self.sem, self.per_batch, self.unit = sem, per_batch, unit

    def at(self, b, k):
        if isinstance(b, int):
            return (b * self.per_batch + k) * self.unit
        return b * (self.per_batch * self.unit) + k * self.unit

    def begun(self, b, k):
        return not isinstance(b, int) or b * self.per_batch + k > 0

    def in_register(self, eng, b, k):
        return self.at(b, k) if isinstance(b, int) else eng.to_reg(self.at(b, k))


class Steps:

    def __init__(self, raised, b):
        self.sem, self.raised, self.b, self.k = raised.sem, raised, b, 0

    def next(self):
        self.k += 1
        return self.raised.at(self.b, self.k)

    def end(self):
        assert self.k == self.raised.per_batch, (self.sem, self.k)


def run_until(strand, slot):
    while strand is not None and strand[0] <= slot:
        try:
            strand[0] = next(strand[1])
        except StopIteration:
            strand[0] = LAST + 1
            break


def rounds(eng, first, second, prepare):
    first(0, [0, prepare()] if prepare else None)
    first(1, [0, second(0)])
    with eng.Fori(2, NB) as b:
        first(b, [0, second(b - 1)])
    run_until([0, second(NB - 1)], LAST)


def at_b(ap, b):
    return ap[b:b + 1] if isinstance(b, int) else ap[bass.ds(b, 1)]


def hybrid_layers_kernel(nc, a, out):
    kernel_ctx = ExitStack()
    with kernel_ctx:
        def sig(name, per_batch=1, unit=1):
            return Signal(kernel_ctx.enter_context(nc.semaphore(name)), per_batch, unit)

        def keep(name, shape, dt=F32):
            return kernel_ctx.enter_context(nc.sbuf_tensor(name, shape, dt))

        bank = [kernel_ctx.enter_context(nc.psum_tensor(f"bank{i}", [P, 512], F32)) for i in range(8)]
        ident = keep("ident", [P, P])
        neg_half = keep("neg_half", [P, NJ])
        x2_dram = nc.dram_tensor("x2_dram", [NB, T, DM], F32, kind="Internal").ap()
        consts = sig("consts", 0)

        class Norm:

            def __init__(self, name, stat, n, n_pow):
                self.mean, self.sq = sig(name + "_mean", n), sig(name + "_sq", n)
                self.var, self.rstd = sig(name + "_var", n_pow), sig(name + "_rstd", n_pow)
                self.total, self.neg, self.ss, self.v, self.r = (stat[:, i, :] for i in range(5))

        def norm_mean(dve, own, ln, src):
            nc.vector.tensor_reduce(ln.total, src, AX, ALU.add).then_inc(own.sem, 1)
            dve.wait_ge(own.sem, own.next())
            nc.vector.tensor_scalar(ln.neg, ln.total, -1.0 / DM, None, ALU.mult).then_inc(ln.mean.sem, 1)

        def norm_square(act, b, ln, k, src, junk):
            act.wait_ge(ln.mean.sem, ln.mean.at(b, k + 1))
            for j in range(NJ):
                ins = nc.scalar.activation(junk[:, j, :], src[:, j, :], ACT.Square, bias=ln.neg[:, j:j + 1],
                                           accum_out=ln.ss[:, j:j + 1])
            ins.then_inc(ln.sq.sem, 1)

        def norm_var(dve, b, ln, k, k_pow, eps):
            dve.wait_ge(ln.sq.sem, ln.sq.at(b, k + 1))
            nc.vector.tensor_scalar(ln.v, ln.ss, 1.0 / DM, eps, ALU.mult, ALU.add).then_inc(ln.var.sem, 1)

        def norm_rstd(pool, b, ln, k_pow):
            pool.wait_ge(ln.var.sem, ln.var.at(b, k_pow + 1))
            nc.gpsimd.tensor_tensor(ln.r, ln.v, neg_half[:, :], ALU.pow).then_inc(ln.rstd.sem, 1)

        def norm_apply(dve, b, ln, k_pow, dst, src):
            dve.wait_ge(ln.rstd.sem, ln.rstd.at(b, k_pow + 1))
            for j in range(NJ):
                ins = nc.vector.tensor_scalar(dst[:, j, :], src[:, j, :], ln.neg[:, j:j + 1], ln.r[:, j:j + 1],
                                              ALU.add, ALU.mult)
            return ins

        def transpose_tiles(dst_bank, src, k):
            for j in range(NJ):
                ins = nc.tensor.transpose(dst_bank[:, j * P:(j + 1) * P], src[:, j, k * P:(k + 1) * P], ident[:, :])
            return ins

        with ExitStack() as ctx:
            def sb(name, shape, dt=F32):
                return ctx.enter_context(nc.sbuf_tensor(name, shape, dt))

            ones_bf = sb("ones_bf", [P, P], BF16)
            one_hot = sb("one_hot", [P, 4, P], F32R)
            state_sum = sb("state_sum", [P, 4, 32])
            projT = sb("projT", [P, KD, CW])
            dt_inT = sb("dt_inT", [P, KD, DTR])
            dt_projT = sb("dt_projT", [P, 1, DI])
            outT = sb("outT", [P, NCT, DM])
            A_neg = sb("A_neg", [P, NCT * NT])
            per_ch = sb("per_ch", [P, NCT, 3 + KC])
            routeT = sb("routeT", [P, KD, NE * DM])
            expertT = sb("expertT", [P, KD, NE * DM])

            x0 = sb("x0", [P, NJ, DM])
            fa = sb("fa", [P, NJ, DM])
            xT = sb("xT", [P, KD, T])
            dtr = sb("dtr", [P, T])
            sp_w = sb("sp_w", [P, T])
            sp_ur = sb("sp_ur", [P, 2, T])
            sp_u, sp_r = sp_ur[:, 0, :], sp_ur[:, 1, :]
            x0_again = sp_ur[:, :, :].rearrange("p k (j d) -> p (k j) d", d=DM)
            xr = sb("xr", [P, KC - 1 + T])
            xact = sb("xact", [P, 2, T])
            zs = sb("zs", [P, 2, T])
            bc_sb = sb("bc_sb", [P, 2, T])
            dtx = sb("dtx", [P, T])
            halves = sb("halves", [P, 2, 2, 2, T], F32R)
            bias_part = sb("bias_part", [P, 3, 32], BF16)
            bias_rows = sb("bias_rows", [3, 2, NE * DM], BF16)
            b_rep = sb("b_rep", [P, B_BUFS, T])
            c_rep = sb("c_rep", [P, C_BUFS, T])
            dA = sb("dA", [P, A_BUFS, T])
            u = sb("u", [P, U_BUFS, T])
            h = sb("h", [P, H_BUFS, T])
            hc = sb("hc", [P, HC_BUFS, T])
            yz = sb("yz", [P, NCT, T])
            f_stat = sb("f_stat", [P, 5, NJ])
            b_dram = nc.dram_tensor("b_dram", [NB, DXB, T], F32, kind="Internal").ap()
            c_dram = nc.dram_tensor("c_dram", [NB, DI, T], F32, kind="Internal").ap()
            bias_dram = nc.dram_tensor("bias_dram", [3, 2, NE * DM], BF16, kind="Internal").ap()

            x1 = sb("x1", [P, NJ, DM])
            ma = sb("ma", [P, NJ, DM])
            mT = sb("mT", [P, KD, T])
            lg = sb("lg", [P, 2, NE, DM])
            hi_t, lo_t = sb("hi_t", [P, 4, DM]), sb("lo_t", [P, 4, DM])
            sel = sb("sel", [P, 2, 2, DM])
            gate_c = sb("gate_c", [P, 2, NE])
            spares = hi_t[:, :, :].rearrange("p a d -> p (a d)").bitcast(BF16).rearrange("p (e d) -> p e d", e=NE)
            acc = hi_t[:, 3, :]
            m_stat = sb("m_stat", [P, 5, NJ])
            stage = c_rep
            y_bank = bank[FRONT_BANKS]
            m_bank = bank[FRONT_BANKS + 1:]

            small_in = sig("small_in", 0, 16)
            f_ln = Norm("f", f_stat, 2, 2)
            x0_in, x0_back = sig("x0_in", 1, 16), sig("x0_back", 1, 16)
            xn0 = sig("xn0")
            f_done = sig("f_done", len(FRONT))
            xT_up = sig("xT_up", 2)
            dtr_up = sig("dtr_up")
            bsb_up, csb_up = sig("bsb_up"), sig("csb_up", NCT)
            sp_abs, sp_relu, sp_exp, sp_ln = (sig("sp_" + n, NCT) for n in ("abs", "relu", "exp", "ln"))
            xr_up, conv_up, xact_up, zs_up = (sig(n, NCT) for n in ("xr_up", "conv_up", "xact_up", "zs_up"))
            dt_up, dtx_up = sig("dt_up", NCT), sig("dtx_up", NCT)
            hi_up, lo_up = sig("hi_up", 2 * NCT), sig("lo_up", 2 * NCT)
            b_out, c_out = sig("b_out", 1, 16), sig("c_out", NCT, 16)
            b_in = [sig(f"b_in{i}", NG // B_BUFS, 16) for i in range(B_BUFS)]
            c_in = [sig(f"c_in{i}", NH // C_BUFS, 16) for i in range(C_BUFS)]
            dA_up, u_up, h_up, hc_up, ysum = (sig(n, NCT * NT) for n in ("dA_up", "u_up", "h_up", "hc_up", "ysum"))
            y_read, yz_up = sig("y_read", NCT), sig("yz_up", NCT)
            fo_up = sig("fo_up", NJ)
            x1_up = sig("x1_up")
            f_step = sig("f_step", 3 + 6 * NCT)

            m_ln = Norm("m", m_stat, 2, 2)
            m_done = sig("m_done", sum(n[0] != "pad" for n in MOE))
            xm_up, mT_up = sig("xm_up"), sig("mT_up", 2)
            lg_up = sig("lg_up", 4 * NJ)
            gap_up, d1_up, tanh_up, c_up = (sig(n, NJ) for n in ("gap_up", "d1_up", "tanh_up", "c_up"))
            mix_up = sig("mix_up", 4 * NJ)
            x2_up, x2_out = sig("x2_up"), sig("x2_out", 1, 16)
            m_step = sig("m_step", 3 + 12 * NJ)

            prep_in = [sig(f"prep_in{i}", 0, 16) for i in range(STAGES)]
            prep_done, prep_act, prep_dve = sig("prep_done", 0), sig("prep_act", 0), sig("prep_dve", 0)
            bias_split, bias_out, bias_in = sig("bias_split", 0), sig("bias_out", 0, 16), sig("bias_in", 0, 16)

            def front_reader(name):
                kind, i = name
                return {"xT": xT_up, "dtr": dtr_up, "B": bsb_up, "dt": sp_relu, "x": xr_up, "C": csb_up,
                        "z": zs_up, "dA": dA_up, "dtx": u_up, "out": fo_up}[kind], i + 1

            def moe_reader(name):
                kind, i = name
                return {"mT": mT_up, "route": lg_up, "expert": mix_up}[kind], i + 1

            units = []

            def unit(loads, turns, dst):
                units.append((loads, turns, dst))

            def row_pair(srcs, dst, col):
                m = len(srcs)
                unit([(r * DM, slice(0, P), s) for r, s in enumerate(srcs)],
                     [(k * m * P + r * P, r * DM + k * P) for r in range(m) for k in range(KD)],
                     dst[:, :, col:col + m * P])

            w_in = a["L0_attn_in_proj_w"]
            row = lambda w, t: w[t * P:(t + 1) * P, :]
            row_pair([row(a["L0_attn_dt_in_proj_w"], 0)], dt_inT, 0)
            unit([(0, slice(0, P), a["L0_attn_dt_proj_w"].rearrange("(t p) k -> p t k", p=P))],
                 [(t * P, t * P) for t in range(NCT)], dt_projT[:, :, :])
            row_pair([row(w_in, (DI + DXB) // P)], projT, CB)
            for t in range(0, NCT, 2):
                loads = []
                for r in range(2):
                    for g in range(2):
                        src = w_in[DI + (2 * (t + r) + g) * NS:DI + (2 * (t + r) + g + 1) * NS, :]
                        loads.append((r * DM, slice(g * REP * NS, (g + 1) * REP * NS),
                                      src.unsqueeze(0).to_broadcast([REP, NS, DM])))
                unit(loads, [(k * 2 * P + r * P, r * DM + k * P) for r in range(2) for k in range(KD)],
                     projT[:, :, CX + t * P:CX + (t + 2) * P])
            for t in range(0, NCT, 2):
                row_pair([row(w_in, (DI + 2 * DXB) // P + t + r) for r in range(2)], projT, CC + t * P)
            for t in range(0, NCT, 2):
                row_pair([row(w_in, t + r) for r in range(2)], projT, CZ + t * P)
            for t in range(KD):
                unit([(0, slice(0, P), row(a["L0_attn_out_proj_w"], t))],
                     [(c * P, c * P) for c in range(NCT)], outT[:, :, t * P:(t + 1) * P])
            w_route = a["L0_ffn_router_w"].rearrange("(o e) d -> e o d", e=NE)
            w_expert = a["L0_ffn_expert_w"]
            for w, dst in ((w_route, routeT), (w_expert, expertT)):
                for e in range(NE):
                    row_pair([w[e, 0:P, :], w[e, P:2 * P, :]], dst, e * DM)
            loaded = [0] * STAGES
            unit_loaded = []
            for n, (loads, _, _) in enumerate(units):
                loaded[n % STAGES] += len(loads)
                unit_loaded.append(loaded[n % STAGES])

            block = ctx.enter_context(nc.Block())

            @block.sync
            def _(sp):
                def load_unit(n):
                    if n >= STAGES:
                        sp.wait_ge(prep_done.sem, prep_done.at(0, n - STAGES + 1))
                    for col, pp, src in units[n][0]:
                        width = src.shape[-1] * (src.shape[1] if len(src.shape) == 3 and pp == slice(0, P) else 1)
                        dst = stage[pp, n % STAGES, col:col + width]
                        if len(src.shape) == 3 and pp == slice(0, P):
                            dst = dst.rearrange("p (t k) -> p t k", t=src.shape[1])
                        sp.dma_start(dst, src).then_inc(prep_in[n % STAGES].sem, 16)

                def load_x0(b):
                    sp.dma_start(x0[:, :, :], at_b(a["x"], b).rearrange("b (j p) d -> p (b j) d", p=P)
                                 ).then_inc(x0_in.sem, 16)

                def c_replica(b, hd):
                    freed = hc_up.in_register(sp, b, 2 * (hd - C_BUFS) + 2)
                    if hd % 8 == 0:
                        sp.wait_ge(c_out.sem, c_out.at(b, hd // 8 + 1))
                    if hc_up.begun(b, 2 * (hd - C_BUFS) + 2):
                        sp.wait_ge(hc_up.sem, freed)
                    src = at_b(c_dram, b)[:, hd * NS:(hd + 1) * NS, :].rearrange("b n t -> (b n) t")
                    sp.dma_start(c_rep[:, hd % C_BUFS, :], src.unsqueeze(0).to_broadcast([NP, NS, T])
                                 ).then_inc(c_in[hd % C_BUFS].sem, 16)

                def b_replica(b, g):
                    if g == 0:
                        sp.wait_ge(b_out.sem, b_out.at(b, 1))
                    if u_up.begun(b, 8 * (g - B_BUFS) + 8):
                        sp.wait_ge(u_up.sem, u_up.at(b, 8 * (g - B_BUFS) + 8))
                    src = at_b(b_dram, b)[:, g * NS:(g + 1) * NS, :].rearrange("b n t -> (b n) t")
                    sp.dma_start(b_rep[:, g % B_BUFS, :], src.unsqueeze(0).to_broadcast([NP, NS, T])
                                 ).then_inc(b_in[g % B_BUFS].sem, 16)

                def c_write(b, ct):
                    sp.wait_ge(csb_up.sem, csb_up.at(b, ct + 1))
                    sp.dma_start(at_b(c_dram, b)[:, ct * P:(ct + 1) * P, :].rearrange("b n t -> (b n) t"),
                                 bc_sb[:, 1, :]).then_inc(c_out.sem, 16)

                def front(b, following):
                    sp.wait_ge(bsb_up.sem, bsb_up.at(b, 1))
                    sp.dma_start(at_b(b_dram, b).rearrange("b n t -> (b n) t"), bc_sb[:, 0, :]).then_inc(b_out.sem, 16)
                    for g in range(B_BUFS):
                        b_replica(b, g)
                    c_write(b, 0)
                    for hd in range(C_BUFS):
                        c_replica(b, hd)
                    if following is not None:
                        sp.wait_ge(xn0.sem, xn0.at(b, 1))
                        load_x0(following)
                    for ct in range(NCT):
                        if ct == NCT - 1:
                            sp.wait_ge(lo_up.sem, lo_up.at(b, 2 * NCT))
                            sp.dma_start(x0_again, at_b(a["x"], b).rearrange("b (j p) d -> p (b j) d", p=P)
                                         ).then_inc(x0_back.sem, 16)
                        for i in range(8):
                            hd = 8 * ct + i + C_BUFS
                            if i == 4 and ct + 1 < NCT:
                                c_write(b, ct + 1)
                            if hd < NH:
                                c_replica(b, hd)
                            if i in (3, 7) and 2 * ct + i // 4 + B_BUFS < NG:
                                b_replica(b, 2 * ct + i // 4 + B_BUFS)

                def send_x2(b):
                    sp.wait_ge(x2_up.sem, x2_up.at(b, 1))
                    sp.dma_start(at_b(x2_dram, b).rearrange("b (j p) d -> p (b j) d", p=P), ma[:, :, :]
                                 ).then_inc(x2_out.sem, 16)

                by_ch = lambda ap: ap.rearrange("(c p) -> p c", p=P)
                load_x0(0)
                for n in range(STAGES):
                    load_unit(n)
                for i, nm in ((DTB, "dt_proj_b"), (CNB, "conv_b"), (DSK, "D")):
                    sp.dma_start(per_ch[:, :, i], by_ch(a["L0_attn_" + nm]),
                                 allow_slow_non_contiguous=True).then_inc(small_in.sem, 16)
                sp.dma_start(per_ch[:, :, TAP:TAP + KC], a["L0_attn_conv_w"].rearrange("(c p) k -> p c k", p=P)
                             ).then_inc(small_in.sem, 16)
                sp.dma_start(sp_w[0:NCT * NT, 0:P], a["L0_attn_A_log"].rearrange("(s c) n -> s (c n)", c=NP)
                             ).then_inc(small_in.sem, 16)
                sp.dma_start(sp_u[:, 0:16], a["L0_ffn_router_b"].rearrange("(p i) -> p i", p=P)).then_inc(small_in.sem, 16)
                sp.dma_start(sp_u[:, 16:32], a["L0_ffn_expert_b"].rearrange("e (q i) -> (e q) i", i=16)
                             ).then_inc(small_in.sem, 16)
                for n in range(STAGES, len(units)):
                    load_unit(n)
                sp.wait_ge(bias_split.sem, bias_split.at(0, 3))
                for part in range(3):
                    for v in range(2):
                        sp.dma_start(bias_dram[part, v, :].rearrange("(p i) -> p i", p=P),
                                     bias_part[:, part, 16 * v:16 * v + 16]).then_inc(bias_out.sem, 16)
                sp.wait_ge(bias_out.sem, bias_out.at(0, 6))
                sp.dma_start(bias_rows[:, :, :], bias_dram).then_inc(bias_in.sem, 16)
                front(0, 1)
                with sp.Fori(2, NB) as b:
                    front(b - 1, b)
                    send_x2(b - 2)
                front(NB - 1, None)
                send_x2(NB - 2)
                send_x2(NB - 1)
                sp.wait_ge(x2_out.sem, x2_out.at(NB, 0))

            @block.tensor
            def _(pe):
                def prepare():
                    pe.wait_ge(consts.sem, consts.at(0, 5 + NQ))
                    for n, (loads, turns, dst) in enumerate(units):
                        pe.wait_ge(prep_in[n % STAGES].sem, prep_in[n % STAGES].at(0, unit_loaded[n]))
                        if n >= 4:
                            emptied = prep_act if n % 2 == 0 else prep_dve
                            pe.wait_ge(emptied.sem, emptied.at(0, (n - 4) // 2 + 1))
                        for col, scol in turns:
                            ins = nc.tensor.transpose(bank[n % 4][:, col:col + P], stage[:, n % STAGES, scol:scol + P],
                                                      ident[:, :])
                        ins.then_inc(prep_done.sem, 1)
                    pe.wait_ge(small_in.sem, small_in.at(0, 7))
                    nc.tensor.transpose(y_bank[:, 0:NCT * NT], sp_w[0:NCT * NT, 0:P], ident[0:NCT * NT, 0:NCT * NT]
                                        ).then_inc(prep_done.sem, 1)
                    pe.wait_ge(prep_act.sem, prep_act.at(0, (len(units) + 1) // 2 + 1))
                    pe.wait_ge(prep_dve.sem, prep_dve.at(0, len(units) // 2 + 1))

                def front_bank(b, name):
                    n = FRONT_AT[name]
                    freed_by, k = front_reader(FRONT[n - FRONT_BANKS])
                    if freed_by.begun(b, k if n >= FRONT_BANKS else k - freed_by.per_batch):
                        pe.wait_ge(freed_by.sem, freed_by.at(b, k if n >= FRONT_BANKS else k - freed_by.per_batch))
                    return bank[n % FRONT_BANKS]

                def project(b, name, lhsT, rhs):
                    dst = front_bank(b, name)
                    for k, (l, r) in enumerate(zip(lhsT, rhs)):
                        ins = nc.tensor.matmul(dst[:, :], l, r, start=(k == 0), stop=(k == len(lhsT) - 1))
                    ins.then_inc(f_done.sem, 1)

                x_feat = [xT[:, k, :] for k in range(KD)]

                def unit_product(b, kind, ct):
                    if kind == "dt":
                        pe.wait_ge(dtr_up.sem, dtr_up.at(b, 1))
                        project(b, (kind, ct), [dt_projT[:, 0, ct * P:(ct + 1) * P]], [dtr[:, :]])
                    else:
                        c0 = {"x": CX, "C": CC, "z": CZ}[kind] + ct * P
                        project(b, (kind, ct), [projT[:, k, c0:c0 + P] for k in range(KD)], x_feat)

                def state_sums(b, s):
                    ct, q, k = s // NT, s % NT // 4, s % 4
                    if s % NT == 0:
                        if y_read.begun(b, ct):
                            pe.wait_ge(y_read.sem, y_read.at(b, ct))
                    pe.wait_ge(hc_up.sem, hc_up.at(b, s + 1))
                    nc.tensor.matmul(y_bank[32 * q:32 * q + 32, :], state_sum[:, k, :], hc[:, s % HC_BUFS, :],
                                     start=(k == 0), stop=(k == 3)).then_inc(ysum.sem, 1)

                def front(b, moe):
                    pe.wait_ge(xn0.sem, xn0.at(b, 1))
                    for k in range(KD):
                        transpose_tiles(front_bank(b, ("xT", k)), fa, k).then_inc(f_done.sem, 1)
                    run_until(moe, 0)
                    pe.wait_ge(xT_up.sem, xT_up.at(b, 2))
                    project(b, ("dtr", 0), [dt_inT[:, k, :] for k in range(KD)], x_feat)
                    project(b, ("B", 0), [projT[:, k, CB:CB + DXB] for k in range(KD)], x_feat)
                    for pair in UNIT_AT.values():
                        for kind in pair:
                            unit_product(b, kind, 0)
                        run_until(moe, 4 if pair == UNIT_AT[min(UNIT_AT)] else 5)
                    for s in range(NCT * NT):
                        ct, i = s // NT, s % NT
                        if i == 0:
                            pe.wait_ge(lo_up.sem, lo_up.at(b, 2 * ct + 2))
                        q, k = i // 4, i % 4
                        for v, name in enumerate(("dA", "dtx")):
                            dst = front_bank(b, (name, s))
                            for half in range(2):
                                ins = nc.tensor.matmul(dst[:, :], one_hot[32 * q:32 * q + 32, k, :],
                                                       halves[32 * q:32 * q + 32, ct % 2, v, half, :],
                                                       start=(half == 0), stop=(half == 1))
                            ins.then_inc(f_done.sem, 1)
                        if i in UNIT_AT and ct + 1 < NCT:
                            for kind in UNIT_AT[i]:
                                unit_product(b, kind, ct + 1)
                        for t in SUMS_AT[s]:
                            state_sums(b, t)
                        run_until(moe, 8 + s)
                    for s in SUMS_AT[NCT * NT]:
                        state_sums(b, s)
                    run_until(moe, 8 + NCT * NT)
                    for j in range(NJ):
                        dst = front_bank(b, ("out", j))
                        pe.wait_ge(yz_up.sem, yz_up.at(b, NCT))
                        for ct in range(NCT):
                            ins = nc.tensor.matmul(dst[:, 0:DM], yz[:, ct, j * P:(j + 1) * P], outT[:, ct, :],
                                                   start=(ct == 0), stop=(ct == NCT - 1))
                        ins.then_inc(f_done.sem, 1)
                    run_until(moe, LAST)

                def moe_bank(b, name):
                    n = MOE_AT[name]
                    before = MOE[n - MOE_BANKS]
                    if before[0] == "pad":
                        before = MOE[n - 2 * MOE_BANKS]
                    freed_by, k = moe_reader(before)
                    if freed_by.begun(b, k if n >= MOE_BANKS else k - freed_by.per_batch):
                        pe.wait_ge(freed_by.sem, freed_by.at(b, k if n >= MOE_BANKS else k - freed_by.per_batch))
                    return m_bank[n % MOE_BANKS]

                def moe(b):
                    pe.wait_ge(xm_up.sem, xm_up.at(b, 1))
                    for k in range(KD):
                        transpose_tiles(moe_bank(b, ("mT", k)), ma, k).then_inc(m_done.sem, 1)
                    yield PE_SLOT[0]
                    pe.wait_ge(mT_up.sem, mT_up.at(b, 2))
                    for (kind, i), slot in zip(MOE[2:-2], PE_SLOT):
                        yield slot
                        j, c = i // 4, i % 4
                        w = routeT if kind == "route" else expertT
                        if kind == "route":
                            bias = bias_rows[:, 0, :].rearrange("a (o e) -> a e o", e=NE)[:, 2 * c:2 * c + 2, :]
                        else:
                            bias = bias_rows[:, 1, c * 512:(c + 1) * 512]
                        dst = moe_bank(b, (kind, i))
                        for k in range(KD):
                            nc.tensor.matmul(dst[:, :], mT[:, k, j * P:(j + 1) * P], w[:, k, c * 512:(c + 1) * 512],
                                             start=(k == 0), stop=False)
                        nc.tensor.matmul(dst[:, :].rearrange("p (e o) -> p e o", e=2) if kind == "route" else dst[:, :],
                                         ones_bf[0:3, :], bias, start=False, stop=True,
                                         ).then_inc(m_done.sem, 1)

                prepare()
                pe.wait_ge(bias_in.sem, bias_in.at(0, 1))
                rounds(pe, front, moe, None)

            @block.scalar
            def _(act):
                def prepare():
                    for n in range(0, len(units), 2):
                        act.wait_ge(prep_done.sem, prep_done.at(0, n + 1))
                        dst = units[n][2]
                        nc.scalar.copy(dst, bank[n % 4][:, 0:dst.shape[1] * dst.shape[2]]
                                       .rearrange("p (k c) -> p k c", k=dst.shape[1])).then_inc(prep_act.sem, 1)
                    act.wait_ge(prep_done.sem, prep_done.at(0, len(units) + 1))
                    nc.scalar.activation(A_neg[:, :], y_bank[:, 0:NCT * NT], ACT.Exp).then_inc(prep_act.sem, 1)
                    act.wait_ge(small_in.sem, small_in.at(0, 7))
                    nc.scalar.copy(bias_part[:, 0, :], sp_u[:, 0:32]).then_inc(bias_split.sem, 1)
                    act.wait_ge(prep_dve.sem, prep_dve.at(0, len(units) // 2 + 2))
                    nc.scalar.copy(bias_part[:, 1, :], sp_r[:, 0:32]).then_inc(bias_split.sem, 1)

                def take_dt(b, ct):
                    src = bank[FRONT_AT[("dt", ct)] % FRONT_BANKS][:, :]
                    act.wait_ge(f_done.sem, f_done.at(b, FRONT_AT[("dt", ct)] + 1))
                    if dt_up.begun(b, ct):
                        act.wait_ge(dt_up.sem, dt_up.at(b, ct))
                    if ct == 0 and x1_up.begun(b, 0):
                        act.wait_ge(x1_up.sem, x1_up.at(b, 0))
                    bias = per_ch[:, ct, DTB:DTB + 1]
                    nc.scalar.activation(sp_u, src, ACT.Abs, bias=bias).then_inc(sp_abs.sem, 1)
                    if hi_up.begun(b, 2 * ct - 1):
                        act.wait_ge(hi_up.sem, hi_up.at(b, 2 * ct - 1))
                    if lo_up.begun(b, 2 * ct - 1):
                        act.wait_ge(lo_up.sem, lo_up.at(b, 2 * ct - 1))
                    if dtx_up.begun(b, ct):
                        act.wait_ge(dtx_up.sem, dtx_up.at(b, ct))
                    nc.scalar.activation(sp_r, src, ACT.Relu, bias=bias).then_inc(sp_relu.sem, 1)

                def dt_exp(b, ct):
                    act.wait_ge(sp_abs.sem, sp_abs.at(b, ct + 1))
                    nc.scalar.activation(sp_u, sp_u, ACT.Exp, scale=-1.0).then_inc(sp_exp.sem, 1)

                def dt_log(b, ct):
                    act.wait_ge(sp_exp.sem, sp_exp.at(b, ct + 1))
                    nc.scalar.activation(sp_w[:, :], sp_u, ACT.Ln, bias=1.0).then_inc(sp_ln.sem, 1)

                def take_x(b, ct):
                    act.wait_ge(f_done.sem, f_done.at(b, FRONT_AT[("x", ct)] + 1))
                    if conv_up.begun(b, ct):
                        act.wait_ge(conv_up.sem, conv_up.at(b, ct))
                    nc.scalar.copy(xr[:, KC - 1:], bank[FRONT_AT[("x", ct)] % FRONT_BANKS][:, :]).then_inc(xr_up.sem, 1)

                def silus(b, ct):
                    act.wait_ge(conv_up.sem, conv_up.at(b, ct + 1))
                    nc.scalar.activation(xact[:, ct % 2, :], xact[:, ct % 2, :], ACT.Silu).then_inc(xact_up.sem, 1)
                    act.wait_ge(f_done.sem, f_done.at(b, FRONT_AT[("z", ct)] + 1))
                    if yz_up.begun(b, ct - 1):
                        act.wait_ge(yz_up.sem, yz_up.at(b, ct - 1))
                    nc.scalar.activation(zs[:, ct % 2, :], bank[FRONT_AT[("z", ct)] % FRONT_BANKS][:, :],
                                         ACT.Silu).then_inc(zs_up.sem, 1)

                def high_part(b, ct, v):
                    made = dtx_up if v else dt_up
                    act.wait_ge(made.sem, made.at(b, ct + 1))
                    last = FRONT_AT[("dtx", (ct - 2) % NCT * NT + NT - 1)] + 1 - (len(FRONT) if ct < 2 else 0)
                    if f_done.begun(b, last):
                        act.wait_ge(f_done.sem, f_done.at(b, last))
                    nc.scalar.copy(halves[:, ct % 2, v, 0, :], (dtx[:, :] if v else sp_r)).then_inc(hi_up.sem, 1)

                def front(b, moe):
                    act.wait_ge(x0_in.sem, x0_in.at(b, 1))
                    norm_square(act, b, f_ln, 0, x0, fa)
                    run_until(moe, 0)
                    for k in range(KD):
                        act.wait_ge(f_done.sem, f_done.at(b, FRONT_AT[("xT", k)] + 1))
                        nc.scalar.copy(xT[:, k, :], bank[FRONT_AT[("xT", k)] % FRONT_BANKS][:, :]).then_inc(xT_up.sem, 1)
                    run_until(moe, 3)
                    take_dt(b, 0)
                    take_x(b, 0)
                    dt_exp(b, 0)
                    dt_log(b, 0)
                    high_part(b, 0, 0)
                    silus(b, 0)
                    high_part(b, 0, 1)
                    run_until(moe, 5)
                    for s in range(NCT * NT):
                        ct, i = s // NT, s % NT
                        n = FRONT_AT[("dA", s)]
                        act.wait_ge(f_done.sem, f_done.at(b, n + 1))
                        if h_up.begun(b, s - A_BUFS + 1):
                            act.wait_ge(h_up.sem, h_up.at(b, s - A_BUFS + 1))
                        nc.scalar.activation(dA[:, s % A_BUFS, :], bank[n % FRONT_BANKS][:, :], ACT.Exp,
                                             scale=A_neg[:, s:s + 1]).then_inc(dA_up.sem, 1)
                        if ct + 1 < NCT:
                            if i == 2:
                                take_dt(b, ct + 1)
                                take_x(b, ct + 1)
                                dt_exp(b, ct + 1)
                            if i == 3:
                                dt_log(b, ct + 1)
                            if i == 5:
                                high_part(b, ct + 1, 0)
                            if i == 6:
                                silus(b, ct + 1)
                            if i == 8:
                                high_part(b, ct + 1, 1)
                        run_until(moe, 8 + s)
                    for j in range(NJ):
                        act.wait_ge(f_done.sem, f_done.at(b, FRONT_AT[("out", j)] + 1))
                        nc.scalar.copy(fa[:, j, :], bank[FRONT_AT[("out", j)] % FRONT_BANKS][:, 0:DM]
                                       ).then_inc(fo_up.sem, 1)
                    norm_square(act, b, f_ln, 1, fa, xT[:, :, :].rearrange("p k (j d) -> p (k j) d", d=DM))
                    run_until(moe, LAST)

                def moe(b):
                    if x2_out.begun(b, 0):
                        act.wait_ge(x2_out.sem, x2_out.at(b, 0))
                    norm_square(act, b, m_ln, 0, x1, ma)
                    yield 3
                    for k in range(KD):
                        act.wait_ge(m_done.sem, m_done.at(b, MOE_AT[("mT", k)] + 1))
                        nc.scalar.copy(mT[:, k, :], m_bank[MOE_AT[("mT", k)] % MOE_BANKS][:, :]).then_inc(mT_up.sem, 1)
                    for n, (kind, i) in enumerate(MOE[2:-2]):
                        yield ACT_SLOT[n]
                        j, c = i // 4, i % 4
                        if MOE[2 + n - 4] in [("route", 4 * t + 3) for t in range(NJ)]:
                            t = MOE[2 + n - 4][1] // 4
                            act.wait_ge(gap_up.sem, gap_up.at(b, t + 1))
                            nc.scalar.activation(sel[:, t % 2, 0, :], sel[:, t % 2, 0, :], ACT.Tanh, scale=0.5
                                                 ).then_inc(tanh_up.sem, 1)
                        if kind == "route":
                            act.wait_ge(m_done.sem, m_done.at(b, MOE_AT[(kind, i)] + 1))
                            if c == 0:
                                if c_up.begun(b, j - 1):
                                    act.wait_ge(c_up.sem, c_up.at(b, j - 1))
                            nc.scalar.copy(lg[:, j % 2, 2 * c:2 * c + 2, :],
                                           m_bank[MOE_AT[(kind, i)] % MOE_BANKS][:, :]
                                           .rearrange("p (e o) -> p e o", e=2)).then_inc(lg_up.sem, 1)
                    yield LAST
                    norm_square(act, b, m_ln, 1, ma, lg[:, 0, :, :])

                prepare()
                rounds(act, front, moe, None)

            @block.vector
            def _(dve):
                def prepare():
                    nc.vector.memset(xr[:, 0:KC - 1], 0.0)
                    for n in range(1, len(units), 2):
                        dve.wait_ge(prep_done.sem, prep_done.at(0, n + 1))
                        dst = units[n][2]
                        nc.vector.tensor_copy(dst, bank[n % 4][:, 0:dst.shape[1] * dst.shape[2]]
                                              .rearrange("p (k c) -> p k c", k=dst.shape[1])).then_inc(prep_dve.sem, 1)
                    dve.wait_ge(prep_act.sem, prep_act.at(0, (len(units) + 1) // 2 + 1))
                    nc.vector.tensor_scalar(A_neg[:, :], A_neg[:, :], -1.0, None, ALU.mult).then_inc(prep_dve.sem, 1)
                    dve.wait_ge(small_in.sem, small_in.at(0, 7))
                    dve.wait_ge(bias_split.sem, bias_split.at(0, 1))
                    nc.vector.tensor_tensor(sp_r[:, 0:32], sp_u[:, 0:32], bias_part[:, 0, :], ALU.subtract
                                            ).then_inc(prep_dve.sem, 1)
                    dve.wait_ge(bias_split.sem, bias_split.at(0, 2))
                    nc.vector.tensor_tensor(bias_part[:, 2, :], sp_r[:, 0:32], bias_part[:, 1, :], ALU.subtract
                                            ).then_inc(bias_split.sem, 1)

                def soft_plus(b, ct, own):
                    exact = dtx[:, :]
                    if hi_up.begun(b, 2 * ct):
                        dve.wait_ge(hi_up.sem, hi_up.at(b, 2 * ct))
                    if lo_up.begun(b, 2 * ct):
                        dve.wait_ge(lo_up.sem, lo_up.at(b, 2 * ct))
                    dve.wait_ge(sp_exp.sem, sp_exp.at(b, ct + 1))
                    nc.vector.tensor_scalar(exact, sp_u, 1.0, -1.0, ALU.add, ALU.add).then_inc(own.sem, 1)
                    dve.wait_ge(own.sem, own.next())
                    nc.vector.tensor_tensor(exact, sp_u, exact, ALU.subtract).then_inc(own.sem, 1)
                    dve.wait_ge(own.sem, own.next())
                    dve.wait_ge(sp_ln.sem, sp_ln.at(b, ct + 1))
                    nc.vector.tensor_tensor(exact, exact, sp_w[:, :], ALU.add).then_inc(own.sem, 1)
                    dve.wait_ge(own.sem, own.next())
                    nc.vector.tensor_tensor(sp_r, sp_r, exact, ALU.add).then_inc(dt_up.sem, 1)

                def convolve(b, ct, own):
                    dst = xact[:, ct % 2, :]
                    tap = lambda k: per_ch[:, ct, TAP + k:TAP + k + 1]
                    dve.wait_ge(xr_up.sem, xr_up.at(b, ct + 1))
                    nc.vector.tensor_scalar(dst, xr[:, 0:T], tap(0), per_ch[:, ct, CNB:CNB + 1],
                                            ALU.mult, ALU.add).then_inc(own.sem, 1)
                    dve.wait_ge(own.sem, own.next())
                    for k in range(1, KC):
                        ins = nc.vector.scalar_tensor_tensor(dst, xr[:, k:k + T], tap(k), dst, ALU.mult, ALU.add)
                        if k < KC - 1:
                            ins.then_inc(own.sem, 1)
                            dve.wait_ge(own.sem, own.next())
                    ins.then_inc(conv_up.sem, 1)

                def take_c(b, ct):
                    dve.wait_ge(f_done.sem, f_done.at(b, FRONT_AT[("C", ct)] + 1))
                    if c_out.begun(b, ct):
                        dve.wait_ge(c_out.sem, c_out.at(b, ct))
                    nc.vector.tensor_copy(bc_sb[:, 1, :], bank[FRONT_AT[("C", ct)] % FRONT_BANKS][:, :]
                                          ).then_inc(csb_up.sem, 1)

                def dt_times_x(b, ct):
                    dve.wait_ge(xact_up.sem, xact_up.at(b, ct + 1))
                    dve.wait_ge(dt_up.sem, dt_up.at(b, ct + 1))
                    nc.vector.tensor_tensor(dtx[:, :], sp_r, xact[:, ct % 2, :], ALU.mult).then_inc(dtx_up.sem, 1)

                def input_term(b, s):
                    g, n = s // 8, FRONT_AT[("dtx", s)]
                    dve.wait_ge(f_done.sem, f_done.at(b, n + 1))
                    if s % 8 == 0:
                        dve.wait_ge(b_in[g % B_BUFS].sem, b_in[g % B_BUFS].at(b, g // B_BUFS + 1))
                    if h_up.begun(b, s - U_BUFS + 1):
                        dve.wait_ge(h_up.sem, h_up.at(b, s - U_BUFS + 1))
                    nc.vector.tensor_tensor(u[:, s % U_BUFS, :], bank[n % FRONT_BANKS][:, :], b_rep[:, g % B_BUFS, :],
                                            ALU.mult).then_inc(u_up.sem, 1)

                def scan(b, s):
                    dve.wait_ge(dA_up.sem, dA_up.at(b, s + 1))
                    dve.wait_ge(u_up.sem, u_up.at(b, s + 1))
                    if hc_up.begun(b, s - H_BUFS + 1):
                        dve.wait_ge(hc_up.sem, hc_up.at(b, s - H_BUFS + 1))
                    nc.vector.tensor_tensor_scan(h[:, s % H_BUFS, :], dA[:, s % A_BUFS, :],
                                                 u[:, s % U_BUFS, :], 0.0, ALU.mult, ALU.add).then_inc(h_up.sem, 1)

                def gate(b, ct):
                    dve.wait_ge(ysum.sem, ysum.at(b, (ct + 1) * NT))
                    nc.vector.scalar_tensor_tensor(yz[:, ct, :], xact[:, ct % 2, :], per_ch[:, ct, DSK:DSK + 1],
                                                   y_bank[:, :], ALU.mult, ALU.add).then_inc(y_read.sem, 1)
                    dve.wait_ge(y_read.sem, y_read.at(b, ct + 1))
                    dve.wait_ge(zs_up.sem, zs_up.at(b, ct + 1))
                    nc.vector.tensor_tensor(yz[:, ct, :], yz[:, ct, :], zs[:, ct % 2, :], ALU.mult).then_inc(yz_up.sem, 1)

                def front(b, moe):
                    own = Steps(f_step, b)
                    dve.wait_ge(x0_in.sem, x0_in.at(b, 1))
                    norm_mean(dve, own, f_ln, x0[:, :, :])
                    run_until(moe, 0)
                    norm_var(dve, b, f_ln, 0, 0, EPS)
                    run_until(moe, 1)
                    norm_apply(dve, b, f_ln, 0, fa, x0).then_inc(xn0.sem, 1)
                    run_until(moe, 2)
                    dve.wait_ge(f_done.sem, f_done.at(b, FRONT_AT[("dtr", 0)] + 1))
                    nc.vector.tensor_copy(dtr[:, :], bank[FRONT_AT[("dtr", 0)] % FRONT_BANKS][:, :]).then_inc(dtr_up.sem, 1)
                    dve.wait_ge(f_done.sem, f_done.at(b, FRONT_AT[("B", 0)] + 1))
                    if b_out.begun(b, 0):
                        dve.wait_ge(b_out.sem, b_out.at(b, 0))
                    nc.vector.tensor_copy(bc_sb[:, 0, :], bank[FRONT_AT[("B", 0)] % FRONT_BANKS][:, :]
                                          ).then_inc(bsb_up.sem, 1)
                    soft_plus(b, 0, own)
                    convolve(b, 0, own)
                    take_c(b, 0)
                    dt_times_x(b, 0)
                    input_term(b, 0)
                    for s in range(NCT * NT):
                        ct, i = s // NT, s % NT
                        if s + 1 < NCT * NT:
                            input_term(b, s + 1)
                        scan(b, s)
                        if ct + 1 < NCT:
                            if i == 3:
                                convolve(b, ct + 1, own)
                            if i == 4:
                                soft_plus(b, ct + 1, own)
                            if i == 5:
                                take_c(b, ct + 1)
                            if i == 7:
                                dt_times_x(b, ct + 1)
                        if i == GATE_AT and ct > 0:
                            gate(b, ct - 1)
                        run_until(moe, 8 + s)
                    gate(b, NCT - 1)
                    run_until(moe, 8 + NCT * NT)
                    dve.wait_ge(fo_up.sem, fo_up.at(b, NJ))
                    norm_mean(dve, own, f_ln, fa[:, :, :])
                    run_until(moe, 8 + NCT * NT + 1)
                    norm_var(dve, b, f_ln, 1, 1, EPS)
                    run_until(moe, 8 + NCT * NT + 2)
                    norm_apply(dve, b, f_ln, 1, fa, fa).then_inc(own.sem, 1)
                    dve.wait_ge(own.sem, own.next())
                    run_until(moe, LAST)
                    if moe is not None:
                        dve.wait_ge(x2_up.sem, x2_up.at(b, 0))
                    dve.wait_ge(x0_back.sem, x0_back.at(b, 1))
                    nc.vector.tensor_tensor(x1[:, :, :], x0_again, fa[:, :, :], ALU.add).then_inc(x1_up.sem, 1)
                    own.end()

                def tournament(own, src, slot):
                    tt = nc.vector.tensor_tensor
                    tt(hi_t[:, 0:4, :], src[:, 0:4, :], src[:, 4:8, :], ALU.max)
                    tt(lo_t[:, 0:4, :], src[:, 0:4, :], src[:, 4:8, :], ALU.min).then_inc(own.sem, 1)
                    dve.wait_ge(own.sem, own.next())
                    yield slot + 1
                    for w in (2, 1):
                        tt(lo_t[:, 0:w, :], lo_t[:, 0:w, :], lo_t[:, w:2 * w, :], ALU.max).then_inc(own.sem, 1)
                        dve.wait_ge(own.sem, own.next())
                        tt(lo_t[:, w:2 * w, :], hi_t[:, 0:w, :], hi_t[:, w:2 * w, :], ALU.min).then_inc(own.sem, 1)
                        dve.wait_ge(own.sem, own.next())
                        tt(hi_t[:, 0:w, :], hi_t[:, 0:w, :], hi_t[:, w:2 * w, :], ALU.max).then_inc(own.sem, 1)
                        dve.wait_ge(own.sem, own.next())
                        tt(lo_t[:, 0:w, :], lo_t[:, 0:w, :], lo_t[:, w:2 * w, :], ALU.max).then_inc(own.sem, 1)
                        dve.wait_ge(own.sem, own.next())

                def moe(b):
                    own = Steps(m_step, b)
                    dve.wait_ge(x1_up.sem, x1_up.at(b, 1))
                    norm_mean(dve, own, m_ln, x1[:, :, :])
                    yield 1
                    norm_var(dve, b, m_ln, 0, 0, EPS)
                    yield 2
                    norm_apply(dve, b, m_ln, 0, ma, x1).then_inc(xm_up.sem, 1)

                    def weights(j, slot):
                        dve.wait_ge(lg_up.sem, lg_up.at(b, 4 * j + 4))
                        if d1_up.begun(b, j):
                            dve.wait_ge(d1_up.sem, d1_up.at(b, j))
                        yield from tournament(own, lg[:, j % 2, :, :], slot)
                        nc.vector.tensor_tensor(sel[:, j % 2, 0, :], hi_t[:, 0, :], lo_t[:, 0, :], ALU.subtract
                                                ).then_inc(gap_up.sem, 1)

                    def sums(j, slot):
                        dve.wait_ge(tanh_up.sem, tanh_up.at(b, j + 1))
                        nc.vector.tensor_scalar(sel[:, j % 2, 1, :], sel[:, j % 2, 0, :], -0.5, 0.5, ALU.mult, ALU.add).then_inc(own.sem, 1)
                        dve.wait_ge(own.sem, own.next())
                        dve.wait_ge(d1_up.sem, d1_up.at(b, j + 1))
                        for e in range(NE):
                            if e == NE // 2:
                                yield slot + 1
                            spare = spares[:, e, :]
                            for i, op, dst in ((1, ALU.is_ge, spare), (0, ALU.is_gt, lg[:, j % 2, e, :])):
                                ins = nc.vector.scalar_tensor_tensor(dst, lg[:, j % 2, e, :], 0.0,
                                                                     sel[:, j % 2, i, :], op, ALU.mult,
                                                                     accum_out=gate_c[:, i, e:e + 1])
                        ins.then_inc(own.sem, 1)
                        dve.wait_ge(own.sem, own.next())
                        nc.vector.tensor_tensor(gate_c[:, 0, :], gate_c[:, 0, :], gate_c[:, 1, :], ALU.add
                                                ).then_inc(c_up.sem, 1)

                    def mix(j, c):
                        if c == 0:
                            dve.wait_ge(c_up.sem, c_up.at(b, j + 1))
                        dve.wait_ge(m_done.sem, m_done.at(b, MOE_AT[("expert", 4 * j + c)] + 1))
                        src = m_bank[MOE_AT[("expert", 4 * j + c)] % MOE_BANKS]
                        dst = [ma[:, j, :], acc]
                        for e in range(2):
                            w = gate_c[:, 0, 2 * c + e:2 * c + e + 1]
                            x = src[:, e * DM:(e + 1) * DM]
                            if c == 0:
                                ins = nc.vector.tensor_scalar(dst[e], x, w, None, ALU.mult)
                            else:
                                ins = nc.vector.scalar_tensor_tensor(dst[e], x, w, dst[e], ALU.mult, ALU.add)
                        ins.then_inc(mix_up.sem, 1)
                        dve.wait_ge(mix_up.sem, mix_up.at(b, 4 * j + c + 1))
                        if c == 3:
                            nc.vector.tensor_tensor(ma[:, j, :], ma[:, j, :], acc, ALU.add).then_inc(own.sem, 1)
                            dve.wait_ge(own.sem, own.next())

                    for (kind, i), slot in zip(MOE[2:-2], DVE_SLOT):
                        yield slot
                        j, c = i // 4, i % 4
                        if kind == "route" and c == 3:
                            yield from weights(j, slot)
                        if kind == "expert":
                            if c == 0:
                                yield from sums(j, slot)
                            mix(j, c)
                    yield 8 + NCT * NT + 1
                    norm_mean(dve, own, m_ln, ma[:, :, :])
                    yield 8 + NCT * NT + 2
                    norm_var(dve, b, m_ln, 1, 1, EPS)
                    yield LAST
                    norm_apply(dve, b, m_ln, 1, ma, ma).then_inc(own.sem, 1)
                    dve.wait_ge(own.sem, own.next())
                    nc.vector.tensor_tensor(ma[:, :, :], x1[:, :, :], ma[:, :, :], ALU.add).then_inc(x2_up.sem, 1)
                    own.end()

                prepare()
                rounds(dve, front, moe, None)

            @block.gpsimd
            def _(pool):
                def prepare():
                    def select(ap, pattern, base, mult, op, fill=0.0):
                        return nc.gpsimd.affine_select(out=ap, in_=ap, compare_op=op, fill=fill, base=base,
                                                       pattern=pattern, channel_multiplier=mult)
                    nc.gpsimd.memset(ident[:, :], 1.0)
                    nc.gpsimd.memset(ones_bf[:, :], 1.0)
                    nc.gpsimd.memset(neg_half[:, :], -0.5)
                    one_hot_f32 = u[:, 0, :].rearrange("r (k c) -> r k c", k=4)
                    nc.gpsimd.memset(one_hot_f32, 1.0)
                    nc.gpsimd.memset(state_sum[:, :, :], 1.0).then_inc(consts.sem, 1)
                    pool.wait_ge(consts.sem, consts.at(0, 1))
                    select(ident[:, :], [[-1, P]], 0, 1, ALU.is_equal).then_inc(consts.sem, 1)
                    for part in range(NQ):
                        pool.wait_ge(consts.sem, consts.at(0, 2 + part))
                        select(one_hot_f32[32 * part:32 * part + 32].rearrange("r k (p n) -> r k p n", p=NP),
                               [[-NP, 4], [-1, NP], [0, NS]], 0, 1, ALU.is_equal).then_inc(consts.sem, 1)
                    pool.wait_ge(consts.sem, consts.at(0, 2 + NQ))
                    select(state_sum[:, :, :], [[NP * NS, 4], [-NS, 32]], 0, 1, ALU.is_ge).then_inc(consts.sem, 1)
                    pool.wait_ge(consts.sem, consts.at(0, 3 + NQ))
                    select(state_sum[:, :, :], [[-NP * NS, 4], [NS, 32]], NS - 1, -1, ALU.is_ge).then_inc(consts.sem, 1)
                    pool.wait_ge(consts.sem, consts.at(0, 4 + NQ))
                    nc.gpsimd.tensor_copy(one_hot[:, :, :], one_hot_f32).then_inc(consts.sem, 1)
                    pool.wait_ge(consts.sem, consts.at(0, 5 + NQ))

                def low_half(b, ct, v):
                    pool.wait_ge(hi_up.sem, hi_up.at(b, 2 * ct + v + 1))
                    nc.gpsimd.tensor_tensor(halves[:, ct % 2, v, 1, :], (dtx[:, :] if v else sp_r),
                                            halves[:, ct % 2, v, 0, :], ALU.subtract).then_inc(lo_up.sem, 1)

                def output_term(b, s):
                    hd = s // 2
                    if s % 2 == 0:
                        pool.wait_ge(c_in[hd % C_BUFS].sem, c_in[hd % C_BUFS].at(b, hd // C_BUFS + 1))
                    pool.wait_ge(h_up.sem, h_up.at(b, s + 1))
                    if ysum.begun(b, s - HC_BUFS + 1):
                        pool.wait_ge(ysum.sem, ysum.at(b, s - HC_BUFS + 1))
                    nc.gpsimd.tensor_tensor(hc[:, s % HC_BUFS, :], h[:, s % H_BUFS, :], c_rep[:, hd % C_BUFS, :],
                                            ALU.mult).then_inc(hc_up.sem, 1)

                def front(b, moe):
                    norm_rstd(pool, b, f_ln, 0)
                    run_until(moe, 0)
                    for v in range(2):
                        low_half(b, 0, v)
                    for s in range(NCT * NT):
                        ct, i = s // NT, s % NT
                        output_term(b, s)
                        if ct + 1 < NCT:
                            if i == 7:
                                low_half(b, ct + 1, 0)
                            if i == 9:
                                low_half(b, ct + 1, 1)
                        run_until(moe, 8 + s)
                    norm_rstd(pool, b, f_ln, 1)
                    run_until(moe, LAST)

                def moe(b):
                    norm_rstd(pool, b, m_ln, 0)
                    for (kind, i), slot in zip(MOE[2:-2], POOL_SLOT):
                        yield slot
                        j, c = i // 4, i % 4
                        if kind == "route" and c == 3:
                            pool.wait_ge(gap_up.sem, gap_up.at(b, j + 1))
                            nc.gpsimd.tensor_tensor(lg[:, j % 2, :, :], lg[:, j % 2, :, :],
                                                    lo_t[:, 0:1, :].to_broadcast([P, NE, DM]), ALU.subtract
                                                    ).then_inc(d1_up.sem, 1)
                    yield LAST
                    norm_rstd(pool, b, m_ln, 1)

                prepare()
                rounds(pool, front, moe, None)

        with ExitStack() as ctx:
            def sb(name, shape, dt=F32):
                return ctx.enter_context(nc.sbuf_tensor(name, shape, dt))

            Wv, Wr, Wo, Wcr = (sb(n, [P, KD, DM]) for n in ("Wv", "Wr", "Wo", "Wcr"))
            Wck = sb("Wck", [P, KD, 4 * DM])
            Wcv = sb("Wcv", [P, NI, DM])
            rows = sb("rows", [P, 5, DM])
            cols = sb("cols", [P, KD, 6])
            w12 = sb("w12", [P, 2, NI, DM])
            w3 = sb("w3", [P, KD, HID])
            w1T, w2T = (sb(n, [P, KD, NM * P], F32R) for n in ("w1T", "w2T"))
            w3T = sb("w3T", [P, NM, DM], F32R)
            abs_junk = sb("abs_junk", [P, NI * DM], BF16)
            absum, recip = sb("absum", [P, 4]), sb("recip", [P, 4])
            ones = sb("ones", [P, P])
            decay = sb("decay", [P, KD, T])
            ramp = sb("ramp", [P, 3, T])

            x2 = sb("x2", [P, NJ, DM])
            x3 = sb("x3", [P, NJ, DM])
            ta, tb = sb("ta", [P, NJ, DM]), sb("tb", [P, NJ, DM])
            rt = sb("rt", [P, NJ, DM])
            featT = sb("featT", [P, KD, 1 + T])
            mixT = sb("mixT", [P, KD, T])
            vjunk = sb("vjunk", [P, KD, T], BF16)
            vmix = sb("vmix", [P, KD])
            qh = sb("qh", [P, 1, DM])
            kr = sb("kr", [P, 2, T])
            kcT = sb("kcT", [P, NI, T])
            r_stat = sb("r_stat", [P, 5, NJ])
            r1 = sb("r1", [P, NJ])
            fb = sb("fb", [P, NJ, DM])
            fT = sb("fT", [P, 2, KD, T], F32R)
            th = sb("th", [P, 2, T])
            gated = sb("gated", [P, 2, T])
            hid = sb("hid", [P, 2, NM, T], F32R)
            x4 = sb("x4", [P, NJ, DM])
            g_stat = sb("g_stat", [P, 5, NJ])
            r_junk, g_junk = (sb(n, [P, NJ, DM], BF16) for n in ("r_junk", "g_junk"))
            r_bank, g_bank = bank[0:4], bank[4:8]

            x2_in = sig("x2_in", 1, 16)
            rwkv_in, tern_in = sig("rwkv_in", 0, 16), sig("tern_in", 0, 16)
            r_consts, ramp_up, decay_up, abs_up, tot_up, rec_up = (
                sig(n, 0) for n in ("r_consts", "ramp_up", "decay_up", "abs_up", "tot_up", "rec_up"))
            tern_up, turned, turned_up = (sig(n, 0) for n in ("tern_up", "turned", "turned_up"))
            t_step = sig("t_step", 0)
            r_ln = Norm("r", r_stat, 5, 6)
            r_done = sig("r_done", sum(n[0] != "pad" for n in RWKV))
            ln1_up, tm_up, cm_up = sig("ln1_up"), sig("tm_up"), sig("cm_up")
            tT_up, cT_up = sig("tT_up", KD), sig("cT_up", KD)
            mix_in, vmix_up = sig("mix_in", KD), sig("vmix_up", KD)
            r_up, q_up, xa_up = sig("r_up", 2), sig("q_up"), sig("xa_up")
            relu_up, kc_up = sig("relu_up", NI), sig("kc_up", NI)
            cr_up, att_up, x3_up = sig("cr_up", 2), sig("att_up", 2), sig("x3_up")
            r_step = sig("r_step", R_STEPS)

            g_ln = Norm("g", g_stat, 2, 2)
            g_done = sig("g_done", len(FFN))
            xg_up, fT_up = sig("xg_up"), sig("fT_up", KD)
            fT_hi, gated_up, hid_hi = sig("fT_hi", KD), sig("gated_up", NM), sig("hid_hi", NM)
            th_up, hid_up, w3_up = sig("th_up", NM), sig("hid_up", NM), sig("w3_up", 2)
            x4_up, sent = sig("x4_up"), sig("sent", 1, 16)
            g_step = sig("g_step", 3)

            N_RWKV_IN, N_TERN_IN = 6 + 5 + 6, 3
            r_bank_of = lambda name: r_bank[RWKV_AT[name] % 4]
            g_bank_of = lambda name: g_bank[FFN_AT[name] % 4]
            r_count = lambda name: 1 + sum(n[0] != "pad" for n in RWKV[:RWKV_AT[name]])
            n_ch = [min(P, HID - m * P) for m in range(NM)]

            turns = []
            half = NI // 2
            for v, dst in ((0, w1T), (1, w2T)):
                for k in range(KD):
                    for g in range(2):
                        turns.append(([(t * HR, w12[0:HR, v, g * half + t, k * P:(k + 1) * P]) for t in range(half)],
                                      P, half * HR, dst[:, k, g * half * HR:(g + 1) * half * HR], 1 + v))
            for m in range(NM):
                turns.append(([(t * P, w3[:, t, m * P:m * P + n_ch[m]]) for t in range(KD)],
                              n_ch[m], DM, w3T[0:n_ch[m], m, :], 3))

            block = ctx.enter_context(nc.Block())

            @block.sync
            def _(sp):
                sp.dma_start(x2[:, :, :], x2_dram[0].rearrange("(j p) d -> p j d", p=P)).then_inc(x2_in.sem, 16)
                w = lambda n: a["L1_attn_" + n]
                by_ch = lambda ap: ap.rearrange("(c p) -> p c", p=P)
                load = lambda dst, src, s=rwkv_in, **kw: sp.dma_start(dst, src, **kw).then_inc(s.sem, 16)
                for i, n in ((G1, "ln1_g"), (B1, "ln1_b"), (G2, "ln2_g"), (B2, "ln2_b"), (BO, "bo")):
                    load(rows[:, i, :], w(n).unsqueeze(0).to_broadcast([P, DM]))
                for i, n in ((TG, "tm_g"), (TB, "tm_b"), (CG, "cm_g"), (CBE, "cm_b"), (TF, "time_first"), (TD, "time_decay")):
                    load(cols[:, :, i], by_ch(w(n)), allow_slow_non_contiguous=True)
                for dst, n in ((Wv, "Wv"), (Wr, "Wr"), (Wo, "Wo"), (Wck, "Wck"), (Wcr, "Wcr"), (Wcv, "Wcv")):
                    load(dst[:, :, :], w(n).rearrange("(k p) n -> p k n", p=P))
                for v, n in enumerate(("w1", "w2")):
                    load(w12[0:HR, v, :, :], a["L1_ffn_" + n].rearrange("(t p) d -> p t d", p=HR), tern_in)
                load(w3[:, :, :], a["L1_ffn_w3"].rearrange("(t p) d -> p t d", p=P), tern_in)

                def send(b):
                    sp.wait_ge(x4_up.sem, x4_up.at(b, 1))
                    sp.dma_start(at_b(out, b).rearrange("b (j p) d -> p (b j) d", p=P), x4[:, :, :]
                                 ).then_inc(sent.sem, 16)
                def load_x2(b):
                    if x3_up.begun(b, 0):
                        sp.wait_ge(x3_up.sem, x3_up.at(b, 0))
                    sp.dma_start(x2[:, :, :], at_b(x2_dram, b).rearrange("b (j p) d -> p (b j) d", p=P)
                                 ).then_inc(x2_in.sem, 16)

                with sp.Fori(1, NB) as b:
                    load_x2(b)
                    send(b - 1)
                send(NB - 1)
                sp.wait_ge(sent.sem, sent.at(0, NB))

            @block.tensor
            def _(pe):
                def group(dst, pairs):
                    for k, (l, r) in enumerate(pairs):
                        ins = nc.tensor.matmul(dst, l, r, start=(k == 0), stop=(k == len(pairs) - 1))
                    return ins

                def prepare():
                    yield 3
                    pe.wait_ge(abs_up.sem, abs_up.at(0, 3))
                    pe.wait_ge(r_consts.sem, r_consts.at(0, 1))
                    nc.tensor.matmul(g_bank[3][:, 0:4], ones[:, :], absum[:, :], start=True, stop=True
                                     ).then_inc(turned.sem, 1)
                    yield 8
                    for n, (srcs, m, _, _, v) in enumerate(turns):
                        pe.wait_ge(tern_up.sem, tern_up.at(0, v))
                        if n >= 4:
                            pe.wait_ge(turned_up.sem, turned_up.at(0, n - 3))
                        if n == 3:
                            pe.wait_ge(tot_up.sem, tot_up.at(0, 1))
                        for col, src in srcs:
                            w = src.shape[0]
                            ins = nc.tensor.transpose(g_bank[n % 4][0:m, col:col + w], src, ident[0:w, 0:w])
                        ins.then_inc(turned.sem, 1)
                        yield 20 + 4 * n
                    pe.wait_ge(turned_up.sem, turned_up.at(0, len(turns)))

                def mix(b, ffn):
                    at = lambda t: run_until(ffn, t)

                    def free(name):
                        n = RWKV_AT[name]
                        m = n - 4
                        while RWKV[m][0] == "pad":
                            m -= 4
                        kind, i = RWKV[m]
                        s, k = {"tT": (tT_up, i + 1), "v": (vmix_up, i + 1), "r": (r_up, i + 1), "q": (q_up, 1),
                                "cT": (cT_up, i + 1), "ck": (relu_up, i + 1), "cr": (cr_up, i + 1),
                                "cv": (att_up, i + 1)}[kind]
                        if s.begun(b, k if m >= 0 else k - s.per_batch):
                            pe.wait_ge(s.sem, s.at(b, k if m >= 0 else k - s.per_batch))
                        return r_bank_of(name)

                    def turn(kind, src):
                        for k in range(KD):
                            transpose_tiles(free((kind, k)), src, k).then_inc(r_done.sem, 1)

                    now = lambda j: featT[:, :, 1 + j * P:1 + (j + 1) * P]
                    at(40)
                    pe.wait_ge(tm_up.sem, tm_up.at(b, 1))
                    turn("tT", tb)
                    at(50)
                    pe.wait_ge(tT_up.sem, tT_up.at(b, KD))
                    for m in range(KD):
                        group(free(("v", m))[:, :], [(Wv[:, k, m * P:(m + 1) * P], featT[:, k, 1:1 + T]) for k in range(KD)]
                              ).then_inc(r_done.sem, 1)
                    at(54)
                    pe.wait_ge(mix_in.sem, mix_in.at(b, KD))
                    for i in range(2):
                        dst = free(("r", i))
                        for j in range(2):
                            t = (2 * i + j) * P
                            ins = group(dst[:, j * DM:(j + 1) * DM], [(mixT[:, k, t:t + P], Wr[:, k, :]) for k in range(KD)])
                        ins.then_inc(r_done.sem, 1)
                    at(58)
                    pe.wait_ge(vmix_up.sem, vmix_up.at(b, KD))
                    group(free(("q", 0))[:, 0:DM], [(vmix[:, k:k + 1].to_broadcast([P, P]), Wo[:, k, :]) for k in range(KD)]
                          ).then_inc(r_done.sem, 1)
                    at(90)
                    pe.wait_ge(cm_up.sem, cm_up.at(b, 1))
                    turn("cT", tb)
                    for m in range(NI):
                        at(100 + 2 * m)
                        pe.wait_ge(cT_up.sem, cT_up.at(b, KD))
                        group(free(("ck", m))[:, :], [(Wck[:, k, m * P:(m + 1) * P], featT[:, k, 0:T]) for k in range(KD)]
                              ).then_inc(r_done.sem, 1)
                    at(116)
                    for i in range(2):
                        dst = free(("cr", i))
                        for j in range(2):
                            t = 1 + (2 * i + j) * P
                            ins = group(dst[:, j * DM:(j + 1) * DM], [(featT[:, k, t:t + P], Wcr[:, k, :]) for k in range(KD)])
                        ins.then_inc(r_done.sem, 1)
                    at(120)
                    pe.wait_ge(kc_up.sem, kc_up.at(b, NI))
                    for i in range(2):
                        dst = free(("cv", i))
                        for j in range(2):
                            t = (2 * i + j) * P
                            ins = group(dst[:, j * DM:(j + 1) * DM], [(kcT[:, m, t:t + P], Wcv[:, m, :]) for m in range(NI)])
                        ins.then_inc(r_done.sem, 1)
                    at(LAST)

                def ffn(b):
                    def free(name):
                        n = FFN_AT[name]
                        kind, i = FFN[n - 4]
                        s, k = {"fT": (fT_up, i + 1), "w1": (th_up, i + 1), "w2": (gated_up, i + 1),
                                "w3": (w3_up, i + 1)}[kind]
                        if s.begun(b, k if n >= 4 else k - s.per_batch):
                            pe.wait_ge(s.sem, s.at(b, k if n >= 4 else k - s.per_batch))
                        return g_bank_of(name)

                    yield 25
                    pe.wait_ge(xg_up.sem, xg_up.at(b, 1))
                    for k in range(KD):
                        transpose_tiles(free(("fT", k)), fb, k).then_inc(g_done.sem, 1)
                    for m in range(NM):
                        yield 31 + 8 * m
                        pe.wait_ge(fT_up.sem, fT_up.at(b, KD))
                        for kind, w in (("w1", w1T), ("w2", w2T)):
                            group(free((kind, m))[:, :], [(w[:, k, m * P:(m + 1) * P], fT[:, half, k, :])
                                                          for k in range(KD) for half in range(2)]
                                  ).then_inc(g_done.sem, 1)
                    yield 81
                    pe.wait_ge(hid_up.sem, hid_up.at(b, NM))
                    for i in range(2):
                        dst = free(("w3", i))
                        for j in range(2):
                            t = (2 * i + j) * P
                            ins = group(dst[:, j * DM:(j + 1) * DM],
                                        [(hid[0:n_ch[m], half, m, t:t + P], w3T[0:n_ch[m], m, :])
                                         for m in range(NM) for half in range(2)])
                        ins.then_inc(g_done.sem, 1)

                pe.wait_ge(rwkv_in.sem, rwkv_in.at(0, N_RWKV_IN))
                rounds(pe, mix, ffn, prepare)

            @block.scalar
            def _(act):
                def prepare():
                    yield 1
                    act.wait_ge(tern_in.sem, tern_in.at(0, N_TERN_IN))
                    act.wait_ge(r_consts.sem, r_consts.at(0, 1))
                    for v in range(2):
                        nc.scalar.activation(abs_junk[0:HR, :],
                                             w12[0:HR, v, :, :].rearrange("p a d -> p (a d)"), ACT.Abs,
                                             accum_out=absum[0:HR, v:v + 1]).then_inc(abs_up.sem, 1)
                        act.wait_ge(abs_up.sem, abs_up.at(0, v + 1))
                    nc.scalar.activation(abs_junk[:, 0:KD * HID],
                                         w3[:, :, :].rearrange("p a d -> p (a d)"), ACT.Abs,
                                         accum_out=absum[:, 2:3]).then_inc(abs_up.sem, 1)
                    for n, (srcs, m, width, dst, _) in enumerate(turns):
                        yield 22 + 4 * n
                        act.wait_ge(turned.sem, turned.at(0, n + 2))
                        nc.scalar.copy(dst, g_bank[n % 4][0:m, 0:width]).then_inc(turned_up.sem, 1)

                def take(b, kind, s, gi, bi):
                    for k in range(KD):
                        act.wait_ge(r_done.sem, r_done.at(b, r_count((kind, k))))
                        nc.scalar.activation(featT[:, k, 1:1 + T], r_bank_of((kind, k))[:, :], ACT.Identity,
                                             bias=cols[:, k, bi:bi + 1], scale=cols[:, k, gi:gi + 1]).then_inc(s.sem, 1)

                def mix(b, ffn):
                    at = lambda t: run_until(ffn, t)
                    at(12)
                    norm_square(act, b, r_ln, 0, x2[:, :, :], r_junk)
                    at(32)
                    norm_square(act, b, r_ln, 1, tb, r_junk)
                    at(42)
                    if r_done.begun(b, r_count(("cr", 1)) - r_done.per_batch):
                        act.wait_ge(r_done.sem, r_done.at(b, r_count(("cr", 1)) - r_done.per_batch))
                    take(b, "tT", tT_up, TG, TB)
                    at(56)
                    if att_up.begun(b, 0):
                        act.wait_ge(att_up.sem, att_up.at(b, 0))
                    for i in range(2):
                        act.wait_ge(r_done.sem, r_done.at(b, r_count(("r", i))))
                        nc.scalar.activation(rt[:, 2 * i:2 * i + 2, :].rearrange("p j d -> p (j d)"),
                                             r_bank_of(("r", i))[:, :], ACT.Tanh, scale=0.5).then_inc(r_up.sem, 1)
                    at(72)
                    norm_square(act, b, r_ln, 2, ta, r_junk)
                    at(82)
                    norm_square(act, b, r_ln, 3, tb, r_junk)
                    at(92)
                    act.wait_ge(mix_in.sem, mix_in.at(b, KD))
                    take(b, "cT", cT_up, CG, CBE)
                    for m in range(NI):
                        at(101 + 2 * m)
                        act.wait_ge(r_done.sem, r_done.at(b, r_count(("ck", m))))
                        if kc_up.begun(b, m - 1):
                            act.wait_ge(kc_up.sem, kc_up.at(b, m - 1))
                        nc.scalar.activation(kr[:, m % 2, :], r_bank_of(("ck", m))[:, :], ACT.Relu).then_inc(relu_up.sem, 1)
                    at(117)
                    act.wait_ge(xa_up.sem, xa_up.at(b, 1))
                    for i in range(2):
                        act.wait_ge(r_done.sem, r_done.at(b, r_count(("cr", i))))
                        nc.scalar.activation(rt[:, 2 * i:2 * i + 2, :].rearrange("p j d -> p (j d)"),
                                             r_bank_of(("cr", i))[:, :], ACT.Tanh, scale=0.5).then_inc(cr_up.sem, 1)
                    at(132)
                    norm_square(act, b, r_ln, 4, ta, r_junk)
                    at(LAST)

                def ffn(b):
                    yield 13
                    norm_square(act, b, g_ln, 0, x3[:, :, :], g_junk)
                    yield 27
                    for k in range(KD):
                        act.wait_ge(g_done.sem, g_done.at(b, FFN_AT[("fT", k)] + 1))
                        nc.scalar.copy(fT[:, 0, k, :], g_bank_of(("fT", k))[:, :]).then_inc(fT_hi.sem, 1)
                    for m in range(NM):
                        yield 33 + 8 * m
                        act.wait_ge(g_done.sem, g_done.at(b, FFN_AT[("w1", m)] + 1))
                        if gated_up.begun(b, m - 1):
                            act.wait_ge(gated_up.sem, gated_up.at(b, m - 1))
                        nc.scalar.activation(th[:, m % 2, :], g_bank_of(("w1", m))[:, :], ACT.Tanh, scale=0.5
                                             ).then_inc(th_up.sem, 1)
                        yield 37 + 8 * m
                        act.wait_ge(gated_up.sem, gated_up.at(b, m + 1))
                        nc.scalar.copy(hid[:, 0, m, :], gated[:, m % 2, :]).then_inc(hid_hi.sem, 1)
                    yield 83
                    for i in range(2):
                        act.wait_ge(g_done.sem, g_done.at(b, FFN_AT[("w3", i)] + 1))
                        nc.scalar.activation(fb[:, 2 * i:2 * i + 2, :].rearrange("p j d -> p (j d)"),
                                             g_bank_of(("w3", i))[:, :], ACT.Copy, scale=0.5).then_inc(w3_up.sem, 1)
                    yield 87
                    norm_square(act, b, g_ln, 1, fb, g_junk)

                act.wait_ge(ramp_up.sem, ramp_up.at(0, 1))
                act.wait_ge(rwkv_in.sem, rwkv_in.at(0, N_RWKV_IN))
                for k in range(KD):
                    nc.scalar.activation(decay[:, k, :], ramp[:, 2, :], ACT.Exp, scale=cols[:, k, TD:TD + 1]
                                         ).then_inc(decay_up.sem, 1)
                rounds(act, mix, ffn, prepare)

            @block.vector
            def _(dve):
                stt, tt, ts = nc.vector.scalar_tensor_tensor, nc.vector.tensor_tensor, nc.vector.tensor_scalar

                def prepare():
                    yield 5
                    dve.wait_ge(turned.sem, turned.at(0, 1))
                    ts(recip[:, :], g_bank[3][:, 0:4], 1.0 / (HID * DM), EPS3, ALU.mult, ALU.add).then_inc(tot_up.sem, 1)
                    dve.wait_ge(tot_up.sem, tot_up.at(0, 1))
                    nc.vector.reciprocal(recip[:, :], recip[:, :]).then_inc(rec_up.sem, 1)
                    dve.wait_ge(rec_up.sem, rec_up.at(0, 1))
                    n = 0
                    for v, w in enumerate((w12[0:HR, 0, :, :], w12[0:HR, 1, :, :], w3[:, :, :])):
                        scale = recip[0:w.shape[0], v:v + 1]
                        for in1, in2, op1, op2 in ((scale, MAGIC, ALU.mult, ALU.add), (MAGIC, 1.0, ALU.subtract, ALU.min)):
                            ts(w, w, in1, in2, op1, op2).then_inc(t_step.sem, 1)
                            n += 1
                            dve.wait_ge(t_step.sem, t_step.at(0, n))
                        ts(w, w, -1.0, None, ALU.max).then_inc(tern_up.sem, 1)
                        yield 7

                def mix(b, ffn):
                    at = lambda t: run_until(ffn, t)
                    own = Steps(r_step, b)

                    def affine(dst, src, k_pow, g, beta):
                        dve.wait_ge(r_ln.rstd.sem, r_ln.rstd.at(b, k_pow + 1))
                        for j in range(NJ):
                            ins = stt(dst[:, j, :], src[:, j, :], r_ln.neg[:, j:j + 1], rows[:, g, :], ALU.add, ALU.mult)
                        ins.then_inc(own.sem, 1)
                        dve.wait_ge(own.sem, own.next())
                        for j in range(NJ):
                            ins = stt(dst[:, j, :], dst[:, j, :], r_ln.r[:, j:j + 1], rows[:, beta, :], ALU.mult, ALU.add)
                        ins.then_inc(own.sem, 1)
                        dve.wait_ge(own.sem, own.next())

                    at(10)
                    dve.wait_ge(x2_in.sem, x2_in.at(b, 1))
                    norm_mean(dve, own, r_ln, x2[:, :, :])
                    at(14)
                    norm_var(dve, b, r_ln, 0, 0, EPS)
                    at(18)
                    norm_apply(dve, b, r_ln, 0, ta, x2[:, :, :]).then_inc(own.sem, 1)
                    dve.wait_ge(own.sem, own.next())
                    tt(r_ln.v, r_ln.ss, r_ln.r, ALU.mult).then_inc(own.sem, 1)
                    dve.wait_ge(own.sem, own.next())
                    tt(r_ln.v, r_ln.v, r_ln.r, ALU.mult).then_inc(own.sem, 1)
                    dve.wait_ge(own.sem, own.next())
                    ts(r_ln.v, r_ln.v, 1.0 / DM, EPS2, ALU.mult, ALU.add).then_inc(r_ln.var.sem, 1)
                    at(22)
                    dve.wait_ge(r_ln.rstd.sem, r_ln.rstd.at(b, 2))
                    for j in range(NJ):
                        ins = stt(tb[:, j, :], ta[:, j, :], r_ln.r[:, j:j + 1], rows[:, G1, :], ALU.mult, ALU.mult)
                    ins.then_inc(own.sem, 1)
                    dve.wait_ge(own.sem, own.next())
                    tt(tb[:, :, :], tb[:, :, :], rows[:, B1:B1 + 1, :].to_broadcast([P, NJ, DM]), ALU.add).then_inc(own.sem, 1)
                    dve.wait_ge(own.sem, own.next())
                    at(30)
                    norm_mean(dve, own, r_ln, tb[:, :, :])
                    at(34)
                    norm_var(dve, b, r_ln, 1, 2, EPS2)
                    at(38)
                    norm_apply(dve, b, r_ln, 2, tb, tb).then_inc(tm_up.sem, 1)
                    at(51)
                    for k in range(KD):
                        dve.wait_ge(tT_up.sem, tT_up.at(b, k + 1))
                        tt(mixT[:, k, :], featT[:, k, 1:1 + T], featT[:, k, 0:T], ALU.subtract).then_inc(own.sem, 1)
                        dve.wait_ge(own.sem, own.next())
                        stt(mixT[:, k, :], mixT[:, k, :], cols[:, k, TF:TF + 1], featT[:, k, 0:T], ALU.mult, ALU.add
                            ).then_inc(mix_in.sem, 1)
                    at(52)
                    for m in range(KD):
                        dve.wait_ge(r_done.sem, r_done.at(b, r_count(("v", m))))
                        stt(vjunk[:, m, :], r_bank_of(("v", m))[:, :], 1.0, decay[:, m, :], ALU.mult, ALU.mult,
                            accum_out=vmix[:, m:m + 1]).then_inc(vmix_up.sem, 1)
                    at(60)
                    dve.wait_ge(r_done.sem, r_done.at(b, r_count(("q", 0))))
                    tt(qh[:, 0, :], r_bank_of(("q", 0))[:, 0:DM], rows[:, BO, :], ALU.add).then_inc(q_up.sem, 1)
                    dve.wait_ge(q_up.sem, q_up.at(b, 1))
                    ts(qh[:, 0, :], qh[:, 0, :], 0.5, None, ALU.mult).then_inc(own.sem, 1)
                    dve.wait_ge(own.sem, own.next())
                    dve.wait_ge(r_up.sem, r_up.at(b, 2))
                    stt(rt[:, :, :], rt[:, :, :], 1.0, qh[:, :, :].to_broadcast([P, NJ, DM]), ALU.add, ALU.mult).then_inc(own.sem, 1)
                    dve.wait_ge(own.sem, own.next())
                    tt(ta[:, :, :], ta[:, :, :], rt[:, :, :], ALU.add).then_inc(xa_up.sem, 1)
                    dve.wait_ge(xa_up.sem, xa_up.at(b, 1))
                    at(70)
                    norm_mean(dve, own, r_ln, ta[:, :, :])
                    at(74)
                    norm_var(dve, b, r_ln, 2, 3, EPS2)
                    at(78)
                    affine(tb, ta, 3, G2, B2)
                    at(80)
                    norm_mean(dve, own, r_ln, tb[:, :, :])
                    at(84)
                    norm_var(dve, b, r_ln, 3, 4, EPS2)
                    at(88)
                    norm_apply(dve, b, r_ln, 4, tb, tb).then_inc(cm_up.sem, 1)
                    at(122)
                    dve.wait_ge(cr_up.sem, cr_up.at(b, 2))
                    for i in range(2):
                        part = lambda ap: ap[:, 2 * i:2 * i + 2, :].rearrange("p j d -> p (j d)")
                        dve.wait_ge(r_done.sem, r_done.at(b, r_count(("cv", i))))
                        stt(part(rt), part(rt), 1.0, r_bank_of(("cv", i))[:, :], ALU.add, ALU.mult).then_inc(att_up.sem, 1)
                        dve.wait_ge(att_up.sem, att_up.at(b, i + 1))
                        stt(part(ta), part(rt), 0.5, part(ta), ALU.mult, ALU.add).then_inc(own.sem, 1)
                        dve.wait_ge(own.sem, own.next())
                    at(130)
                    norm_mean(dve, own, r_ln, ta[:, :, :])
                    at(134)
                    norm_var(dve, b, r_ln, 4, 5, EPS)
                    at(138)
                    norm_apply(dve, b, r_ln, 5, ta, ta).then_inc(own.sem, 1)
                    dve.wait_ge(own.sem, own.next())
                    if x4_up.begun(b, 0):
                        dve.wait_ge(x4_up.sem, x4_up.at(b, 0))
                    tt(x3[:, :, :], x2[:, :, :], ta[:, :, :], ALU.add).then_inc(x3_up.sem, 1)
                    at(LAST)
                    own.end()

                def ffn(b):
                    own = Steps(g_step, b)
                    yield 11
                    dve.wait_ge(x3_up.sem, x3_up.at(b, 1))
                    norm_mean(dve, own, g_ln, x3[:, :, :])
                    yield 15
                    norm_var(dve, b, g_ln, 0, 0, EPS)
                    yield 19
                    norm_apply(dve, b, g_ln, 0, fb, x3[:, :, :]).then_inc(xg_up.sem, 1)
                    yield 28
                    for k in range(KD):
                        dve.wait_ge(fT_hi.sem, fT_hi.at(b, k + 1))
                        tt(fT[:, 1, k, :], g_bank_of(("fT", k))[:, :], fT[:, 0, k, :], ALU.subtract).then_inc(fT_up.sem, 1)
                    for m in range(NM):
                        yield 35 + 8 * m
                        dve.wait_ge(g_done.sem, g_done.at(b, FFN_AT[("w2", m)] + 1))
                        dve.wait_ge(th_up.sem, th_up.at(b, m + 1))
                        if hid_up.begun(b, m - 1):
                            dve.wait_ge(hid_up.sem, hid_up.at(b, m - 1))
                        stt(gated[:, m % 2, :], th[:, m % 2, :], 1.0, g_bank_of(("w2", m))[:, :], ALU.add, ALU.mult
                            ).then_inc(gated_up.sem, 1)
                    yield 85
                    dve.wait_ge(w3_up.sem, w3_up.at(b, 2))
                    norm_mean(dve, own, g_ln, fb[:, :, :])
                    yield 89
                    norm_var(dve, b, g_ln, 1, 1, EPS)
                    yield 93
                    norm_apply(dve, b, g_ln, 1, fb, fb).then_inc(own.sem, 1)
                    dve.wait_ge(own.sem, own.next())
                    if sent.begun(b, 0):
                        dve.wait_ge(sent.sem, sent.at(b, 0))
                    tt(x4[:, :, :], x3[:, :, :], fb[:, :, :], ALU.add).then_inc(x4_up.sem, 1)
                    own.end()

                nc.vector.memset(featT[:, :, 0:1], 0.0)
                nc.vector.memset(w1T[:, :, HID:].bitcast(F32), 0.0)
                nc.vector.memset(w2T[:, :, HID:].bitcast(F32), 0.0)
                dve.wait_ge(r_consts.sem, r_consts.at(0, 1))
                nc.vector.tensor_tensor_scan(ramp[:, 2, :], ramp[:, 0, :], ramp[:, 1, :], float(T), ALU.mult, ALU.add
                                             ).then_inc(ramp_up.sem, 1)
                dve.wait_ge(rwkv_in.sem, rwkv_in.at(0, N_RWKV_IN))
                dve.wait_ge(decay_up.sem, decay_up.at(0, KD))
                rounds(dve, mix, ffn, prepare)

            @block.gpsimd
            def _(pool):
                def mix(b, ffn):
                    at = lambda t: run_until(ffn, t)
                    for k, t in enumerate((16, 20, 36, 76, 86)):
                        at(t)
                        norm_rstd(pool, b, r_ln, k)
                    for m in range(NI):
                        at(101 + 2 * m)
                        pool.wait_ge(relu_up.sem, relu_up.at(b, m + 1))
                        if m == 0:
                            if r_done.begun(b, 0):
                                pool.wait_ge(r_done.sem, r_done.at(b, 0))
                        nc.gpsimd.tensor_tensor(kcT[:, m, :], kr[:, m % 2, :], kr[:, m % 2, :], ALU.mult
                                                ).then_inc(kc_up.sem, 1)
                    at(136)
                    norm_rstd(pool, b, r_ln, 5)
                    at(LAST)

                def ffn(b):
                    yield 17
                    norm_rstd(pool, b, g_ln, 0)
                    for m in range(NM):
                        yield 38 + 8 * m
                        pool.wait_ge(hid_hi.sem, hid_hi.at(b, m + 1))
                        nc.gpsimd.tensor_tensor(hid[:, 1, m, :], gated[:, m % 2, :], hid[:, 0, m, :], ALU.subtract
                                                ).then_inc(hid_up.sem, 1)
                    yield 91
                    norm_rstd(pool, b, g_ln, 1)

                nc.gpsimd.memset(absum[:, :], 0.0)
                nc.gpsimd.memset(ones[:, :], 1.0)
                nc.gpsimd.memset(ramp[:, 0, :], 1.0)
                nc.gpsimd.memset(ramp[:, 1, :], -1.0).then_inc(r_consts.sem, 1)
                rounds(pool, mix, ffn, None)



_INS = ["x", "L0_attn_in_proj_w", "L0_attn_dt_in_proj_w", "L0_attn_dt_proj_w", "L0_attn_dt_proj_b",
        "L0_attn_conv_w", "L0_attn_conv_b", "L0_attn_A_log", "L0_attn_D", "L0_attn_out_proj_w",
        "L0_ffn_router_w", "L0_ffn_router_b", "L0_ffn_expert_w", "L0_ffn_expert_b",
        "L1_attn_ln1_g", "L1_attn_ln1_b", "L1_attn_ln2_g", "L1_attn_ln2_b", "L1_attn_tm_g", "L1_attn_tm_b",
        "L1_attn_time_decay", "L1_attn_time_first", "L1_attn_Wv", "L1_attn_Wr", "L1_attn_Wo",
        "L1_attn_bo", "L1_attn_cm_g", "L1_attn_cm_b", "L1_attn_Wck", "L1_attn_Wcv", "L1_attn_Wcr",
        "L1_ffn_w1", "L1_ffn_w2", "L1_ffn_w3"]


def kernel(**inputs):
    import numpy as _np
    import concourse.bacc as _bacc
    from concourse import mybir as _mybir
    from concourse.bass_utils import run_bass_kernel_spmd as _run

    nc = _bacc.Bacc("TRN2", target_bir_lowering=False, num_devices=1)
    arrays, a = {}, {}
    for name in _INS:
        arr = _np.ascontiguousarray(inputs["L0_attn_hidden_states" if name == "x" else name])
        arrays[f"in_{name}_dram"] = arr
        a[name] = nc.dram_tensor(f"in_{name}_dram", arr.shape, _mybir.dt.from_np(arr.dtype), kind="ExternalInput").ap()
    out = nc.dram_tensor("out_0_dram", (NB, T, DM), _mybir.dt.float32, kind="ExternalOutput").ap()
    hybrid_layers_kernel(nc, a, out)
    r = _run(nc, [arrays], core_ids=[0])
    return r.results[0]["out_0_dram"]
```

```python
from contextlib import ExitStack

import concourse.bass as bass
from concourse import mybir

F32 = mybir.dt.float32
BF16 = mybir.dt.bfloat16
F32R = mybir.dt.float32r
ACT = mybir.ActivationFunctionType
ALU = mybir.AluOpType
AX = mybir.AxisListType.X

P = 128
NB, T, DM = 4, 512, 256
NJ = T // P
KD = DM // P
DI, DXB, NS, DTR, KC = 512, 128, 16, 128, 4
NCT = DI // P
NP = P // NS
NT = P // NP
NQ = 4
REP = 4
NH = DI // NS
NG = DXB // NS
NE = 8
HID = 704
HR = HID // 8
NM = -(-HID // P)
NI = 4 * DM // P
EPS, EPS2, EPS3 = 1e-5, 1e-12, 1e-8
MAGIC = 1.5 * 2.0 ** 23

CZ, CX, CC, CB = 0, DI, 2 * DI, 3 * DI
CW = 3 * DI + DXB

X0_AT = {"mean": 5, "square": 6, "var": 7, "rstd": 8, "apply": 9}
STAGES = 4
A_BUFS, U_BUFS, H_BUFS, HC_BUFS, C_BUFS, B_BUFS = 3, 2, 3, 7, 4, 2
Y_LAG, Y_HOLD = 4, 1
GATE_AT = 2

DTB, CNB, DSK, TAP = 0, 1, 2, 3
G1, B1, G2, B2, BO = range(5)
TG, TB, CG, CBE, TF, TD = range(6)
T_STEPS, C_STEPS = 11, 8

FRONT_BANKS, MOE_BANKS = 4, 3
UNIT_AT = {1: ("dt", "x"), 5: ("C", "z")}


def front_order():
    names = [("xT", 0), ("xT", 1), ("dtr", 0), ("B", 0)]
    names += [(kind, 0) for pair in UNIT_AT.values() for kind in pair]
    for ct in range(NCT):
        for i in range(NT):
            names += [("dA", ct * NT + i), ("dtx", ct * NT + i)]
            if i in UNIT_AT and ct + 1 < NCT:
                names += [(kind, ct + 1) for kind in UNIT_AT[i]]
    names += [("out", j) for j in range(NJ)]
    assert len(names) % FRONT_BANKS == 0
    return names


def moe_order():
    names = [("mT", 0), ("mT", 1)]
    for j in range(NJ + 1):
        if j < NJ:
            names += [("route", 4 * j + c) for c in range(4)]
        if j > 0:
            names += [("expert", 4 * (j - 1) + c) for c in range(4)]
    names += [("pad", 0), ("pad", 1)]
    assert len(names) % MOE_BANKS == 0
    return names


LATE_PE = [12 + 3 * n for n in range(2 * NE)]
LATE_ACT = [14 + 3 * n for n in range(2 * NE)]
LATE_LOADS = [[n for n in range(2 * NE) if max(0, (3 * n - 10) // 2) == i] for i in range(NH)]
MOE_EARLY = 6
PE_SLOT = [4, 4] + [5] * (MOE_EARLY - 2) + [8 + 24 * n // 10 for n in range(8 * NJ - MOE_EARLY)]
ACT_SLOT = [5] * MOE_EARLY + [t + 1 for t in PE_SLOT[MOE_EARLY:]]
DVE_SLOT = [8] * 4 + [11] * (MOE_EARLY - 4) + [t + 4 for t in PE_SLOT[MOE_EARLY:]]
POOL_SLOT = [11] * MOE_EARLY + [t + 6 for t in PE_SLOT[MOE_EARLY:]]


def sums_order():
    order, t = [[] for _ in range(NCT * NT + 1)], 0
    for s in range(NCT * NT):
        hold = t > 0 and t % NT == 0 and s < t + Y_LAG + Y_HOLD
        for _ in range(2):
            if not hold and t <= s - Y_LAG:
                if t % NT == 0 and order[s]:
                    break
                order[s].append(t)
                t += 1
    order[-1] = list(range(t, NCT * NT))
    return order


SUMS_AT = sums_order()


TIME_BANKS, CHAN_BANKS, FFN_BANKS = 2, 3, 3


def ring(names, banks):
    return names + [("pad", i) for i in range(-len(names) % banks)]


FRONT, MOE = front_order(), moe_order()
TIME = ring([("tT", 0), ("tT", 1), ("v", 0), ("v", 1), ("r", 0), ("r", 1), ("q", 0)], TIME_BANKS)
CHAN = ring([("cT", 0), ("cT", 1)] + [("ck", m) for m in range(NI)]
            + [("cr", 0), ("cr", 1), ("cv", 0), ("cv", 1)], CHAN_BANKS)
FFN = ring([("fT", 0), ("fT", 1)] + [(w, m) for m in range(NM) for w in ("w1", "w2")]
           + [("w3", 0), ("w3", 1)], FFN_BANKS)
FRONT_AT, MOE_AT, TIME_AT, CHAN_AT, FFN_AT = ({name: n for n, name in enumerate(o)}
                                              for o in (FRONT, MOE, TIME, CHAN, FFN))
LAST = 1 << 20


def products(order):
    return sum(kind != "pad" for kind, _ in order)


class Signal:

    def __init__(self, sem, per_batch, unit=1, ahead=0):
        self.sem, self.per_batch, self.unit, self.ahead = sem, per_batch, unit, ahead

    def at(self, b, k):
        if isinstance(b, int):
            return (b * self.per_batch + k + self.ahead) * self.unit
        return b * (self.per_batch * self.unit) + (k + self.ahead) * self.unit

    def begun(self, b, k):
        return not isinstance(b, int) or b * self.per_batch + k + self.ahead > 0

    def in_register(self, eng, b, k):
        return self.at(b, k) if isinstance(b, int) else eng.to_reg(self.at(b, k))


class Steps:

    def __init__(self, raised, b):
        self.sem, self.raised, self.b, self.k = raised.sem, raised, b, 0

    def next(self):
        self.k += 1
        return self.raised.at(self.b, self.k)

    def end(self):
        assert self.k == self.raised.per_batch, (self.sem, self.k)


def run_until(strand, slot):
    while strand is not None and strand[0] <= slot:
        try:
            strand[0] = next(strand[1])
        except StopIteration:
            strand[0] = LAST + 1
            break


def rounds(eng, first, second, prepare):
    first(0, [0, prepare()] if prepare else None)
    first(1, [0, second(0)])
    with eng.Fori(2, NB) as b:
        first(b, [0, second(b - 1)])
    run_until([0, second(NB - 1)], LAST)


def side_by_side(*strands):
    nexts = [[next(strand), n, strand] for n, strand in enumerate(strands)]
    while nexts:
        first = min(nexts, key=lambda entry: entry[:2])
        try:
            first[0] = next(first[2])
        except StopIteration:
            nexts.remove(first)


def three_rounds(eng, first, second, third, prepare):
    side_by_side(first(0), *([prepare()] if prepare else []))
    side_by_side(first(1), second(0))
    with eng.Fori(2, NB) as b:
        side_by_side(first(b), second(b - 1), third(b - 2))
    side_by_side(second(NB - 1), third(NB - 2))
    side_by_side(third(NB - 1))


def at_b(ap, b):
    return ap[b:b + 1] if isinstance(b, int) else ap[bass.ds(b, 1)]


def hybrid_layers_kernel(nc, a, out):
    kernel_ctx = ExitStack()
    with kernel_ctx:
        def sig(name, per_batch=1, unit=1, ahead=0):
            return Signal(kernel_ctx.enter_context(nc.semaphore(name)), per_batch, unit, ahead)

        def keep(name, shape, dt=F32):
            return kernel_ctx.enter_context(nc.sbuf_tensor(name, shape, dt))

        bank = [kernel_ctx.enter_context(nc.psum_tensor(f"bank{i}", [P, 512], F32)) for i in range(8)]
        ident = keep("ident", [P, P])
        neg_half = keep("neg_half", [P, NJ])
        x2_dram = nc.dram_tensor("x2_dram", [NB, T, DM], F32, kind="Internal").ap()
        consts = sig("consts", 0)

        class Norm:

            def __init__(self, name, stat, n, n_pow, ahead=0):
                self.mean, self.sq = (sig(name + w, n, ahead=ahead) for w in ("_mean", "_sq"))
                self.var, self.rstd = (sig(name + w, n_pow, ahead=ahead) for w in ("_var", "_rstd"))
                self.total, self.neg, self.ss, self.v, self.r = (stat[:, i, :] for i in range(5))

        def norm_mean(dve, own, ln, src):
            nc.vector.tensor_reduce(ln.total, src, AX, ALU.add).then_inc(own.sem, 1)
            dve.wait_ge(own.sem, own.next())
            nc.vector.tensor_scalar(ln.neg, ln.total, -1.0 / DM, None, ALU.mult).then_inc(ln.mean.sem, 1)

        def norm_square(act, b, ln, k, src, junk):
            act.wait_ge(ln.mean.sem, ln.mean.at(b, k + 1))
            for j in range(NJ):
                ins = nc.scalar.activation(junk[:, j, :], src[:, j, :], ACT.Square, bias=ln.neg[:, j:j + 1],
                                           accum_out=ln.ss[:, j:j + 1])
            ins.then_inc(ln.sq.sem, 1)

        def norm_var(dve, b, ln, k, k_pow, eps):
            dve.wait_ge(ln.sq.sem, ln.sq.at(b, k + 1))
            nc.vector.tensor_scalar(ln.v, ln.ss, 1.0 / DM, eps, ALU.mult, ALU.add).then_inc(ln.var.sem, 1)

        def norm_rstd(pool, b, ln, k_pow):
            pool.wait_ge(ln.var.sem, ln.var.at(b, k_pow + 1))
            nc.gpsimd.tensor_tensor(ln.r, ln.v, neg_half[:, :], ALU.pow).then_inc(ln.rstd.sem, 1)

        def norm_apply(dve, b, ln, k_pow, dst, src):
            dve.wait_ge(ln.rstd.sem, ln.rstd.at(b, k_pow + 1))
            for j in range(NJ):
                ins = nc.vector.tensor_scalar(dst[:, j, :], src[:, j, :], ln.neg[:, j:j + 1], ln.r[:, j:j + 1],
                                              ALU.add, ALU.mult)
            return ins

        def transpose_tiles(dst_bank, src, k):
            for j in range(NJ):
                ins = nc.tensor.transpose(dst_bank[:, j * P:(j + 1) * P], src[:, j, k * P:(k + 1) * P], ident[:, :])
            return ins

        with ExitStack() as ctx:
            def sb(name, shape, dt=F32):
                return ctx.enter_context(nc.sbuf_tensor(name, shape, dt))

            ones_bf = sb("ones_bf", [P, P], BF16)
            one_hot = sb("one_hot", [P, 4, P], F32R)
            state_sum = sb("state_sum", [P, 4, 32])
            projT = sb("projT", [P, KD, CW])
            dt_inT = sb("dt_inT", [P, KD, DTR])
            dt_projT = sb("dt_projT", [P, 1, DI])
            outT = sb("outT", [P, NCT, DM])
            A_neg = sb("A_neg", [P, NCT * NT])
            per_ch = sb("per_ch", [P, NCT, 3 + KC])
            routeT = sb("routeT", [P, KD, NE * DM])
            expertT = sb("expertT", [P, KD, NE * DM])

            x0 = sb("x0", [P, NJ, DM])
            fa = sb("fa", [P, NJ, DM])
            xT = sb("xT", [P, KD, T])
            dtr = sb("dtr", [P, T])
            sp_w = sb("sp_w", [P, T])
            sp_ur = sb("sp_ur", [P, 2, T])
            sp_u, sp_r = sp_ur[:, 0, :], sp_ur[:, 1, :]
            x0_again = sp_ur[:, :, :].rearrange("p k (j d) -> p (k j) d", d=DM)
            xr = sb("xr", [P, KC - 1 + T])
            xact = sb("xact", [P, 2, T])
            zs = sb("zs", [P, 2, T])
            bc_sb = sb("bc_sb", [P, 2, T])
            dtx = sb("dtx", [P, T])
            halves = sb("halves", [P, 2, 2, 2, T], F32R)
            bias_part = sb("bias_part", [P, 3, 32], BF16)
            bias_rows = sb("bias_rows", [3, 2, NE * DM], BF16)
            b_rep = sb("b_rep", [P, B_BUFS, T])
            c_rep = sb("c_rep", [P, C_BUFS, T])
            dA = sb("dA", [P, A_BUFS, T])
            u = sb("u", [P, U_BUFS, T])
            h = sb("h", [P, H_BUFS, T])
            hc = sb("hc", [P, HC_BUFS, T])
            yz = sb("yz", [P, NCT, T])
            f_stat = sb("f_stat", [P, 5, NJ])
            b_dram = nc.dram_tensor("b_dram", [NB, DXB, T], F32, kind="Internal").ap()
            c_dram = nc.dram_tensor("c_dram", [NB, DI, T], F32, kind="Internal").ap()
            bias_dram = nc.dram_tensor("bias_dram", [3, 2, NE * DM], BF16, kind="Internal").ap()

            x1 = sb("x1", [P, NJ, DM])
            ma = sb("ma", [P, NJ, DM])
            mT = sb("mT", [P, KD, T])
            lg = sb("lg", [P, 2, NE, DM])
            hi_t, lo_t = sb("hi_t", [P, 4, DM]), sb("lo_t", [P, 4, DM])
            sel = sb("sel", [P, 2, 2, DM])
            gate_c = sb("gate_c", [P, 2, NE])
            spares = hi_t[:, :, :].rearrange("p a d -> p (a d)").bitcast(BF16).rearrange("p (e d) -> p e d", e=NE)
            acc = hi_t[:, 3, :]
            m_stat = sb("m_stat", [P, 5, NJ])
            stage = c_rep
            y_bank = bank[FRONT_BANKS]
            m_bank = bank[FRONT_BANKS + 1:]

            small_in = sig("small_in", 0, 16)
            f_ln = Norm("f", f_stat, 2, 2, ahead=1)
            x0_in, x0_back = sig("x0_in", 1, 16), sig("x0_back", 1, 16)
            xn0 = sig("xn0")
            f_done = sig("f_done", len(FRONT))
            xT_up = sig("xT_up", 2)
            dtr_up = sig("dtr_up")
            bsb_up, csb_up = sig("bsb_up"), sig("csb_up", NCT)
            sp_abs, sp_relu, sp_exp, sp_ln = (sig("sp_" + n, NCT) for n in ("abs", "relu", "exp", "ln"))
            xr_up, conv_up, xact_up, zs_up = (sig(n, NCT) for n in ("xr_up", "conv_up", "xact_up", "zs_up"))
            dt_up, dtx_up = sig("dt_up", NCT), sig("dtx_up", NCT)
            hi_up, lo_up = sig("hi_up", 2 * NCT), sig("lo_up", (2 * NCT - 1) * NQ)
            lo_first = sig("lo_first", NQ)
            b_out, c_out = sig("b_out", 1, 16), sig("c_out", NCT, 16)
            b_in = [sig(f"b_in{i}", NG // B_BUFS, 16) for i in range(B_BUFS)]
            c_in = [sig(f"c_in{i}", NH // C_BUFS, 16) for i in range(C_BUFS)]
            dA_up, u_up, h_up, hc_up, ysum = (sig(n, NCT * NT) for n in ("dA_up", "u_up", "h_up", "hc_up", "ysum"))
            y_read, yz_up = sig("y_read", NCT), sig("yz_up", NCT)
            fo_up = sig("fo_up", NJ)
            x1_up = sig("x1_up")
            f_step = sig("f_step", 3 + 6 * NCT, ahead=1)

            m_ln = Norm("m", m_stat, 2, 2)
            m_done = sig("m_done", sum(n[0] != "pad" for n in MOE))
            xm_up, mT_up = sig("xm_up"), sig("mT_up", 2)
            lg_up = sig("lg_up", 4 * NJ)
            gap_up, d1_up, tanh_up, c_up = (sig(n, NJ) for n in ("gap_up", "d1_up", "tanh_up", "c_up"))
            mix_up = sig("mix_up", 4 * NJ)
            x2_up, x2_out = sig("x2_up"), sig("x2_out", 1, 16)
            m_step = sig("m_step", 3 + 12 * NJ)

            prep_in = [sig(f"prep_in{i}", 0, 16) for i in range(STAGES)]
            late_in = [sig(f"late_in{i}", 0, 16) for i in range(STAGES)]
            late_done, late_up = sig("late_done", 0), sig("late_up", 0)
            prep_done, prep_act, prep_dve = sig("prep_done", 0), sig("prep_act", 0), sig("prep_dve", 0)
            bias_split, bias_out, bias_in = sig("bias_split", 0), sig("bias_out", 0, 16), sig("bias_in", 0, 16)

            def low_steps(splits):
                return splits * NQ - (NQ if splits >= 2 else 0)

            def front_reader(name):
                kind, i = name
                return {"xT": xT_up, "dtr": dtr_up, "B": bsb_up, "dt": sp_relu, "x": xr_up, "C": csb_up,
                        "z": zs_up, "dA": dA_up, "dtx": u_up, "out": fo_up}[kind], i + 1

            def moe_reader(name):
                kind, i = name
                return {"mT": mT_up, "route": lg_up, "expert": mix_up}[kind], i + 1

            units = []

            def unit(loads, turns, dst):
                units.append((loads, turns, dst))

            def row_pair(srcs, dst, col):
                m = len(srcs)
                unit([(r * DM, slice(0, P), s) for r, s in enumerate(srcs)],
                     [(k * m * P + r * P, r * DM + k * P) for r in range(m) for k in range(KD)],
                     dst[:, :, col:col + m * P])

            w_in = a["L0_attn_in_proj_w"]
            row = lambda w, t: w[t * P:(t + 1) * P, :]
            row_pair([row(a["L0_attn_dt_in_proj_w"], 0)], dt_inT, 0)
            unit([(0, slice(0, P), a["L0_attn_dt_proj_w"].rearrange("(t p) k -> p t k", p=P))],
                 [(t * P, t * P) for t in range(NCT)], dt_projT[:, :, :])
            row_pair([row(w_in, (DI + DXB) // P)], projT, CB)
            for t in range(0, NCT, 2):
                loads = []
                for r in range(2):
                    for g in range(2):
                        src = w_in[DI + (2 * (t + r) + g) * NS:DI + (2 * (t + r) + g + 1) * NS, :]
                        loads.append((r * DM, slice(g * REP * NS, (g + 1) * REP * NS),
                                      src.unsqueeze(0).to_broadcast([REP, NS, DM])))
                unit(loads, [(k * 2 * P + r * P, r * DM + k * P) for r in range(2) for k in range(KD)],
                     projT[:, :, CX + t * P:CX + (t + 2) * P])
            for t in range(0, NCT, 2):
                row_pair([row(w_in, (DI + 2 * DXB) // P + t + r) for r in range(2)], projT, CC + t * P)
            for t in range(0, NCT, 2):
                row_pair([row(w_in, t + r) for r in range(2)], projT, CZ + t * P)
            for t in range(KD):
                unit([(0, slice(0, P), row(a["L0_attn_out_proj_w"], t))],
                     [(c * P, c * P) for c in range(NCT)], outT[:, :, t * P:(t + 1) * P])
            w_route = a["L0_ffn_router_w"].rearrange("(o e) d -> e o d", e=NE)
            w_expert = a["L0_ffn_expert_w"]
            late = [(w[e], dst[:, :, e * DM:(e + 1) * DM]) for w, dst in ((w_route, routeT), (w_expert, expertT))
                    for e in range(NE)]
            late_slot = lambda n: lg[:, 0, 2 * (n % STAGES):2 * (n % STAGES) + 2, :]
            loaded = [0] * STAGES
            unit_loaded = []
            for n, (loads, _, _) in enumerate(units):
                loaded[n % STAGES] += len(loads)
                unit_loaded.append(loaded[n % STAGES])

            block = ctx.enter_context(nc.Block())

            @block.sync
            def _(sp):
                def load_unit(n):
                    if n >= STAGES:
                        sp.wait_ge(prep_done.sem, prep_done.at(0, n - STAGES + 1))
                    for col, pp, src in units[n][0]:
                        width = src.shape[-1] * (src.shape[1] if len(src.shape) == 3 and pp == slice(0, P) else 1)
                        dst = stage[pp, n % STAGES, col:col + width]
                        if len(src.shape) == 3 and pp == slice(0, P):
                            dst = dst.rearrange("p (t k) -> p t k", t=src.shape[1])
                        sp.dma_start(dst, src).then_inc(prep_in[n % STAGES].sem, 16)

                def load_x0(b):
                    sp.dma_start(x0[:, :, :], at_b(a["x"], b).rearrange("b (j p) d -> p (b j) d", p=P)
                                 ).then_inc(x0_in.sem, 16)

                def c_replica(b, hd):
                    freed = hc_up.in_register(sp, b, 2 * (hd - C_BUFS) + 2)
                    if hd % 8 == 0:
                        sp.wait_ge(c_out.sem, c_out.at(b, hd // 8 + 1))
                    if hc_up.begun(b, 2 * (hd - C_BUFS) + 2):
                        sp.wait_ge(hc_up.sem, freed)
                    src = at_b(c_dram, b)[:, hd * NS:(hd + 1) * NS, :].rearrange("b n t -> (b n) t")
                    sp.dma_start(c_rep[:, hd % C_BUFS, :], src.unsqueeze(0).to_broadcast([NP, NS, T])
                                 ).then_inc(c_in[hd % C_BUFS].sem, 16)

                def b_replica(b, g):
                    if g == 0:
                        sp.wait_ge(b_out.sem, b_out.at(b, 1))
                    if u_up.begun(b, 8 * (g - B_BUFS) + 8):
                        sp.wait_ge(u_up.sem, u_up.at(b, 8 * (g - B_BUFS) + 8))
                    src = at_b(b_dram, b)[:, g * NS:(g + 1) * NS, :].rearrange("b n t -> (b n) t")
                    sp.dma_start(b_rep[:, g % B_BUFS, :], src.unsqueeze(0).to_broadcast([NP, NS, T])
                                 ).then_inc(b_in[g % B_BUFS].sem, 16)

                def c_write(b, ct):
                    sp.wait_ge(csb_up.sem, csb_up.at(b, ct + 1))
                    sp.dma_start(at_b(c_dram, b)[:, ct * P:(ct + 1) * P, :].rearrange("b n t -> (b n) t"),
                                 bc_sb[:, 1, :]).then_inc(c_out.sem, 16)

                def load_late(n):
                    if n >= STAGES:
                        sp.wait_ge(late_done.sem, late_done.at(0, n - STAGES + 1))
                    sp.dma_start(late_slot(n), late[n][0].rearrange("(r p) d -> p r d", p=P)
                                 ).then_inc(late_in[n % STAGES].sem, 16)

                def front(b, following):
                    sp.wait_ge(bsb_up.sem, bsb_up.at(b, 1))
                    sp.dma_start(at_b(b_dram, b).rearrange("b n t -> (b n) t"), bc_sb[:, 0, :]).then_inc(b_out.sem, 16)
                    for g in range(B_BUFS):
                        b_replica(b, g)
                    c_write(b, 0)
                    for hd in range(C_BUFS):
                        c_replica(b, hd)
                    sp.wait_ge(f_done.sem, f_done.at(b, FRONT_AT[("xT", KD - 1)] + 1))
                    load_x0(following)
                    for ct in range(NCT):
                        if ct == NCT - 1:
                            sp.wait_ge(lo_up.sem, lo_up.at(b, low_steps(2 * NCT)))
                            sp.dma_start(x0_again, at_b(a["x"], b).rearrange("b (j p) d -> p (b j) d", p=P)
                                         ).then_inc(x0_back.sem, 16)
                        for i in range(8):
                            hd = 8 * ct + i + C_BUFS
                            if isinstance(b, int) and b == 0:
                                for n in LATE_LOADS[8 * ct + i]:
                                    load_late(n)
                            if i == 4 and ct + 1 < NCT:
                                c_write(b, ct + 1)
                            if hd < NH:
                                c_replica(b, hd)
                            if i in (3, 7) and 2 * ct + i // 4 + B_BUFS < NG:
                                b_replica(b, 2 * ct + i // 4 + B_BUFS)

                def send_x2(b):
                    sp.wait_ge(x2_up.sem, x2_up.at(b, 1))
                    sp.dma_start(at_b(x2_dram, b).rearrange("b (j p) d -> p (b j) d", p=P), ma[:, :, :]
                                 ).then_inc(x2_out.sem, 16)

                by_ch = lambda ap: ap.rearrange("(c p) -> p c", p=P)
                load_x0(0)
                for n in range(STAGES):
                    load_unit(n)
                for i, nm in ((DTB, "dt_proj_b"), (CNB, "conv_b"), (DSK, "D")):
                    sp.dma_start(per_ch[:, :, i], by_ch(a["L0_attn_" + nm]),
                                 allow_slow_non_contiguous=True).then_inc(small_in.sem, 16)
                sp.dma_start(per_ch[:, :, TAP:TAP + KC], a["L0_attn_conv_w"].rearrange("(c p) k -> p c k", p=P)
                             ).then_inc(small_in.sem, 16)
                sp.dma_start(sp_w[0:NCT * NT, 0:P], a["L0_attn_A_log"].rearrange("(s c) n -> s (c n)", c=NP)
                             ).then_inc(small_in.sem, 16)
                sp.dma_start(sp_u[:, 0:16], a["L0_ffn_router_b"].rearrange("(p i) -> p i", p=P)).then_inc(small_in.sem, 16)
                sp.dma_start(sp_u[:, 16:32], a["L0_ffn_expert_b"].rearrange("e (q i) -> (e q) i", i=16)
                             ).then_inc(small_in.sem, 16)
                for n in range(STAGES, len(units)):
                    load_unit(n)
                sp.wait_ge(bias_split.sem, bias_split.at(0, 3))
                for part in range(3):
                    for v in range(2):
                        sp.dma_start(bias_dram[part, v, :].rearrange("(p i) -> p i", p=P),
                                     bias_part[:, part, 16 * v:16 * v + 16]).then_inc(bias_out.sem, 16)
                sp.wait_ge(bias_out.sem, bias_out.at(0, 6))
                sp.dma_start(bias_rows[:, :, :], bias_dram).then_inc(bias_in.sem, 16)
                front(0, 1)
                with sp.Fori(2, NB) as b:
                    front(b - 1, b)
                    send_x2(b - 2)
                front(NB - 1, NB - 1)
                send_x2(NB - 2)
                send_x2(NB - 1)
                sp.wait_ge(x2_out.sem, x2_out.at(NB, 0))

            @block.tensor
            def _(pe):
                def prepare():
                    pe.wait_ge(consts.sem, consts.at(0, 5 + NQ))
                    for n, (loads, turns, dst) in enumerate(units):
                        pe.wait_ge(prep_in[n % STAGES].sem, prep_in[n % STAGES].at(0, unit_loaded[n]))
                        if n >= 4:
                            emptied = prep_act if n % 2 == 0 else prep_dve
                            pe.wait_ge(emptied.sem, emptied.at(0, (n - 4) // 2 + 1))
                        for col, scol in turns:
                            ins = nc.tensor.transpose(bank[n % 4][:, col:col + P], stage[:, n % STAGES, scol:scol + P],
                                                      ident[:, :])
                        ins.then_inc(prep_done.sem, 1)
                    pe.wait_ge(small_in.sem, small_in.at(0, 7))
                    nc.tensor.transpose(y_bank[:, 0:NCT * NT], sp_w[0:NCT * NT, 0:P], ident[0:NCT * NT, 0:NCT * NT]
                                        ).then_inc(prep_done.sem, 1)
                    pe.wait_ge(prep_act.sem, prep_act.at(0, (len(units) + 1) // 2 + 1))
                    pe.wait_ge(prep_dve.sem, prep_dve.at(0, len(units) // 2 + 1))

                def front_bank(b, name):
                    n = FRONT_AT[name]
                    freed_by, k = front_reader(FRONT[n - FRONT_BANKS])
                    if freed_by.begun(b, k if n >= FRONT_BANKS else k - freed_by.per_batch):
                        pe.wait_ge(freed_by.sem, freed_by.at(b, k if n >= FRONT_BANKS else k - freed_by.per_batch))
                    return bank[n % FRONT_BANKS]

                def project(b, name, lhsT, rhs):
                    dst = front_bank(b, name)
                    for k, (l, r) in enumerate(zip(lhsT, rhs)):
                        ins = nc.tensor.matmul(dst[:, :], l, r, start=(k == 0), stop=(k == len(lhsT) - 1))
                    ins.then_inc(f_done.sem, 1)

                x_feat = [xT[:, k, :] for k in range(KD)]

                def unit_product(b, kind, ct):
                    if kind == "dt":
                        pe.wait_ge(dtr_up.sem, dtr_up.at(b, 1))
                        project(b, (kind, ct), [dt_projT[:, 0, ct * P:(ct + 1) * P]], [dtr[:, :]])
                    else:
                        c0 = {"x": CX, "C": CC, "z": CZ}[kind] + ct * P
                        project(b, (kind, ct), [projT[:, k, c0:c0 + P] for k in range(KD)], x_feat)

                def state_sums(b, s):
                    ct, q, k = s // NT, s % NT // 4, s % 4
                    if s % NT == 0:
                        if y_read.begun(b, ct):
                            pe.wait_ge(y_read.sem, y_read.at(b, ct))
                    pe.wait_ge(hc_up.sem, hc_up.at(b, s + 1))
                    nc.tensor.matmul(y_bank[32 * q:32 * q + 32, :], state_sum[:, k, :], hc[:, s % HC_BUFS, :],
                                     start=(k == 0), stop=(k == 3)).then_inc(ysum.sem, 1)

                def front(b, moe):
                    pe.wait_ge(xn0.sem, xn0.at(b, 1))
                    for k in range(KD):
                        transpose_tiles(front_bank(b, ("xT", k)), x0, k).then_inc(f_done.sem, 1)
                    pe.wait_ge(xT_up.sem, xT_up.at(b, 2))
                    project(b, ("dtr", 0), [dt_inT[:, k, :] for k in range(KD)], x_feat)
                    project(b, ("B", 0), [projT[:, k, CB:CB + DXB] for k in range(KD)], x_feat)
                    for pair in UNIT_AT.values():
                        for kind in pair:
                            unit_product(b, kind, 0)
                    run_until(moe, 5)
                    for s in range(NCT * NT):
                        ct, i = s // NT, s % NT
                        if i == 0:
                            pe.wait_ge(lo_up.sem, lo_up.at(b, low_steps(2 * ct + 2)))
                            if ct == 0:
                                pe.wait_ge(lo_first.sem, lo_first.at(b, NQ))
                        q, k = i // 4, i % 4
                        for v, name in enumerate(("dA", "dtx")):
                            rows = slice(64 * (q // 2), 64 * (q // 2) + 64)
                            nc.tensor.matmul(front_bank(b, (name, s))[:, :], one_hot[rows, k, :],
                                             halves[rows, ct % 2, v, q % 2, :], start=True, stop=True
                                             ).then_inc(f_done.sem, 1)
                        if i in UNIT_AT and ct + 1 < NCT:
                            for kind in UNIT_AT[i]:
                                unit_product(b, kind, ct + 1)
                        for t in SUMS_AT[s]:
                            state_sums(b, t)
                        run_until(moe, 8 + s)
                    last_sums = SUMS_AT[NCT * NT]
                    for j in range(NJ):
                        dst = front_bank(b, ("out", j))
                        pe.wait_ge(yz_up.sem, yz_up.at(b, NCT - 1))
                        for ct in range(NCT - 1):
                            nc.tensor.matmul(dst[:, 0:DM], yz[:, ct, j * P:(j + 1) * P], outT[:, ct, :],
                                             start=(ct == 0), stop=False)
                        for s in last_sums[j:j + 1] if j < NJ - 1 else last_sums[j:]:
                            state_sums(b, s)
                    run_until(moe, 8 + NCT * NT)
                    pe.wait_ge(yz_up.sem, yz_up.at(b, NCT))
                    for j in range(NJ):
                        nc.tensor.matmul(bank[FRONT_AT[("out", j)] % FRONT_BANKS][:, 0:DM],
                                         yz[:, NCT - 1, j * P:(j + 1) * P], outT[:, NCT - 1, :],
                                         start=False, stop=True).then_inc(f_done.sem, 1)
                    run_until(moe, LAST)

                def moe_bank(b, name):
                    n = MOE_AT[name]
                    before = MOE[n - MOE_BANKS]
                    if before[0] == "pad":
                        before = MOE[n - 2 * MOE_BANKS]
                    freed_by, k = moe_reader(before)
                    if freed_by.begun(b, k if n >= MOE_BANKS else k - freed_by.per_batch):
                        pe.wait_ge(freed_by.sem, freed_by.at(b, k if n >= MOE_BANKS else k - freed_by.per_batch))
                    return m_bank[n % MOE_BANKS]

                def moe(b):
                    yield 3
                    pe.wait_ge(xm_up.sem, xm_up.at(b, 1))
                    for k in range(KD):
                        transpose_tiles(moe_bank(b, ("mT", k)), ma, k).then_inc(m_done.sem, 1)
                    yield PE_SLOT[0]
                    pe.wait_ge(mT_up.sem, mT_up.at(b, 2))
                    for (kind, i), slot in zip(MOE[2:-2], PE_SLOT):
                        yield slot
                        j, c = i // 4, i % 4
                        w = routeT if kind == "route" else expertT
                        if kind == "route":
                            bias = bias_rows[:, 0, :].rearrange("a (o e) -> a e o", e=NE)[:, 2 * c:2 * c + 2, :]
                        else:
                            bias = bias_rows[:, 1, c * 512:(c + 1) * 512]
                        dst = moe_bank(b, (kind, i))
                        for k in range(KD):
                            nc.tensor.matmul(dst[:, :], mT[:, k, j * P:(j + 1) * P], w[:, k, c * 512:(c + 1) * 512],
                                             start=(k == 0), stop=False)
                        nc.tensor.matmul(dst[:, :].rearrange("p (e o) -> p e o", e=2) if kind == "route" else dst[:, :],
                                         ones_bf[0:3, :], bias, start=False, stop=True,
                                         ).then_inc(m_done.sem, 1)

                def late_units():
                    for n, slot in enumerate(LATE_PE):
                        yield slot
                        pe.wait_ge(late_in[n % STAGES].sem, late_in[n % STAGES].at(0, n // STAGES + 1))
                        if n >= MOE_BANKS:
                            pe.wait_ge(late_up.sem, late_up.at(0, n - MOE_BANKS + 1))
                        for r in range(2):
                            for k in range(KD):
                                ins = nc.tensor.transpose(m_bank[n % MOE_BANKS][:, k * DM + r * P:k * DM + (r + 1) * P],
                                                          late_slot(n)[:, r, k * P:(k + 1) * P], ident[:, :])
                        ins.then_inc(late_done.sem, 1)
                    yield LAST
                    pe.wait_ge(late_up.sem, late_up.at(0, 2 * NE))

                prepare()
                pe.wait_ge(bias_in.sem, bias_in.at(0, 1))
                rounds(pe, front, moe, late_units)

            @block.scalar
            def _(act):
                def prepare():
                    for n in range(0, len(units), 2):
                        act.wait_ge(prep_done.sem, prep_done.at(0, n + 1))
                        dst = units[n][2]
                        nc.scalar.copy(dst, bank[n % 4][:, 0:dst.shape[1] * dst.shape[2]]
                                       .rearrange("p (k c) -> p k c", k=dst.shape[1])).then_inc(prep_act.sem, 1)
                    act.wait_ge(prep_done.sem, prep_done.at(0, len(units) + 1))
                    nc.scalar.activation(A_neg[:, :], y_bank[:, 0:NCT * NT], ACT.Exp).then_inc(prep_act.sem, 1)
                    act.wait_ge(small_in.sem, small_in.at(0, 7))
                    nc.scalar.copy(bias_part[:, 0, :], sp_u[:, 0:32]).then_inc(bias_split.sem, 1)
                    act.wait_ge(prep_dve.sem, prep_dve.at(0, len(units) // 2 + 2))
                    nc.scalar.copy(bias_part[:, 1, :], sp_r[:, 0:32]).then_inc(bias_split.sem, 1)

                def take_dt(b, ct):
                    src = bank[FRONT_AT[("dt", ct)] % FRONT_BANKS][:, :]
                    act.wait_ge(f_done.sem, f_done.at(b, FRONT_AT[("dt", ct)] + 1))
                    if dt_up.begun(b, ct):
                        act.wait_ge(dt_up.sem, dt_up.at(b, ct))
                    if ct == 0 and x1_up.begun(b, 0):
                        act.wait_ge(x1_up.sem, x1_up.at(b, 0))
                    bias = per_ch[:, ct, DTB:DTB + 1]
                    nc.scalar.activation(sp_u, src, ACT.Abs, bias=bias).then_inc(sp_abs.sem, 1)
                    if hi_up.begun(b, 2 * ct - 1):
                        act.wait_ge(hi_up.sem, hi_up.at(b, 2 * ct - 1))
                    if lo_up.begun(b, low_steps(2 * ct - 1)):
                        act.wait_ge(lo_up.sem, lo_up.at(b, low_steps(2 * ct - 1)))
                    if dtx_up.begun(b, ct):
                        act.wait_ge(dtx_up.sem, dtx_up.at(b, ct))
                    nc.scalar.activation(sp_r, src, ACT.Relu, bias=bias).then_inc(sp_relu.sem, 1)

                def dt_exp(b, ct):
                    act.wait_ge(sp_abs.sem, sp_abs.at(b, ct + 1))
                    nc.scalar.activation(sp_u, sp_u, ACT.Exp, scale=-1.0).then_inc(sp_exp.sem, 1)

                def dt_log(b, ct):
                    act.wait_ge(sp_exp.sem, sp_exp.at(b, ct + 1))
                    nc.scalar.activation(sp_w[:, :], sp_u, ACT.Ln, bias=1.0).then_inc(sp_ln.sem, 1)

                def take_x(b, ct):
                    act.wait_ge(f_done.sem, f_done.at(b, FRONT_AT[("x", ct)] + 1))
                    if conv_up.begun(b, ct):
                        act.wait_ge(conv_up.sem, conv_up.at(b, ct))
                    nc.scalar.copy(xr[:, KC - 1:], bank[FRONT_AT[("x", ct)] % FRONT_BANKS][:, :]).then_inc(xr_up.sem, 1)

                def take_c(b, ct):
                    act.wait_ge(f_done.sem, f_done.at(b, FRONT_AT[("C", ct)] + 1))
                    if c_out.begun(b, ct):
                        act.wait_ge(c_out.sem, c_out.at(b, ct))
                    nc.scalar.copy(bc_sb[:, 1, :], bank[FRONT_AT[("C", ct)] % FRONT_BANKS][:, :]
                                   ).then_inc(csb_up.sem, 1)

                def silus(b, ct):
                    act.wait_ge(conv_up.sem, conv_up.at(b, ct + 1))
                    nc.scalar.activation(xact[:, ct % 2, :], xact[:, ct % 2, :], ACT.Silu).then_inc(xact_up.sem, 1)
                    act.wait_ge(f_done.sem, f_done.at(b, FRONT_AT[("z", ct)] + 1))
                    if yz_up.begun(b, ct - 1):
                        act.wait_ge(yz_up.sem, yz_up.at(b, ct - 1))
                    nc.scalar.activation(zs[:, ct % 2, :], bank[FRONT_AT[("z", ct)] % FRONT_BANKS][:, :],
                                         ACT.Silu).then_inc(zs_up.sem, 1)

                def high_part(b, ct, v):
                    made = dtx_up if v else dt_up
                    act.wait_ge(made.sem, made.at(b, ct + 1))
                    last = FRONT_AT[("dtx", (ct - 2) % NCT * NT + NT - 1)] + 1 - (len(FRONT) if ct < 2 else 0)
                    if f_done.begun(b, last):
                        act.wait_ge(f_done.sem, f_done.at(b, last))
                    for odd in range(2):
                        ins = nc.scalar.copy(halves[:, ct % 2, v, odd, :], dtx[:, :] if v else sp_r)
                    ins.then_inc(hi_up.sem, 1)

                def front(b, moe):
                    act.wait_ge(f_ln.sq.sem, f_ln.sq.at(b, 0))
                    for k in range(KD):
                        act.wait_ge(f_done.sem, f_done.at(b, FRONT_AT[("xT", k)] + 1))
                        nc.scalar.copy(xT[:, k, :], bank[FRONT_AT[("xT", k)] % FRONT_BANKS][:, :]).then_inc(xT_up.sem, 1)
                    run_until(moe, 0)
                    take_dt(b, 0)
                    take_x(b, 0)
                    dt_exp(b, 0)
                    dt_log(b, 0)
                    take_c(b, 0)
                    high_part(b, 0, 0)
                    silus(b, 0)
                    run_until(moe, 3)
                    high_part(b, 0, 1)
                    run_until(moe, 5)
                    for s in range(NCT * NT):
                        ct, i = s // NT, s % NT
                        n = FRONT_AT[("dA", s)]
                        act.wait_ge(f_done.sem, f_done.at(b, n + 1))
                        if h_up.begun(b, s - A_BUFS + 1):
                            act.wait_ge(h_up.sem, h_up.at(b, s - A_BUFS + 1))
                        nc.scalar.activation(dA[:, s % A_BUFS, :], bank[n % FRONT_BANKS][:, :], ACT.Exp,
                                             scale=A_neg[:, s:s + 1]).then_inc(dA_up.sem, 1)
                        if ct + 1 < NCT:
                            if i == 2:
                                take_dt(b, ct + 1)
                                take_x(b, ct + 1)
                                dt_exp(b, ct + 1)
                            if i == 3:
                                dt_log(b, ct + 1)
                            if i == 5:
                                take_c(b, ct + 1)
                                high_part(b, ct + 1, 0)
                            if i == 6:
                                silus(b, ct + 1)
                            if i == 8:
                                high_part(b, ct + 1, 1)
                        elif i == X0_AT["square"]:
                            norm_square(act, b, f_ln, 0, x0, fa)
                        run_until(moe, 8 + s)
                    for j in range(NJ):
                        act.wait_ge(f_done.sem, f_done.at(b, FRONT_AT[("out", j)] + 1))
                        nc.scalar.copy(fa[:, j, :], bank[FRONT_AT[("out", j)] % FRONT_BANKS][:, 0:DM]
                                       ).then_inc(fo_up.sem, 1)
                    norm_square(act, b, f_ln, 1, fa, xT[:, :, :].rearrange("p k (j d) -> p (k j) d", d=DM))
                    run_until(moe, LAST)

                def moe(b):
                    if x2_out.begun(b, 0):
                        act.wait_ge(x2_out.sem, x2_out.at(b, 0))
                    norm_square(act, b, m_ln, 0, x1, ma)
                    yield 3
                    for k in range(KD):
                        act.wait_ge(m_done.sem, m_done.at(b, MOE_AT[("mT", k)] + 1))
                        nc.scalar.copy(mT[:, k, :], m_bank[MOE_AT[("mT", k)] % MOE_BANKS][:, :]).then_inc(mT_up.sem, 1)
                    for n, (kind, i) in enumerate(MOE[2:-2]):
                        yield ACT_SLOT[n]
                        j, c = i // 4, i % 4
                        if MOE[2 + n - 4] in [("route", 4 * t + 3) for t in range(NJ)]:
                            t = MOE[2 + n - 4][1] // 4
                            act.wait_ge(gap_up.sem, gap_up.at(b, t + 1))
                            nc.scalar.activation(sel[:, t % 2, 0, :], sel[:, t % 2, 0, :], ACT.Tanh, scale=0.5
                                                 ).then_inc(tanh_up.sem, 1)
                        if kind == "route":
                            act.wait_ge(m_done.sem, m_done.at(b, MOE_AT[(kind, i)] + 1))
                            if c == 0:
                                if c_up.begun(b, j - 1):
                                    act.wait_ge(c_up.sem, c_up.at(b, j - 1))
                            nc.scalar.copy(lg[:, j % 2, 2 * c:2 * c + 2, :],
                                           m_bank[MOE_AT[(kind, i)] % MOE_BANKS][:, :]
                                           .rearrange("p (e o) -> p e o", e=2)).then_inc(lg_up.sem, 1)
                    yield LAST
                    norm_square(act, b, m_ln, 1, ma, lg[:, 0, :, :])

                def late_units():
                    for n, slot in enumerate(LATE_ACT):
                        yield slot
                        act.wait_ge(late_done.sem, late_done.at(0, n + 1))
                        nc.scalar.copy(late[n][1], m_bank[n % MOE_BANKS][:, :].rearrange("p (k c) -> p k c", k=KD)
                                       ).then_inc(late_up.sem, 1)

                norm_square(act, 0, f_ln, -1, x0, fa)
                prepare()
                rounds(act, front, moe, late_units)

            @block.vector
            def _(dve):
                def prepare():
                    nc.vector.memset(xr[:, 0:KC - 1], 0.0)
                    for n in range(1, len(units), 2):
                        dve.wait_ge(prep_done.sem, prep_done.at(0, n + 1))
                        dst = units[n][2]
                        nc.vector.tensor_copy(dst, bank[n % 4][:, 0:dst.shape[1] * dst.shape[2]]
                                              .rearrange("p (k c) -> p k c", k=dst.shape[1])).then_inc(prep_dve.sem, 1)
                    dve.wait_ge(prep_act.sem, prep_act.at(0, (len(units) + 1) // 2 + 1))
                    nc.vector.tensor_scalar(A_neg[:, :], A_neg[:, :], -1.0, None, ALU.mult).then_inc(prep_dve.sem, 1)
                    dve.wait_ge(small_in.sem, small_in.at(0, 7))
                    dve.wait_ge(bias_split.sem, bias_split.at(0, 1))
                    nc.vector.tensor_tensor(sp_r[:, 0:32], sp_u[:, 0:32], bias_part[:, 0, :], ALU.subtract
                                            ).then_inc(prep_dve.sem, 1)
                    dve.wait_ge(bias_split.sem, bias_split.at(0, 2))
                    nc.vector.tensor_tensor(bias_part[:, 2, :], sp_r[:, 0:32], bias_part[:, 1, :], ALU.subtract
                                            ).then_inc(bias_split.sem, 1)

                def soft_plus(b, ct, own):
                    exact = dtx[:, :]
                    if hi_up.begun(b, 2 * ct):
                        dve.wait_ge(hi_up.sem, hi_up.at(b, 2 * ct))
                    if ct == 1:
                        dve.wait_ge(lo_first.sem, lo_first.at(b, NQ))
                    elif lo_up.begun(b, low_steps(2 * ct)):
                        dve.wait_ge(lo_up.sem, lo_up.at(b, low_steps(2 * ct)))
                    dve.wait_ge(sp_exp.sem, sp_exp.at(b, ct + 1))
                    nc.vector.tensor_scalar(exact, sp_u, 1.0, -1.0, ALU.add, ALU.add).then_inc(own.sem, 1)
                    dve.wait_ge(own.sem, own.next())
                    nc.vector.tensor_tensor(exact, sp_u, exact, ALU.subtract).then_inc(own.sem, 1)
                    dve.wait_ge(own.sem, own.next())
                    dve.wait_ge(sp_ln.sem, sp_ln.at(b, ct + 1))
                    nc.vector.tensor_tensor(exact, exact, sp_w[:, :], ALU.add).then_inc(own.sem, 1)
                    dve.wait_ge(own.sem, own.next())
                    nc.vector.tensor_tensor(sp_r, sp_r, exact, ALU.add).then_inc(dt_up.sem, 1)

                def convolve(b, ct, own):
                    dst = xact[:, ct % 2, :]
                    tap = lambda k: per_ch[:, ct, TAP + k:TAP + k + 1]
                    dve.wait_ge(xr_up.sem, xr_up.at(b, ct + 1))
                    nc.vector.tensor_scalar(dst, xr[:, 0:T], tap(0), per_ch[:, ct, CNB:CNB + 1],
                                            ALU.mult, ALU.add).then_inc(own.sem, 1)
                    dve.wait_ge(own.sem, own.next())
                    for k in range(1, KC):
                        ins = nc.vector.scalar_tensor_tensor(dst, xr[:, k:k + T], tap(k), dst, ALU.mult, ALU.add)
                        if k < KC - 1:
                            ins.then_inc(own.sem, 1)
                            dve.wait_ge(own.sem, own.next())
                    ins.then_inc(conv_up.sem, 1)

                def dt_times_x(b, ct):
                    dve.wait_ge(xact_up.sem, xact_up.at(b, ct + 1))
                    dve.wait_ge(dt_up.sem, dt_up.at(b, ct + 1))
                    nc.vector.tensor_tensor(dtx[:, :], sp_r, xact[:, ct % 2, :], ALU.mult).then_inc(dtx_up.sem, 1)

                def input_term(b, s):
                    g, n = s // 8, FRONT_AT[("dtx", s)]
                    dve.wait_ge(f_done.sem, f_done.at(b, n + 1))
                    if s % 8 == 0:
                        dve.wait_ge(b_in[g % B_BUFS].sem, b_in[g % B_BUFS].at(b, g // B_BUFS + 1))
                    if h_up.begun(b, s - U_BUFS + 1):
                        dve.wait_ge(h_up.sem, h_up.at(b, s - U_BUFS + 1))
                    nc.vector.tensor_tensor(u[:, s % U_BUFS, :], bank[n % FRONT_BANKS][:, :], b_rep[:, g % B_BUFS, :],
                                            ALU.mult).then_inc(u_up.sem, 1)

                def scan(b, s):
                    dve.wait_ge(dA_up.sem, dA_up.at(b, s + 1))
                    dve.wait_ge(u_up.sem, u_up.at(b, s + 1))
                    if hc_up.begun(b, s - H_BUFS + 1):
                        dve.wait_ge(hc_up.sem, hc_up.at(b, s - H_BUFS + 1))
                    nc.vector.tensor_tensor_scan(h[:, s % H_BUFS, :], dA[:, s % A_BUFS, :],
                                                 u[:, s % U_BUFS, :], 0.0, ALU.mult, ALU.add).then_inc(h_up.sem, 1)

                def gate(b, ct):
                    dve.wait_ge(ysum.sem, ysum.at(b, (ct + 1) * NT))
                    nc.vector.scalar_tensor_tensor(yz[:, ct, :], xact[:, ct % 2, :], per_ch[:, ct, DSK:DSK + 1],
                                                   y_bank[:, :], ALU.mult, ALU.add).then_inc(y_read.sem, 1)
                    dve.wait_ge(y_read.sem, y_read.at(b, ct + 1))
                    dve.wait_ge(zs_up.sem, zs_up.at(b, ct + 1))
                    nc.vector.tensor_tensor(yz[:, ct, :], yz[:, ct, :], zs[:, ct % 2, :], ALU.mult).then_inc(yz_up.sem, 1)

                def front(b, moe):
                    own = Steps(f_step, b)
                    run_until(moe, 0)
                    dve.wait_ge(f_done.sem, f_done.at(b, FRONT_AT[("dtr", 0)] + 1))
                    nc.vector.tensor_copy(dtr[:, :], bank[FRONT_AT[("dtr", 0)] % FRONT_BANKS][:, :]).then_inc(dtr_up.sem, 1)
                    dve.wait_ge(f_done.sem, f_done.at(b, FRONT_AT[("B", 0)] + 1))
                    if b_out.begun(b, 0):
                        dve.wait_ge(b_out.sem, b_out.at(b, 0))
                    nc.vector.tensor_copy(bc_sb[:, 0, :], bank[FRONT_AT[("B", 0)] % FRONT_BANKS][:, :]
                                          ).then_inc(bsb_up.sem, 1)
                    run_until(moe, 1)
                    soft_plus(b, 0, own)
                    run_until(moe, 2)
                    convolve(b, 0, own)
                    dt_times_x(b, 0)
                    dve.wait_ge(hi_up.sem, hi_up.at(b, 2))
                    for q in range(NQ):
                        here, beside = slice(32 * q, 32 * q + 32), slice(32 * (q ^ 1), 32 * (q ^ 1) + 32)
                        nc.vector.tensor_tensor(halves[beside, 0, 1, q % 2, :], dtx[here, :],
                                                halves[here, 0, 1, q % 2, :], ALU.subtract).then_inc(lo_first.sem, 1)
                    input_term(b, 0)
                    for s in range(NCT * NT):
                        ct, i = s // NT, s % NT
                        if s + 1 < NCT * NT:
                            input_term(b, s + 1)
                        scan(b, s)
                        if i == GATE_AT and ct > 0:
                            gate(b, ct - 1)
                        if ct + 1 < NCT:
                            if i == 3:
                                convolve(b, ct + 1, own)
                            if i == 4:
                                soft_plus(b, ct + 1, own)
                            if i == 7:
                                dt_times_x(b, ct + 1)
                        elif i == X0_AT["mean"]:
                            dve.wait_ge(x0_in.sem, x0_in.at(b + 1, 1))
                            norm_mean(dve, own, f_ln, x0[:, :, :])
                        elif i == X0_AT["var"]:
                            norm_var(dve, b, f_ln, 0, 0, EPS)
                        elif i == X0_AT["apply"]:
                            norm_apply(dve, b, f_ln, 0, x0, x0).then_inc(xn0.sem, 1)
                        run_until(moe, 8 + s)
                    gate(b, NCT - 1)
                    run_until(moe, 8 + NCT * NT)
                    dve.wait_ge(fo_up.sem, fo_up.at(b, NJ))
                    norm_mean(dve, own, f_ln, fa[:, :, :])
                    run_until(moe, 8 + NCT * NT + 1)
                    norm_var(dve, b, f_ln, 1, 1, EPS)
                    run_until(moe, 8 + NCT * NT + 2)
                    norm_apply(dve, b, f_ln, 1, fa, fa).then_inc(own.sem, 1)
                    dve.wait_ge(own.sem, own.next())
                    run_until(moe, LAST)
                    if moe is not None:
                        dve.wait_ge(x2_up.sem, x2_up.at(b, 0))
                    dve.wait_ge(x0_back.sem, x0_back.at(b, 1))
                    nc.vector.tensor_tensor(x1[:, :, :], x0_again, fa[:, :, :], ALU.add).then_inc(x1_up.sem, 1)
                    own.end()

                def tournament(own, src, slot):
                    tt = nc.vector.tensor_tensor
                    tt(hi_t[:, 0:4, :], src[:, 0:4, :], src[:, 4:8, :], ALU.max)
                    tt(lo_t[:, 0:4, :], src[:, 0:4, :], src[:, 4:8, :], ALU.min).then_inc(own.sem, 1)
                    dve.wait_ge(own.sem, own.next())
                    yield slot + 1
                    for w in (2, 1):
                        tt(lo_t[:, 0:w, :], lo_t[:, 0:w, :], lo_t[:, w:2 * w, :], ALU.max).then_inc(own.sem, 1)
                        dve.wait_ge(own.sem, own.next())
                        tt(lo_t[:, w:2 * w, :], hi_t[:, 0:w, :], hi_t[:, w:2 * w, :], ALU.min).then_inc(own.sem, 1)
                        dve.wait_ge(own.sem, own.next())
                        tt(hi_t[:, 0:w, :], hi_t[:, 0:w, :], hi_t[:, w:2 * w, :], ALU.max).then_inc(own.sem, 1)
                        dve.wait_ge(own.sem, own.next())
                        tt(lo_t[:, 0:w, :], lo_t[:, 0:w, :], lo_t[:, w:2 * w, :], ALU.max).then_inc(own.sem, 1)
                        dve.wait_ge(own.sem, own.next())

                def moe(b):
                    own = Steps(m_step, b)
                    dve.wait_ge(x1_up.sem, x1_up.at(b, 1))
                    norm_mean(dve, own, m_ln, x1[:, :, :])
                    yield 1
                    norm_var(dve, b, m_ln, 0, 0, EPS)
                    yield 2
                    norm_apply(dve, b, m_ln, 0, ma, x1).then_inc(xm_up.sem, 1)

                    def weights(j, slot):
                        dve.wait_ge(lg_up.sem, lg_up.at(b, 4 * j + 4))
                        if d1_up.begun(b, j):
                            dve.wait_ge(d1_up.sem, d1_up.at(b, j))
                        yield from tournament(own, lg[:, j % 2, :, :], slot)
                        nc.vector.tensor_tensor(sel[:, j % 2, 0, :], hi_t[:, 0, :], lo_t[:, 0, :], ALU.subtract
                                                ).then_inc(gap_up.sem, 1)

                    def sums(j, slot):
                        dve.wait_ge(tanh_up.sem, tanh_up.at(b, j + 1))
                        nc.vector.tensor_scalar(sel[:, j % 2, 1, :], sel[:, j % 2, 0, :], -0.5, 0.5, ALU.mult, ALU.add).then_inc(own.sem, 1)
                        dve.wait_ge(own.sem, own.next())
                        dve.wait_ge(d1_up.sem, d1_up.at(b, j + 1))
                        for e in range(NE):
                            if e == NE // 2:
                                yield slot + 1
                            spare = spares[:, e, :]
                            for i, op, dst in ((1, ALU.is_ge, spare), (0, ALU.is_gt, lg[:, j % 2, e, :])):
                                ins = nc.vector.scalar_tensor_tensor(dst, lg[:, j % 2, e, :], 0.0,
                                                                     sel[:, j % 2, i, :], op, ALU.mult,
                                                                     accum_out=gate_c[:, i, e:e + 1])
                        ins.then_inc(own.sem, 1)
                        dve.wait_ge(own.sem, own.next())
                        nc.vector.tensor_tensor(gate_c[:, 0, :], gate_c[:, 0, :], gate_c[:, 1, :], ALU.add
                                                ).then_inc(c_up.sem, 1)

                    def mix(j, c):
                        if c == 0:
                            dve.wait_ge(c_up.sem, c_up.at(b, j + 1))
                        dve.wait_ge(m_done.sem, m_done.at(b, MOE_AT[("expert", 4 * j + c)] + 1))
                        src = m_bank[MOE_AT[("expert", 4 * j + c)] % MOE_BANKS]
                        dst = [ma[:, j, :], acc]
                        for e in range(2):
                            w = gate_c[:, 0, 2 * c + e:2 * c + e + 1]
                            x = src[:, e * DM:(e + 1) * DM]
                            if c == 0:
                                ins = nc.vector.tensor_scalar(dst[e], x, w, None, ALU.mult)
                            else:
                                ins = nc.vector.scalar_tensor_tensor(dst[e], x, w, dst[e], ALU.mult, ALU.add)
                        ins.then_inc(mix_up.sem, 1)
                        dve.wait_ge(mix_up.sem, mix_up.at(b, 4 * j + c + 1))
                        if c == 3:
                            nc.vector.tensor_tensor(ma[:, j, :], ma[:, j, :], acc, ALU.add).then_inc(own.sem, 1)
                            dve.wait_ge(own.sem, own.next())

                    for (kind, i), slot in zip(MOE[2:-2], DVE_SLOT):
                        yield slot
                        j, c = i // 4, i % 4
                        if kind == "route" and c == 3:
                            yield from weights(j, slot)
                        if kind == "expert":
                            if c == 0:
                                yield from sums(j, slot)
                            mix(j, c)
                    yield 8 + NCT * NT + 1
                    norm_mean(dve, own, m_ln, ma[:, :, :])
                    yield 8 + NCT * NT + 2
                    norm_var(dve, b, m_ln, 1, 1, EPS)
                    yield LAST
                    norm_apply(dve, b, m_ln, 1, ma, ma).then_inc(own.sem, 1)
                    dve.wait_ge(own.sem, own.next())
                    nc.vector.tensor_tensor(ma[:, :, :], x1[:, :, :], ma[:, :, :], ALU.add).then_inc(x2_up.sem, 1)
                    own.end()

                def first_x0():
                    own = Steps(f_step, 0)
                    own.k = -1
                    dve.wait_ge(x0_in.sem, x0_in.at(0, 1))
                    norm_mean(dve, own, f_ln, x0[:, :, :])
                    norm_var(dve, 0, f_ln, -1, -1, EPS)
                    norm_apply(dve, 0, f_ln, -1, x0, x0).then_inc(xn0.sem, 1)

                first_x0()
                prepare()
                rounds(dve, front, moe, None)

            @block.gpsimd
            def _(pool):
                def prepare():
                    def select(ap, pattern, base, mult, op, fill=0.0):
                        return nc.gpsimd.affine_select(out=ap, in_=ap, compare_op=op, fill=fill, base=base,
                                                       pattern=pattern, channel_multiplier=mult)
                    nc.gpsimd.memset(ident[:, :], 1.0)
                    nc.gpsimd.memset(ones_bf[:, :], 1.0)
                    nc.gpsimd.memset(neg_half[:, :], -0.5)
                    one_hot_f32 = u[:, 0, :].rearrange("r (k c) -> r k c", k=4)
                    nc.gpsimd.memset(one_hot_f32, 1.0)
                    nc.gpsimd.memset(state_sum[:, :, :], 1.0).then_inc(consts.sem, 1)
                    pool.wait_ge(consts.sem, consts.at(0, 1))
                    select(ident[:, :], [[-1, P]], 0, 1, ALU.is_equal).then_inc(consts.sem, 1)
                    for part in range(NQ):
                        pool.wait_ge(consts.sem, consts.at(0, 2 + part))
                        select(one_hot_f32[32 * part:32 * part + 32].rearrange("r k (p n) -> r k p n", p=NP),
                               [[-NP, 4], [-1, NP], [0, NS]], 0, 1, ALU.is_equal).then_inc(consts.sem, 1)
                    pool.wait_ge(consts.sem, consts.at(0, 2 + NQ))
                    select(state_sum[:, :, :], [[NP * NS, 4], [-NS, 32]], 0, 1, ALU.is_ge).then_inc(consts.sem, 1)
                    pool.wait_ge(consts.sem, consts.at(0, 3 + NQ))
                    select(state_sum[:, :, :], [[-NP * NS, 4], [NS, 32]], NS - 1, -1, ALU.is_ge).then_inc(consts.sem, 1)
                    pool.wait_ge(consts.sem, consts.at(0, 4 + NQ))
                    nc.gpsimd.tensor_copy(one_hot[:, :, :], one_hot_f32).then_inc(consts.sem, 1)
                    pool.wait_ge(consts.sem, consts.at(0, 5 + NQ))

                def low_half(b, ct, v, terms, quadrants=range(NQ)):
                    if hc_up.begun(b, terms):
                        pool.wait_ge(hc_up.sem, hc_up.at(b, terms))
                    pool.wait_ge(hi_up.sem, hi_up.at(b, 2 * ct + v + 1))
                    for q in quadrants:
                        own, beside = slice(32 * q, 32 * q + 32), slice(32 * (q ^ 1), 32 * (q ^ 1) + 32)
                        nc.gpsimd.tensor_tensor(halves[beside, ct % 2, v, q % 2, :], (dtx[:, :] if v else sp_r)[own],
                                                halves[own, ct % 2, v, q % 2, :], ALU.subtract).then_inc(lo_up.sem, 1)
                        pool.wait_ge(lo_up.sem, lo_up.at(b, low_steps(2 * ct + v) + q + 1))

                def output_term(b, s):
                    hd = s // 2
                    if s % 2 == 0:
                        pool.wait_ge(c_in[hd % C_BUFS].sem, c_in[hd % C_BUFS].at(b, hd // C_BUFS + 1))
                    pool.wait_ge(h_up.sem, h_up.at(b, s + 1))
                    if ysum.begun(b, s - HC_BUFS + 1):
                        pool.wait_ge(ysum.sem, ysum.at(b, s - HC_BUFS + 1))
                    nc.gpsimd.tensor_tensor(hc[:, s % HC_BUFS, :], h[:, s % H_BUFS, :], c_rep[:, hd % C_BUFS, :],
                                            ALU.mult).then_inc(hc_up.sem, 1)

                def front(b, moe):
                    run_until(moe, 0)
                    pool.wait_ge(f_ln.rstd.sem, f_ln.rstd.at(b, 0))
                    if moe is not None:
                        pool.wait_ge(m_ln.rstd.sem, m_ln.rstd.at(b, 1 - m_ln.rstd.per_batch))
                    low_half(b, 0, 0, 0)
                    for s in range(NCT * NT):
                        ct, i = s // NT, s % NT
                        output_term(b, s)
                        if ct + 1 < NCT:
                            if i in (6, 7):
                                low_half(b, ct + 1, 0, s + 1, range(2 * (i - 6), 2 * (i - 6) + 2))
                            if i in (9, 10):
                                low_half(b, ct + 1, 1, s + 1, range(2 * (i - 9), 2 * (i - 9) + 2))
                        elif i == X0_AT["rstd"]:
                            norm_rstd(pool, b, f_ln, 0)
                        run_until(moe, 8 + s)
                    norm_rstd(pool, b, f_ln, 1)
                    run_until(moe, LAST)

                def moe(b):
                    norm_rstd(pool, b, m_ln, 0)
                    for (kind, i), slot in zip(MOE[2:-2], POOL_SLOT):
                        yield slot
                        j, c = i // 4, i % 4
                        if kind == "route" and c == 3:
                            pool.wait_ge(gap_up.sem, gap_up.at(b, j + 1))
                            nc.gpsimd.tensor_tensor(lg[:, j % 2, :, :], lg[:, j % 2, :, :],
                                                    lo_t[:, 0:1, :].to_broadcast([P, NE, DM]), ALU.subtract
                                                    ).then_inc(d1_up.sem, 1)
                    yield LAST
                    norm_rstd(pool, b, m_ln, 1)

                prepare()
                norm_rstd(pool, 0, f_ln, -1)
                rounds(pool, front, moe, None)

        with ExitStack() as ctx:
            def sb(name, shape, dt=F32):
                return ctx.enter_context(nc.sbuf_tensor(name, shape, dt))

            Wv, Wr, Wo, Wcr = (sb(n, [P, KD, DM]) for n in ("Wv", "Wr", "Wo", "Wcr"))
            Wck = sb("Wck", [P, KD, 4 * DM])
            Wcv = sb("Wcv", [P, NI, DM])
            rows = sb("rows", [P, 5, DM])
            cols = sb("cols", [P, KD, 6])
            w12 = sb("w12", [P, 2, NI, DM])
            w3 = sb("w3", [P, KD, HID])
            w1T, w2T = (sb(n, [P, KD, NM * P], F32R) for n in ("w1T", "w2T"))
            w3T = sb("w3T", [P, NM, DM], F32R)
            abs_junk = sb("abs_junk", [P, NI * DM], BF16)
            absum, recip = sb("absum", [P, 4]), sb("recip", [P, 4])
            ones = sb("ones", [P, P])
            decay = sb("decay", [P, KD, T])

            x2 = sb("x2", [P, NJ, DM])
            x2_res = sb("x2_res", [P, NJ, DM])
            x3 = sb("x3", [P, NJ, DM])
            ca, cb = sb("ca", [P, NJ, DM]), sb("cb", [P, NJ, DM])
            c_gate = sb("c_gate", [P, NJ, DM])
            cfeatT = sb("cfeatT", [P, KD, 1 + T])
            c_stat = sb("c_stat", [P, 5, NJ])
            c_junk = sb("c_junk", [P, NJ, DM], BF16)
            ta, tb = sb("ta", [P, NJ, DM]), sb("tb", [P, NJ, DM])
            rt = sb("rt", [P, NJ, DM])
            featT = sb("featT", [P, KD, 1 + T])
            mixT = sb("mixT", [P, KD, T])
            vjunk = sb("vjunk", [P, KD, T], BF16)
            vmix = sb("vmix", [P, KD])
            qh = sb("qh", [P, 1, DM])
            kr = sb("kr", [P, 2, T])
            kcT = sb("kcT", [P, NI, T])
            ramp = kcT[:, 0:3, :]
            r_stat = sb("r_stat", [P, 5, NJ])
            fb = sb("fb", [P, NJ, DM])
            fT = sb("fT", [P, 2, KD, T], F32R)
            th = sb("th", [P, 2, T])
            gated = sb("gated", [P, 2, T])
            hid = sb("hid", [P, 2, NM, T], F32R)
            x4 = sb("x4", [P, NJ, DM])
            g_stat = sb("g_stat", [P, 5, NJ])
            r_junk, g_junk = (sb(n, [P, NJ, DM], BF16) for n in ("r_junk", "g_junk"))
            t_bank, c_bank = bank[0:TIME_BANKS], bank[TIME_BANKS:TIME_BANKS + CHAN_BANKS]
            g_bank, prep_bank = bank[TIME_BANKS + CHAN_BANKS:], bank[4:8]

            x2_in, res_in, small2_in = sig("x2_in", 1, 16), sig("res_in", 1, 16), sig("small2_in", 0, 16)
            rwkv_in, tern_in = sig("rwkv_in", 0, 16), sig("tern_in", 0, 16)
            r_consts, ramp_up, decay_up, abs_up, tot_up, rec_up = (
                sig(n, 0) for n in ("r_consts", "ramp_up", "decay_up", "abs_up", "tot_up", "rec_up"))
            tern_up, turned, turned_up = (sig(n, 0) for n in ("tern_up", "turned", "turned_up"))
            t_step = sig("t_step", 0)
            r_ln = Norm("r", r_stat, 2, 3)
            c_ln = Norm("c", c_stat, 3, 3)
            r_done = sig("r_done", products(TIME))
            c_done = sig("c_done", products(CHAN))
            ln1_up, tm_up, cm_up = sig("ln1_up"), sig("tm_up"), sig("cm_up")
            tT_up, cT_up = sig("tT_up", KD), sig("cT_up", KD)
            mix_in, vmix_up = sig("mix_in", KD), sig("vmix_up", KD)
            r_up, q_up, xa_up = sig("r_up", 2), sig("q_up"), sig("xa_up")
            relu_up, kc_up = sig("relu_up", NI), sig("kc_up", NI)
            cr_up, att_up, x3_up = sig("cr_up", 2), sig("att_up", 2), sig("x3_up")
            r_step, c_step = sig("r_step", T_STEPS), sig("c_step", C_STEPS)

            g_ln = Norm("g", g_stat, 2, 2)
            g_done = sig("g_done", products(FFN))
            xg_up, fT_up = sig("xg_up"), sig("fT_up", KD)
            fT_hi, gated_up, hid_hi = sig("fT_hi", KD), sig("gated_up", NM), sig("hid_hi", NM)
            th_up, hid_up, w3_up = sig("th_up", NM), sig("hid_up", NM), sig("w3_up", 2)
            x4_up, sent = sig("x4_up", ahead=1), sig("sent", 1, 16, ahead=1)
            g_step = sig("g_step", 3)

            N_SMALL2_IN, N_RWKV_IN, N_TERN_IN = 5 + 6, 6, 3
            t_bank_of = lambda name: t_bank[TIME_AT[name] % TIME_BANKS]
            c_bank_of = lambda name: c_bank[CHAN_AT[name] % CHAN_BANKS]
            g_bank_of = lambda name: g_bank[FFN_AT[name] % FFN_BANKS]
            n_ch = [min(P, HID - m * P) for m in range(NM)]

            turns = []
            half = NI // 2
            for v, dst in ((0, w1T), (1, w2T)):
                for k in range(KD):
                    for g in range(2):
                        turns.append(([(t * HR, w12[0:HR, v, g * half + t, k * P:(k + 1) * P]) for t in range(half)],
                                      P, half * HR, dst[:, k, g * half * HR:(g + 1) * half * HR], 1 + v))
            for m in range(NM):
                turns.append(([(t * P, w3[:, t, m * P:m * P + n_ch[m]]) for t in range(KD)],
                              n_ch[m], DM, w3T[0:n_ch[m], m, :], 3))

            block = ctx.enter_context(nc.Block())

            @block.sync
            def _(sp):
                w = lambda n: a["L1_attn_" + n]
                by_ch = lambda ap: ap.rearrange("(c p) -> p c", p=P)
                load = lambda dst, src, s, **kw: sp.dma_start(dst, src, **kw).then_inc(s.sem, 16)

                def load_x2(b):
                    if tm_up.begun(b, 0):
                        sp.wait_ge(tm_up.sem, tm_up.at(b, 0))
                    sp.dma_start(x2[:, :, :], at_b(x2_dram, b).rearrange("b (j p) d -> p (b j) d", p=P)
                                 ).then_inc(x2_in.sem, 16)

                def load_residual(b):
                    if x3_up.begun(b, 0):
                        sp.wait_ge(x3_up.sem, x3_up.at(b, 0))
                    sp.dma_start(x2_res[:, :, :], at_b(x2_dram, b).rearrange("b (j p) d -> p (b j) d", p=P)
                                 ).then_inc(res_in.sem, 16)

                def send(b):
                    sp.wait_ge(x4_up.sem, x4_up.at(b, 1))
                    sp.dma_start(at_b(out, b).rearrange("b (j p) d -> p (b j) d", p=P), x4[:, :, :]
                                 ).then_inc(sent.sem, 16)

                load_x2(0)
                for i, n in ((G1, "ln1_g"), (B1, "ln1_b"), (G2, "ln2_g"), (B2, "ln2_b"), (BO, "bo")):
                    load(rows[:, i, :], w(n).unsqueeze(0).to_broadcast([P, DM]), small2_in)
                for i, n in ((TG, "tm_g"), (TB, "tm_b"), (CG, "cm_g"), (CBE, "cm_b"), (TF, "time_first"), (TD, "time_decay")):
                    load(cols[:, :, i], by_ch(w(n)), small2_in, allow_slow_non_contiguous=True)
                for dst, n in ((Wv, "Wv"), (Wr, "Wr"), (Wo, "Wo"), (Wck, "Wck"), (Wcr, "Wcr"), (Wcv, "Wcv")):
                    load(dst[:, :, :], w(n).rearrange("(k p) n -> p k n", p=P), rwkv_in)
                for v, n in enumerate(("w1", "w2")):
                    load(w12[0:HR, v, :, :], a["L1_ffn_" + n].rearrange("(t p) d -> p t d", p=HR), tern_in)
                load(w3[:, :, :], a["L1_ffn_w3"].rearrange("(t p) d -> p t d", p=P), tern_in)
                load_residual(0)
                load_x2(1)
                with sp.Fori(2, NB) as b:
                    load_x2(b)
                    load_residual(b - 1)
                    send(b - 2)
                load_residual(NB - 1)
                send(NB - 2)
                send(NB - 1)
                sp.wait_ge(sent.sem, sent.at(0, NB))

            @block.tensor
            def _(pe):
                def group(dst, pairs):
                    for k, (l, r) in enumerate(pairs):
                        ins = nc.tensor.matmul(dst, l, r, start=(k == 0), stop=(k == len(pairs) - 1))
                    return ins

                def prepare():
                    yield 37
                    pe.wait_ge(abs_up.sem, abs_up.at(0, 3))
                    pe.wait_ge(r_consts.sem, r_consts.at(0, 1))
                    nc.tensor.matmul(prep_bank[3][:, 0:4], ones[:, :], absum[:, :], start=True, stop=True
                                     ).then_inc(turned.sem, 1)
                    for n, (srcs, m, _, _, v) in enumerate(turns):
                        yield 50 + 2 * n
                        pe.wait_ge(tern_up.sem, tern_up.at(0, v))
                        if n >= 4:
                            pe.wait_ge(turned_up.sem, turned_up.at(0, n - 3))
                        if n == 3:
                            pe.wait_ge(tot_up.sem, tot_up.at(0, 1))
                        for col, src in srcs:
                            w = src.shape[0]
                            ins = nc.tensor.transpose(prep_bank[n % 4][0:m, col:col + w], src, ident[0:w, 0:w])
                        ins.then_inc(turned.sem, 1)
                    yield 52 + 2 * len(turns)
                    pe.wait_ge(turned_up.sem, turned_up.at(0, len(turns)))

                def time_mix(b):

                    def free(name):
                        n = TIME_AT[name]
                        m = n - TIME_BANKS
                        while TIME[m][0] == "pad":
                            m -= TIME_BANKS
                        kind, i = TIME[m]
                        s, k = {"tT": (tT_up, i + 1), "v": (vmix_up, i + 1), "r": (r_up, i + 1), "q": (q_up, 1)}[kind]
                        if s.begun(b, k if m >= 0 else k - s.per_batch):
                            pe.wait_ge(s.sem, s.at(b, k if m >= 0 else k - s.per_batch))
                        return t_bank_of(name)

                    yield 32
                    pe.wait_ge(tm_up.sem, tm_up.at(b, 1))
                    for k in range(KD):
                        transpose_tiles(free(("tT", k)), tb, k).then_inc(r_done.sem, 1)
                    yield 36
                    if isinstance(b, int) and b == 0:
                        pe.wait_ge(rwkv_in.sem, rwkv_in.at(0, N_RWKV_IN))
                    pe.wait_ge(tT_up.sem, tT_up.at(b, KD))
                    for m in range(KD):
                        group(free(("v", m))[:, :], [(Wv[:, k, m * P:(m + 1) * P], featT[:, k, 1:1 + T]) for k in range(KD)]
                              ).then_inc(r_done.sem, 1)
                    yield 41
                    pe.wait_ge(mix_in.sem, mix_in.at(b, KD))
                    for i in range(2):
                        dst = free(("r", i))
                        for j in range(2):
                            t = (2 * i + j) * P
                            ins = group(dst[:, j * DM:(j + 1) * DM], [(mixT[:, k, t:t + P], Wr[:, k, :]) for k in range(KD)])
                        ins.then_inc(r_done.sem, 1)
                    yield 45
                    pe.wait_ge(vmix_up.sem, vmix_up.at(b, KD))
                    group(free(("q", 0))[:, 0:DM], [(vmix[:, k:k + 1].to_broadcast([P, P]), Wo[:, k, :]) for k in range(KD)]
                          ).then_inc(r_done.sem, 1)

                def channel_mix(b):
                    def free(name):
                        n = CHAN_AT[name]
                        m = n - CHAN_BANKS
                        while CHAN[m][0] == "pad":
                            m -= CHAN_BANKS
                        kind, i = CHAN[m]
                        s, k = {"cT": (cT_up, i + 1), "ck": (relu_up, i + 1), "cr": (cr_up, i + 1),
                                "cv": (att_up, i + 1)}[kind]
                        if s.begun(b, k if m >= 0 else k - s.per_batch):
                            pe.wait_ge(s.sem, s.at(b, k if m >= 0 else k - s.per_batch))
                        return c_bank_of(name)

                    yield 30
                    pe.wait_ge(cm_up.sem, cm_up.at(b, 1))
                    for k in range(KD):
                        transpose_tiles(free(("cT", k)), cb, k).then_inc(c_done.sem, 1)
                    for m in range(NI):
                        yield 34 + 2 * m
                        pe.wait_ge(cT_up.sem, cT_up.at(b, KD))
                        group(free(("ck", m))[:, :], [(Wck[:, k, m * P:(m + 1) * P], cfeatT[:, k, 0:T]) for k in range(KD)]
                              ).then_inc(c_done.sem, 1)
                    yield 49
                    for i in range(2):
                        dst = free(("cr", i))
                        for j in range(2):
                            t = 1 + (2 * i + j) * P
                            ins = group(dst[:, j * DM:(j + 1) * DM], [(cfeatT[:, k, t:t + P], Wcr[:, k, :]) for k in range(KD)])
                        ins.then_inc(c_done.sem, 1)
                    yield 55
                    pe.wait_ge(kc_up.sem, kc_up.at(b, NI))
                    for i in range(2):
                        dst = free(("cv", i))
                        for j in range(2):
                            t = (2 * i + j) * P
                            ins = group(dst[:, j * DM:(j + 1) * DM], [(kcT[:, m, t:t + P], Wcv[:, m, :]) for m in range(NI)])
                        ins.then_inc(c_done.sem, 1)

                def ffn(b):
                    def free(name):
                        n = FFN_AT[name]
                        if n >= FFN_BANKS:
                            kind, i = FFN[n - FFN_BANKS]
                            s = {"fT": fT_up, "w1": th_up, "w2": gated_up, "w3": w3_up}[kind]
                            pe.wait_ge(s.sem, s.at(b, i + 1))
                        return g_bank_of(name)

                    yield 20
                    pe.wait_ge(x4_up.sem, x4_up.at(b, 0))
                    pe.wait_ge(xg_up.sem, xg_up.at(b, 1))
                    for k in range(KD):
                        transpose_tiles(free(("fT", k)), fb, k).then_inc(g_done.sem, 1)
                    for m in range(NM):
                        yield 24 + 4 * m
                        pe.wait_ge(fT_up.sem, fT_up.at(b, KD))
                        for kind, w in (("w1", w1T), ("w2", w2T)):
                            group(free((kind, m))[:, :], [(w[:, k, m * P:(m + 1) * P], fT[:, half, k, :])
                                                          for k in range(KD) for half in range(2)]
                                  ).then_inc(g_done.sem, 1)
                    yield 50
                    pe.wait_ge(hid_up.sem, hid_up.at(b, NM))
                    for i in range(2):
                        dst = free(("w3", i))
                        for j in range(2):
                            t = (2 * i + j) * P
                            ins = group(dst[:, j * DM:(j + 1) * DM],
                                        [(hid[0:n_ch[m], half, m, t:t + P], w3T[0:n_ch[m], m, :])
                                         for m in range(NM) for half in range(2)])
                        ins.then_inc(g_done.sem, 1)

                three_rounds(pe, time_mix, channel_mix, ffn, prepare)

            @block.scalar
            def _(act):
                def prepare():
                    yield 34
                    act.wait_ge(tern_in.sem, tern_in.at(0, N_TERN_IN))
                    act.wait_ge(r_consts.sem, r_consts.at(0, 1))
                    for v in range(2):
                        nc.scalar.activation(abs_junk[0:HR, :],
                                             w12[0:HR, v, :, :].rearrange("p a d -> p (a d)"), ACT.Abs,
                                             accum_out=absum[0:HR, v:v + 1]).then_inc(abs_up.sem, 1)
                        act.wait_ge(abs_up.sem, abs_up.at(0, v + 1))
                    nc.scalar.activation(abs_junk[:, 0:KD * HID],
                                         w3[:, :, :].rearrange("p a d -> p (a d)"), ACT.Abs,
                                         accum_out=absum[:, 2:3]).then_inc(abs_up.sem, 1)
                    for n, (srcs, m, width, dst, _) in enumerate(turns):
                        yield 51 + 2 * n
                        act.wait_ge(turned.sem, turned.at(0, n + 2))
                        nc.scalar.copy(dst, prep_bank[n % 4][0:m, 0:width]).then_inc(turned_up.sem, 1)

                def take(dst, k, src, gi, bi):
                    return nc.scalar.activation(dst[:, k, 1:1 + T], src[:, :], ACT.Identity,
                                                bias=cols[:, k, bi:bi + 1], scale=cols[:, k, gi:gi + 1])

                def time_mix(b):
                    yield 11
                    norm_square(act, b, r_ln, 0, x2[:, :, :], r_junk)
                    yield 22
                    norm_square(act, b, r_ln, 1, tb, r_junk)
                    yield 33
                    if isinstance(b, int) and b == 0:
                        act.wait_ge(small2_in.sem, small2_in.at(0, N_SMALL2_IN))
                        act.wait_ge(ramp_up.sem, ramp_up.at(0, 1))
                        for k in range(KD):
                            nc.scalar.activation(decay[:, k, :], ramp[:, 2, :], ACT.Exp,
                                                 scale=cols[:, k, TD:TD + 1]).then_inc(decay_up.sem, 1)
                    if r_done.begun(b, 0):
                        act.wait_ge(r_done.sem, r_done.at(b, 0))
                        act.wait_ge(mix_in.sem, mix_in.at(b, 0))
                    for k in range(KD):
                        act.wait_ge(r_done.sem, r_done.at(b, TIME_AT[("tT", k)] + 1))
                        take(featT, k, t_bank_of(("tT", k)), TG, TB).then_inc(tT_up.sem, 1)
                    yield 43
                    if xa_up.begun(b, 0):
                        act.wait_ge(xa_up.sem, xa_up.at(b, 0))
                    for i in range(2):
                        act.wait_ge(r_done.sem, r_done.at(b, TIME_AT[("r", i)] + 1))
                        nc.scalar.activation(rt[:, 2 * i:2 * i + 2, :].rearrange("p j d -> p (j d)"),
                                             t_bank_of(("r", i))[:, :], ACT.Tanh, scale=0.5).then_inc(r_up.sem, 1)

                def channel_mix(b):
                    yield 11
                    norm_square(act, b, c_ln, 0, ca, c_junk)
                    yield 19
                    norm_square(act, b, c_ln, 1, cb, c_junk)
                    yield 31
                    if c_done.begun(b, 0):
                        act.wait_ge(c_done.sem, c_done.at(b, 0))
                    for k in range(KD):
                        act.wait_ge(c_done.sem, c_done.at(b, CHAN_AT[("cT", k)] + 1))
                        take(cfeatT, k, c_bank_of(("cT", k)), CG, CBE).then_inc(cT_up.sem, 1)
                    for m in range(NI):
                        yield 35 + 2 * m
                        act.wait_ge(c_done.sem, c_done.at(b, CHAN_AT[("ck", m)] + 1))
                        if kc_up.begun(b, m - 1):
                            act.wait_ge(kc_up.sem, kc_up.at(b, m - 1))
                        nc.scalar.activation(kr[:, m % 2, :], c_bank_of(("ck", m))[:, :], ACT.Relu).then_inc(relu_up.sem, 1)
                    yield 50
                    if x3_up.begun(b, 0):
                        act.wait_ge(x3_up.sem, x3_up.at(b, 0))
                    for i in range(2):
                        act.wait_ge(c_done.sem, c_done.at(b, CHAN_AT[("cr", i)] + 1))
                        nc.scalar.activation(c_gate[:, 2 * i:2 * i + 2, :].rearrange("p j d -> p (j d)"),
                                             c_bank_of(("cr", i))[:, :], ACT.Tanh, scale=0.5).then_inc(cr_up.sem, 1)
                    yield 61
                    norm_square(act, b, c_ln, 2, ca, c_junk)

                def ffn(b):
                    yield 10
                    norm_square(act, b, g_ln, 0, x3[:, :, :], g_junk)
                    yield 22
                    for k in range(KD):
                        act.wait_ge(g_done.sem, g_done.at(b, FFN_AT[("fT", k)] + 1))
                        nc.scalar.copy(fT[:, 0, k, :], g_bank_of(("fT", k))[:, :]).then_inc(fT_hi.sem, 1)
                    for m in range(NM):
                        yield 25 + 4 * m
                        act.wait_ge(g_done.sem, g_done.at(b, FFN_AT[("w1", m)] + 1))
                        if m >= 2:
                            act.wait_ge(gated_up.sem, gated_up.at(b, m - 1))
                        nc.scalar.activation(th[:, m % 2, :], g_bank_of(("w1", m))[:, :], ACT.Tanh, scale=0.5
                                             ).then_inc(th_up.sem, 1)
                        yield 27 + 4 * m
                        act.wait_ge(gated_up.sem, gated_up.at(b, m + 1))
                        nc.scalar.copy(hid[:, 0, m, :], gated[:, m % 2, :]).then_inc(hid_hi.sem, 1)
                    yield 51
                    for i in range(2):
                        act.wait_ge(g_done.sem, g_done.at(b, FFN_AT[("w3", i)] + 1))
                        nc.scalar.activation(fb[:, 2 * i:2 * i + 2, :].rearrange("p j d -> p (j d)"),
                                             g_bank_of(("w3", i))[:, :], ACT.Copy, scale=0.5).then_inc(w3_up.sem, 1)
                    yield 53
                    norm_square(act, b, g_ln, 1, fb, g_junk)

                three_rounds(act, time_mix, channel_mix, ffn, prepare)

            @block.vector
            def _(dve):
                stt, tt, ts = nc.vector.scalar_tensor_tensor, nc.vector.tensor_tensor, nc.vector.tensor_scalar

                def prepare():
                    yield 39
                    dve.wait_ge(turned.sem, turned.at(0, 1))
                    ts(recip[:, :], prep_bank[3][:, 0:4], 1.0 / (HID * DM), EPS3, ALU.mult, ALU.add).then_inc(tot_up.sem, 1)
                    dve.wait_ge(tot_up.sem, tot_up.at(0, 1))
                    nc.vector.reciprocal(recip[:, :], recip[:, :]).then_inc(rec_up.sem, 1)
                    dve.wait_ge(rec_up.sem, rec_up.at(0, 1))
                    n = 0
                    for v, w in enumerate((w12[0:HR, 0, :, :], w12[0:HR, 1, :, :], w3[:, :, :])):
                        scale = recip[0:w.shape[0], v:v + 1]
                        for in1, in2, op1, op2 in ((scale, MAGIC, ALU.mult, ALU.add), (MAGIC, 1.0, ALU.subtract, ALU.min)):
                            ts(w, w, in1, in2, op1, op2).then_inc(t_step.sem, 1)
                            n += 1
                            dve.wait_ge(t_step.sem, t_step.at(0, n))
                        ts(w, w, -1.0, None, ALU.max).then_inc(tern_up.sem, 1)
                        yield 42 + 2 * v

                def time_mix(b):
                    own = Steps(r_step, b)

                    yield 9
                    dve.wait_ge(x2_in.sem, x2_in.at(b, 1))
                    norm_mean(dve, own, r_ln, x2[:, :, :])
                    yield 13
                    norm_var(dve, b, r_ln, 0, 0, EPS)
                    yield 17
                    norm_apply(dve, b, r_ln, 0, ta, x2[:, :, :]).then_inc(own.sem, 1)
                    dve.wait_ge(own.sem, own.next())
                    tt(r_ln.v, r_ln.ss, r_ln.r, ALU.mult).then_inc(own.sem, 1)
                    dve.wait_ge(own.sem, own.next())
                    tt(r_ln.v, r_ln.v, r_ln.r, ALU.mult).then_inc(own.sem, 1)
                    dve.wait_ge(own.sem, own.next())
                    ts(r_ln.v, r_ln.v, 1.0 / DM, EPS2, ALU.mult, ALU.add).then_inc(r_ln.var.sem, 1)
                    yield 20
                    if isinstance(b, int) and b == 0:
                        dve.wait_ge(small2_in.sem, small2_in.at(0, N_SMALL2_IN))
                    dve.wait_ge(r_ln.rstd.sem, r_ln.rstd.at(b, 2))
                    for j in range(NJ):
                        ins = stt(tb[:, j, :], ta[:, j, :], r_ln.r[:, j:j + 1], rows[:, G1, :], ALU.mult, ALU.mult)
                    ins.then_inc(own.sem, 1)
                    dve.wait_ge(own.sem, own.next())
                    tt(tb[:, :, :], tb[:, :, :], rows[:, B1:B1 + 1, :].to_broadcast([P, NJ, DM]), ALU.add).then_inc(own.sem, 1)
                    dve.wait_ge(own.sem, own.next())
                    yield 21
                    norm_mean(dve, own, r_ln, tb[:, :, :])
                    yield 26
                    norm_var(dve, b, r_ln, 1, 2, EPS2)
                    yield 28
                    norm_apply(dve, b, r_ln, 2, tb, tb).then_inc(tm_up.sem, 1)
                    yield 35
                    for k in range(KD):
                        dve.wait_ge(tT_up.sem, tT_up.at(b, k + 1))
                        tt(mixT[:, k, :], featT[:, k, 1:1 + T], featT[:, k, 0:T], ALU.subtract).then_inc(own.sem, 1)
                        dve.wait_ge(own.sem, own.next())
                        stt(mixT[:, k, :], mixT[:, k, :], cols[:, k, TF:TF + 1], featT[:, k, 0:T], ALU.mult, ALU.add
                            ).then_inc(mix_in.sem, 1)
                    yield 38
                    if isinstance(b, int) and b == 0:
                        dve.wait_ge(decay_up.sem, decay_up.at(0, KD))
                    for m in range(KD):
                        dve.wait_ge(r_done.sem, r_done.at(b, TIME_AT[("v", m)] + 1))
                        stt(vjunk[:, m, :], t_bank_of(("v", m))[:, :], 1.0, decay[:, m, :], ALU.mult, ALU.mult,
                            accum_out=vmix[:, m:m + 1]).then_inc(vmix_up.sem, 1)
                    yield 47
                    dve.wait_ge(r_done.sem, r_done.at(b, TIME_AT[("q", 0)] + 1))
                    tt(qh[:, 0, :], t_bank_of(("q", 0))[:, 0:DM], rows[:, BO, :], ALU.add).then_inc(q_up.sem, 1)
                    dve.wait_ge(q_up.sem, q_up.at(b, 1))
                    ts(qh[:, 0, :], qh[:, 0, :], 0.5, None, ALU.mult).then_inc(own.sem, 1)
                    dve.wait_ge(own.sem, own.next())
                    dve.wait_ge(r_up.sem, r_up.at(b, 2))
                    stt(rt[:, :, :], rt[:, :, :], 1.0, qh[:, :, :].to_broadcast([P, NJ, DM]), ALU.add, ALU.mult).then_inc(own.sem, 1)
                    dve.wait_ge(own.sem, own.next())
                    yield 68
                    if x3_up.begun(b, 0):
                        dve.wait_ge(x3_up.sem, x3_up.at(b, 0))
                    tt(ca[:, :, :], ta[:, :, :], rt[:, :, :], ALU.add).then_inc(xa_up.sem, 1)
                    own.end()

                def channel_mix(b):
                    own = Steps(c_step, b)

                    def affine(dst, src, k_pow, g, beta):
                        dve.wait_ge(c_ln.rstd.sem, c_ln.rstd.at(b, k_pow + 1))
                        for j in range(NJ):
                            ins = stt(dst[:, j, :], src[:, j, :], c_ln.neg[:, j:j + 1], rows[:, g, :], ALU.add, ALU.mult)
                        ins.then_inc(own.sem, 1)
                        dve.wait_ge(own.sem, own.next())
                        for j in range(NJ):
                            ins = stt(dst[:, j, :], dst[:, j, :], c_ln.r[:, j:j + 1], rows[:, beta, :], ALU.mult, ALU.add)
                        ins.then_inc(own.sem, 1)
                        dve.wait_ge(own.sem, own.next())

                    yield 9
                    dve.wait_ge(xa_up.sem, xa_up.at(b, 1))
                    norm_mean(dve, own, c_ln, ca[:, :, :])
                    yield 13
                    norm_var(dve, b, c_ln, 0, 0, EPS2)
                    yield 17
                    affine(cb, ca, 0, G2, B2)
                    yield 18
                    norm_mean(dve, own, c_ln, cb[:, :, :])
                    yield 25
                    norm_var(dve, b, c_ln, 1, 1, EPS2)
                    yield 27
                    norm_apply(dve, b, c_ln, 1, cb, cb).then_inc(cm_up.sem, 1)
                    yield 57
                    dve.wait_ge(cr_up.sem, cr_up.at(b, 2))
                    for i in range(2):
                        part = lambda ap: ap[:, 2 * i:2 * i + 2, :].rearrange("p j d -> p (j d)")
                        dve.wait_ge(c_done.sem, c_done.at(b, CHAN_AT[("cv", i)] + 1))
                        stt(part(c_gate), part(c_gate), 1.0, c_bank_of(("cv", i))[:, :], ALU.add, ALU.mult).then_inc(att_up.sem, 1)
                        dve.wait_ge(att_up.sem, att_up.at(b, i + 1))
                        stt(part(ca), part(c_gate), 0.5, part(ca), ALU.mult, ALU.add).then_inc(own.sem, 1)
                        dve.wait_ge(own.sem, own.next())
                    yield 60
                    norm_mean(dve, own, c_ln, ca[:, :, :])
                    yield 62
                    norm_var(dve, b, c_ln, 2, 2, EPS)
                    yield 64
                    norm_apply(dve, b, c_ln, 2, ca, ca).then_inc(own.sem, 1)
                    dve.wait_ge(own.sem, own.next())
                    if x4_up.begun(b, 0):
                        dve.wait_ge(x4_up.sem, x4_up.at(b, 0))
                    dve.wait_ge(res_in.sem, res_in.at(b, 1))
                    tt(x3[:, :, :], x2_res[:, :, :], ca[:, :, :], ALU.add).then_inc(x3_up.sem, 1)
                    own.end()

                def ffn(b):
                    own = Steps(g_step, b)
                    yield 8
                    dve.wait_ge(x3_up.sem, x3_up.at(b, 1))
                    norm_mean(dve, own, g_ln, x3[:, :, :])
                    yield 12
                    norm_var(dve, b, g_ln, 0, 0, EPS)
                    yield 16
                    norm_apply(dve, b, g_ln, 0, fb, x3[:, :, :]).then_inc(xg_up.sem, 1)
                    yield 23
                    for k in range(KD):
                        dve.wait_ge(fT_hi.sem, fT_hi.at(b, k + 1))
                        tt(fT[:, 1, k, :], g_bank_of(("fT", k))[:, :], fT[:, 0, k, :], ALU.subtract).then_inc(fT_up.sem, 1)
                    for m in range(NM):
                        yield 26 + 4 * m
                        dve.wait_ge(g_done.sem, g_done.at(b, FFN_AT[("w2", m)] + 1))
                        dve.wait_ge(th_up.sem, th_up.at(b, m + 1))
                        if m >= 2:
                            dve.wait_ge(hid_up.sem, hid_up.at(b, m - 1))
                        stt(gated[:, m % 2, :], th[:, m % 2, :], 1.0, g_bank_of(("w2", m))[:, :], ALU.add, ALU.mult
                            ).then_inc(gated_up.sem, 1)
                    yield 52
                    dve.wait_ge(w3_up.sem, w3_up.at(b, 2))
                    norm_mean(dve, own, g_ln, fb[:, :, :])
                    yield 54
                    norm_var(dve, b, g_ln, 1, 1, EPS)
                    yield 56
                    norm_apply(dve, b, g_ln, 1, fb, fb).then_inc(own.sem, 1)
                    dve.wait_ge(own.sem, own.next())
                    if sent.begun(b, 0):
                        dve.wait_ge(sent.sem, sent.at(b, 0))
                    tt(x4[:, :, :], x3[:, :, :], fb[:, :, :], ALU.add).then_inc(x4_up.sem, 1)
                    own.end()

                nc.vector.memset(featT[:, :, 0:1], 0.0)
                nc.vector.memset(cfeatT[:, :, 0:1], 0.0)
                nc.vector.memset(w1T[:, :, HID:].bitcast(F32), 0.0)
                nc.vector.memset(w2T[:, :, HID:].bitcast(F32), 0.0)
                dve.wait_ge(r_consts.sem, r_consts.at(0, 1))
                nc.vector.tensor_tensor_scan(ramp[:, 2, :], ramp[:, 0, :], ramp[:, 1, :], float(T), ALU.mult, ALU.add
                                             ).then_inc(ramp_up.sem, 1)
                three_rounds(dve, time_mix, channel_mix, ffn, prepare)

            @block.gpsimd
            def _(pool):
                def time_mix(b):
                    for k, t in enumerate((15, 18, 27)):
                        yield t
                        norm_rstd(pool, b, r_ln, k)

                def channel_mix(b):
                    for k, t in enumerate((15, 26)):
                        yield t
                        norm_rstd(pool, b, c_ln, k)
                    for m in range(NI):
                        yield 35 + 2 * m
                        pool.wait_ge(relu_up.sem, relu_up.at(b, m + 1))
                        if m == 0 and c_done.begun(b, 0):
                            pool.wait_ge(c_done.sem, c_done.at(b, 0))
                        nc.gpsimd.tensor_tensor(kcT[:, m, :], kr[:, m % 2, :], kr[:, m % 2, :], ALU.mult
                                                ).then_inc(kc_up.sem, 1)
                    yield 63
                    norm_rstd(pool, b, c_ln, 2)

                def ffn(b):
                    yield 14
                    norm_rstd(pool, b, g_ln, 0)
                    for m in range(NM):
                        yield 27 + 4 * m
                        pool.wait_ge(hid_hi.sem, hid_hi.at(b, m + 1))
                        nc.gpsimd.tensor_tensor(hid[:, 1, m, :], gated[:, m % 2, :], hid[:, 0, m, :], ALU.subtract
                                                ).then_inc(hid_up.sem, 1)
                    yield 55
                    norm_rstd(pool, b, g_ln, 1)

                nc.gpsimd.memset(x4[:, 0, :], 0.0).then_inc(x4_up.sem, 1)
                nc.gpsimd.memset(x4[:, 1, :], 0.0).then_inc(sent.sem, 16)
                nc.gpsimd.memset(absum[:, :], 0.0)
                nc.gpsimd.memset(ones[:, :], 1.0)
                nc.gpsimd.memset(ramp[:, 0, :], 1.0)
                nc.gpsimd.memset(ramp[:, 1, :], -1.0).then_inc(r_consts.sem, 1)
                three_rounds(pool, time_mix, channel_mix, ffn, None)



_INS = ["x", "L0_attn_in_proj_w", "L0_attn_dt_in_proj_w", "L0_attn_dt_proj_w", "L0_attn_dt_proj_b",
        "L0_attn_conv_w", "L0_attn_conv_b", "L0_attn_A_log", "L0_attn_D", "L0_attn_out_proj_w",
        "L0_ffn_router_w", "L0_ffn_router_b", "L0_ffn_expert_w", "L0_ffn_expert_b",
        "L1_attn_ln1_g", "L1_attn_ln1_b", "L1_attn_ln2_g", "L1_attn_ln2_b", "L1_attn_tm_g", "L1_attn_tm_b",
        "L1_attn_time_decay", "L1_attn_time_first", "L1_attn_Wv", "L1_attn_Wr", "L1_attn_Wo",
        "L1_attn_bo", "L1_attn_cm_g", "L1_attn_cm_b", "L1_attn_Wck", "L1_attn_Wcv", "L1_attn_Wcr",
        "L1_ffn_w1", "L1_ffn_w2", "L1_ffn_w3"]


def kernel(**inputs):
    import numpy as _np
    import concourse.bacc as _bacc
    from concourse import mybir as _mybir
    from concourse.bass_utils import run_bass_kernel_spmd as _run

    nc = _bacc.Bacc("TRN2", target_bir_lowering=False, num_devices=1)
    arrays, a = {}, {}
    for name in _INS:
        arr = _np.ascontiguousarray(inputs["L0_attn_hidden_states" if name == "x" else name])
        arrays[f"in_{name}_dram"] = arr
        a[name] = nc.dram_tensor(f"in_{name}_dram", arr.shape, _mybir.dt.from_np(arr.dtype), kind="ExternalInput").ap()
    out = nc.dram_tensor("out_0_dram", (NB, T, DM), _mybir.dt.float32, kind="ExternalOutput").ap()
    hybrid_layers_kernel(nc, a, out)
    r = _run(nc, [arrays], core_ids=[0])
    return r.results[0]["out_0_dram"]
```
